# Optimizing a Trainium2 kernel written in Bass

```python
import numpy as np
import jax
import jax.numpy as jnp

def _softmax(x, axis=-1):
    return jax.nn.softmax(x, axis=axis)

def _gelu(x):
    return jax.nn.gelu(x, approximate=True)

def _silu(x):
    return jax.nn.silu(x)

def _sigmoid(x):
    return jax.nn.sigmoid(x)

def _layernorm(x, axis=-1, eps=1e-05):
    m = jnp.mean(x, axis=axis, keepdims=True)
    v = jnp.var(x, axis=axis, keepdims=True)
    return (x - m) / jnp.sqrt(v + eps)

def _scatter_add(tgt, idx, src, axis=0):
    return tgt.at[idx].add(src)

def _segment_sum(src, seg, n):
    return jax.ops.segment_sum(src, seg, n)
kernel_name = 'mk_prb_d2_jaxref_r8_3bb18f'

def setup_inputs(seed: int=0):
    np.random.seed(seed)
    _w = jnp.asarray

    def _L0_attn_setup():
        import jax, jax.numpy as jnp
        import numpy as np
        D = 128
        H = 16
        DH = D // H
        B = 2
        T = 256
        GN_EPS = 0.00064

        def _wkv_scan(r, k, v, w):

            def step(state, inp):
                r_t, k_t, v_t, w_t = inp
                state = state * jnp.exp(w_t)[..., None] + k_t[..., None] * v_t[..., None, :]
                o_t = jnp.einsum('bhkv,bhv->bhk', state, r_t)
                return (state, o_t)
            tm = lambda a: jnp.swapaxes(a, 0, 1)
            state0 = jnp.zeros((r.shape[0], H, DH, DH), dtype=r.dtype)
            _, out = jax.lax.scan(step, state0, (tm(r), tm(k), tm(v), tm(w)))
            return jnp.swapaxes(out, 0, 1)
        key = jax.random.key(seed)
        ks = jax.random.split(key, 16)

        def w(k):
            return jax.random.normal(k, (D, D), dtype=jnp.float32) * 0.02
        inp = {'x': jax.random.normal(ks[0], (B, T, D), dtype=jnp.float32), 'ddlerp_w': w(ks[1]), 'mix_r': jnp.full((D,), 0.5, dtype=jnp.float32), 'mix_k': jnp.full((D,), 0.5, dtype=jnp.float32), 'mix_v': jnp.full((D,), 0.5, dtype=jnp.float32), 'mix_g': jnp.full((D,), 0.5, dtype=jnp.float32), 'mix_w': jnp.full((D,), 0.5, dtype=jnp.float32), 'r_w': w(ks[2]), 'k_w': w(ks[3]), 'v_w': w(ks[4]), 'g_w': w(ks[5]), 'w_w': w(ks[6]), 'out_w': w(ks[7]), 'gn_weight': jnp.ones((D,), dtype=jnp.float32), 'gn_bias': jnp.zeros((D,), dtype=jnp.float32)}
        return inp
    _L0_attn_in = _L0_attn_setup()

    def _L0_ffn_setup():
        import jax, jax.numpy as jnp
        import numpy as np
        NQ, NK, H, DH = (128, 64, 8, 64)
        key = jax.random.key(seed)
        ks = jax.random.split(key, 8)
        b, n, d, g = (4, 512, 128, 4)
        di = H * DH
        s = lambda fan: 1.0 / np.sqrt(fan)
        return {'x': jax.random.normal(ks[0], (b, n, d), jnp.float32), 'w_qr': jax.random.normal(ks[1], (g, d), jnp.float32) * s(d), 'w_kvr': jax.random.normal(ks[2], (g, d), jnp.float32) * s(d), 'w_q': jax.random.normal(ks[3], (g, di, d), jnp.float32) * s(d), 'w_kv': jax.random.normal(ks[4], (g, 2 * di, d), jnp.float32) * s(d), 'w_out': jax.random.normal(ks[5], (g, d, di), jnp.float32) * s(di), 'null_kv': jax.random.normal(ks[6], (2, g, H, 1, DH), jnp.float32), 'null_token': jax.random.normal(ks[7], (1, 1, d), jnp.float32)}
    _L0_ffn_in = _L0_ffn_setup()

    def _L1_attn_setup():
        import jax, jax.numpy as jnp
        import numpy as np
        from jax import lax
        B, S, E, SD = (8, 512, 128, 8)

        def _reference_tuple_inner(x, W_in, b_in, W_g, b_g, W_out, b_out):
            embed_dim = W_in.shape[0]
            combined = jnp.einsum('bse,ec->bsc', x, W_in) + b_in
            embed = combined[..., :embed_dim]
            state_in = combined[..., embed_dim:]
            gate = jax.nn.sigmoid(jnp.einsum('bsc,cd->bsd', combined, W_g) + b_g)

            def step(state, gs):
                g, si = gs
                new = g * state + (1.0 - g) * si
                return (new, new)
            state0 = jnp.zeros((x.shape[0], state_in.shape[-1]), dtype=x.dtype)
            g_t = jnp.moveaxis(gate, 1, 0)
            si_t = jnp.moveaxis(state_in, 1, 0)
            final_state, states = lax.scan(step, state0, (g_t, si_t))
            states = jnp.moveaxis(states, 0, 1)
            out = jnp.einsum('bsc,cd->bsd', jnp.concatenate([embed, states], axis=-1), W_out) + b_out
            return (out, final_state)
        key = jax.random.key(seed)
        ks = jax.random.split(key, 4)
        x = jax.random.normal(ks[0], (B, S, E), dtype=jnp.float32)
        W_in = jax.random.normal(ks[1], (E, E + SD), dtype=jnp.float32) / np.sqrt(E)
        b_in = jnp.zeros((E + SD,), dtype=jnp.float32)
        W_g = jax.random.normal(ks[2], (E + SD, SD), dtype=jnp.float32) / np.sqrt(E + SD)
        b_g = jnp.zeros((SD,), dtype=jnp.float32)
        W_out = jax.random.normal(ks[3], (E + SD, E), dtype=jnp.float32) / np.sqrt(E + SD)
        b_out = jnp.zeros((E,), dtype=jnp.float32)
        return {'x': x, 'W_in': W_in, 'b_in': b_in, 'W_g': W_g, 'b_g': b_g, 'W_out': W_out, 'b_out': b_out}
    _L1_attn_in = _L1_attn_setup()

    def _L1_ffn_setup():
        import jax, jax.numpy as jnp
        import numpy as np
        B, T, DIM = (4, 128, 128)
        H, E, DH, K = (8, 5, 64, 3)

        def _topk_mask(s, k):
            idx = jax.lax.top_k(s, k)[1]
            return jnp.sum(jax.nn.one_hot(idx, s.shape[-1], dtype=s.dtype), axis=-2)
        key = jax.random.key(seed)
        ks = jax.random.split(key, 6)
        w = lambda k, shape: jax.random.normal(k, shape, jnp.float32) * 0.02
        return {'x': jax.random.normal(ks[0], (B, T, DIM), jnp.float32), 'Wq': w(ks[1], (DIM, H * E * DH)), 'Wkv': w(ks[2], (DIM, 2 * H * E * DH)), 'Ws': w(ks[3], (DIM, H * E)), 'Wd': w(ks[4], (DIM, H * E)), 'Wo': w(ks[5], (DH, E * DIM))}
    _L1_ffn_in = _L1_ffn_setup()
    _d = {'L0_attn_x': _L0_attn_in['x'], 'L0_attn_ddlerp_w': _L0_attn_in['ddlerp_w'], 'L0_attn_mix_r': _L0_attn_in['mix_r'], 'L0_attn_mix_k': _L0_attn_in['mix_k'], 'L0_attn_mix_v': _L0_attn_in['mix_v'], 'L0_attn_mix_g': _L0_attn_in['mix_g'], 'L0_attn_mix_w': _L0_attn_in['mix_w'], 'L0_attn_r_w': _L0_attn_in['r_w'], 'L0_attn_k_w': _L0_attn_in['k_w'], 'L0_attn_v_w': _L0_attn_in['v_w'], 'L0_attn_g_w': _L0_attn_in['g_w'], 'L0_attn_w_w': _L0_attn_in['w_w'], 'L0_attn_out_w': _L0_attn_in['out_w'], 'L0_attn_gn_weight': _L0_attn_in['gn_weight'], 'L0_attn_gn_bias': _L0_attn_in['gn_bias'], 'L0_ffn_w_qr': _L0_ffn_in['w_qr'], 'L0_ffn_w_kvr': _L0_ffn_in['w_kvr'], 'L0_ffn_w_q': _L0_ffn_in['w_q'], 'L0_ffn_w_kv': _L0_ffn_in['w_kv'], 'L0_ffn_w_out': _L0_ffn_in['w_out'], 'L0_ffn_null_kv': _L0_ffn_in['null_kv'], 'L0_ffn_null_token': _L0_ffn_in['null_token'], 'L1_attn_W_in': _L1_attn_in['W_in'], 'L1_attn_b_in': _L1_attn_in['b_in'], 'L1_attn_W_g': _L1_attn_in['W_g'], 'L1_attn_b_g': _L1_attn_in['b_g'], 'L1_attn_W_out': _L1_attn_in['W_out'], 'L1_attn_b_out': _L1_attn_in['b_out'], 'L1_ffn_Wq': _L1_ffn_in['Wq'], 'L1_ffn_Wkv': _L1_ffn_in['Wkv'], 'L1_ffn_Ws': _L1_ffn_in['Ws'], 'L1_ffn_Wd': _L1_ffn_in['Wd'], 'L1_ffn_Wo': _L1_ffn_in['Wo']}
    _x0 = _d['L0_attn_x']
    _d['L0_attn_x'] = jax.random.normal(jax.random.fold_in(jax.random.key(seed), 1), (8, 512, 128), dtype=_x0.dtype)
    del _x0
    return _d

def reference(L0_attn_x, L0_attn_ddlerp_w, L0_attn_mix_r, L0_attn_mix_k, L0_attn_mix_v, L0_attn_mix_g, L0_attn_mix_w, L0_attn_r_w, L0_attn_k_w, L0_attn_v_w, L0_attn_g_w, L0_attn_w_w, L0_attn_out_w, L0_attn_gn_weight, L0_attn_gn_bias, L0_ffn_w_qr, L0_ffn_w_kvr, L0_ffn_w_q, L0_ffn_w_kv, L0_ffn_w_out, L0_ffn_null_kv, L0_ffn_null_token, L1_attn_W_in, L1_attn_b_in, L1_attn_W_g, L1_attn_b_g, L1_attn_W_out, L1_attn_b_out, L1_ffn_Wq, L1_ffn_Wkv, L1_ffn_Ws, L1_ffn_Wd, L1_ffn_Wo):

    def _L0_attn_ref(x, ddlerp_w, mix_r, mix_k, mix_v, mix_g, mix_w, r_w, k_w, v_w, g_w, w_w, out_w, gn_weight, gn_bias):
        import jax, jax.numpy as jnp
        import numpy as np
        D = 128
        H = 16
        DH = D // H
        B = 2
        T = 256
        GN_EPS = 0.00064

        def _wkv_scan(r, k, v, w):

            def step(state, inp):
                r_t, k_t, v_t, w_t = inp
                state = state * jnp.exp(w_t)[..., None] + k_t[..., None] * v_t[..., None, :]
                o_t = jnp.einsum('bhkv,bhv->bhk', state, r_t)
                return (state, o_t)
            tm = lambda a: jnp.swapaxes(a, 0, 1)
            state0 = jnp.zeros((r.shape[0], H, DH, DH), dtype=r.dtype)
            _, out = jax.lax.scan(step, state0, (tm(r), tm(k), tm(v), tm(w)))
            return jnp.swapaxes(out, 0, 1)
        Bc, Tc, Dc = x.shape
        x_shift = jnp.pad(x, ((0, 0), (1, 0), (0, 0)))[:, :Tc]
        dd = jax.nn.sigmoid(jnp.tanh(jnp.einsum('btd,ed->bte', x_shift, ddlerp_w)))

        def lerp(mix):
            m = mix + dd * (1.0 - mix)
            return x * m + x_shift * (1.0 - m)
        proj = lambda a, wgt: jnp.einsum('btd,ed->bte', a, wgt)
        r = proj(lerp(mix_r), r_w)
        k = proj(lerp(mix_k), k_w)
        v = proj(lerp(mix_v), v_w)
        g = jax.nn.silu(proj(lerp(mix_g), g_w))
        w = -jax.nn.softplus(-proj(lerp(mix_w), w_w)) - 0.5
        shape4 = (Bc, Tc, H, DH)
        out = _wkv_scan(r.reshape(shape4), k.reshape(shape4), v.reshape(shape4), w.reshape(shape4))
        mu = out.mean(axis=-1, keepdims=True)
        var = out.var(axis=-1, keepdims=True)
        out = (out - mu) / jnp.sqrt(var + GN_EPS)
        out = out * gn_weight.reshape(H, DH) + gn_bias.reshape(H, DH)
        out = out.reshape(Bc, Tc, Dc)
        return jnp.einsum('btd,ed->bte', out * g, out_w)

    def _L0_ffn_ref(x, w_qr, w_kvr, w_q, w_kv, w_out, null_kv, null_token):
        import jax, jax.numpy as jnp
        import numpy as np
        NQ, NK, H, DH = (128, 64, 8, 64)
        b, n, d = x.shape
        g = w_qr.shape[0]
        bidx = jnp.arange(b)[:, None, None]
        q_logits = jnp.einsum('bnd,gd->bgn', x, w_qr)
        q_top, q_idx = jax.lax.top_k(q_logits, NQ)
        q_scores = jax.nn.sigmoid(q_top)[..., None]
        queries = x[bidx, q_idx]
        kv_logits = jnp.einsum('bnd,gd->bgn', x, w_kvr)
        kv_top, kv_idx = jax.lax.top_k(kv_logits, NK)
        kv_scores = jax.nn.sigmoid(kv_top)[:, :, None, :, None]
        key_values = x[bidx, kv_idx]
        q = jnp.einsum('bgnd,ged->bgne', queries, w_q)
        kv = jnp.einsum('bgnd,ged->bgne', key_values, w_kv)
        k, v = jnp.split(kv, 2, axis=-1)
        heads = lambda t: t.reshape(b, g, -1, H, DH).transpose(0, 1, 3, 2, 4)
        q, k, v = (heads(q), heads(k), heads(v))
        v = v * kv_scores
        nk = jnp.broadcast_to(null_kv[0][None], (b, g, H, 1, DH))
        nv = jnp.broadcast_to(null_kv[1][None], (b, g, H, 1, DH))
        k = jnp.concatenate([nk, k], axis=-2)
        v = jnp.concatenate([nv, v], axis=-2)
        attn = jax.nn.softmax(jnp.einsum('bghid,bghjd->bghij', q, k) * DH ** (-0.5), axis=-1)
        o = jnp.einsum('bghij,bghjd->bghid', attn, v)
        o = o.transpose(0, 1, 3, 2, 4).reshape(b, g, NQ, H * DH)
        o = jnp.einsum('bgne,gde->bgnd', o, w_out)
        o = o * q_scores
        flat_idx = q_idx.reshape(b, g * NQ)
        flat_o = o.reshape(b, g * NQ, d)
        b2 = jnp.arange(b)[:, None]
        summed = jnp.zeros_like(x).at[b2, flat_idx].add(flat_o)
        counts = jnp.zeros((b, n), x.dtype).at[b2, flat_idx].add(1.0)[..., None]
        meaned = summed / jnp.clip(counts, 1e-05)
        return jnp.where(counts > 0, meaned, null_token)

    def _L1_attn_ref(x, W_in, b_in, W_g, b_g, W_out, b_out):
        import jax, jax.numpy as jnp
        import numpy as np
        from jax import lax
        B, S, E, SD = (8, 512, 128, 8)

        def _reference_tuple_inner(x, W_in, b_in, W_g, b_g, W_out, b_out):
            embed_dim = W_in.shape[0]
            combined = jnp.einsum('bse,ec->bsc', x, W_in) + b_in
            embed = combined[..., :embed_dim]
            state_in = combined[..., embed_dim:]
            gate = jax.nn.sigmoid(jnp.einsum('bsc,cd->bsd', combined, W_g) + b_g)

            def step(state, gs):
                g, si = gs
                new = g * state + (1.0 - g) * si
                return (new, new)
            state0 = jnp.zeros((x.shape[0], state_in.shape[-1]), dtype=x.dtype)
            g_t = jnp.moveaxis(gate, 1, 0)
            si_t = jnp.moveaxis(state_in, 1, 0)
            final_state, states = lax.scan(step, state0, (g_t, si_t))
            states = jnp.moveaxis(states, 0, 1)
            out = jnp.einsum('bsc,cd->bsd', jnp.concatenate([embed, states], axis=-1), W_out) + b_out
            return (out, final_state)
        return _reference_tuple_inner(x, W_in, b_in, W_g, b_g, W_out, b_out)[0]

    def _L1_ffn_ref(x, Wq, Wkv, Ws, Wd, Wo):
        import jax, jax.numpy as jnp
        import numpy as np
        B, T, DIM = (4, 128, 128)
        H, E, DH, K = (8, 5, 64, 3)

        def _topk_mask(s, k):
            idx = jax.lax.top_k(s, k)[1]
            return jnp.sum(jax.nn.one_hot(idx, s.shape[-1], dtype=s.dtype), axis=-2)
        b, t, _ = x.shape
        scale = DH ** (-0.5)
        ss = jax.nn.sigmoid(x @ Ws).reshape(b, t, H, E)
        sd = jax.nn.sigmoid(x @ Wd).reshape(b, t, H, E)
        ms = _topk_mask(ss, K)
        md = _topk_mask(sd, K)
        ss_g = ss * ms
        sd_g = sd * md
        q5 = (x @ Wq).reshape(b, t, H, E, DH)
        kv = (x @ Wkv).reshape(b, t, 2, H, E, DH)
        k5, v5 = (kv[:, :, 0], kv[:, :, 1])
        q = jnp.einsum('bthed,bthe->bhtd', q5, sd_g)
        k = jnp.einsum('bthed,bthe->bhtd', k5, ss_g)
        v = jnp.einsum('bthed,bthe->bhtd', v5, ss_g)
        attn = jax.nn.softmax(jnp.einsum('bhid,bhjd->bhij', q * scale, k), axis=-1)
        out = jnp.einsum('bhij,bhjd->bihd', attn, v)
        o5 = jnp.einsum('bthd,dm->bthm', out, Wo).reshape(b, t, H, E, DIM)
        return jnp.einsum('bthem,bthe->btm', o5, md)
    x = L0_attn_x
    xn = _layernorm(x, axis=-1)
    x = x + _L0_attn_ref(xn, L0_attn_ddlerp_w, L0_attn_mix_r, L0_attn_mix_k, L0_attn_mix_v, L0_attn_mix_g, L0_attn_mix_w, L0_attn_r_w, L0_attn_k_w, L0_attn_v_w, L0_attn_g_w, L0_attn_w_w, L0_attn_out_w, L0_attn_gn_weight, L0_attn_gn_bias) + _L0_ffn_ref(xn, L0_ffn_w_qr, L0_ffn_w_kvr, L0_ffn_w_q, L0_ffn_w_kv, L0_ffn_w_out, L0_ffn_null_kv, L0_ffn_null_token)
    xn = _layernorm(x, axis=-1)
    x = x + _L1_attn_ref(xn, L1_attn_W_in, L1_attn_b_in, L1_attn_W_g, L1_attn_b_g, L1_attn_W_out, L1_attn_b_out) + _L1_ffn_ref(xn, L1_ffn_Wq, L1_ffn_Wkv, L1_ffn_Ws, L1_ffn_Wd, L1_ffn_Wo)
    return x

_drawn_inputs = setup_inputs


def setup_inputs(seed=0):
    import zlib

    import numpy as np

    out = dict(_drawn_inputs(seed))
    spreads = {'L0_attn_mix_r': (0.5, 0.6),
     'L0_attn_mix_k': (0.5, 0.6),
     'L0_attn_mix_v': (0.5, 0.6),
     'L0_attn_mix_g': (0.5, 0.6),
     'L0_attn_mix_w': (0.5, 0.6),
     'L0_attn_gn_weight': (1.0, 0.6),
     'L0_attn_gn_bias': (0.0, 0.8),
     'L1_attn_b_in': (0.0, 0.1),
     'L1_attn_b_g': (0.0, 2.0),
     'L1_attn_b_out': (0.0, 0.1)}
    factors = {'L0_attn_ddlerp_w': 8.0,
     'L0_attn_r_w': 6.34,
     'L0_attn_k_w': 6.318,
     'L0_attn_v_w': 6.294,
     'L0_attn_g_w': 6.256,
     'L0_attn_w_w': 8.0,
     'L0_attn_out_w': 6.209,
     'L0_ffn_null_kv': 4.107,
     'L1_ffn_Wq': 37.606,
     'L1_ffn_Ws': 14.231,
     'L1_ffn_Wd': 4.281,
     'L1_ffn_Wo': 2.842}
    for name, (base, spread) in spreads.items():
        noise = np.random.default_rng([zlib.crc32(name.encode()), seed]).standard_normal(out[name].shape)
        drawn = base * np.exp(spread * noise) if base else spread * noise
        out[name] = jnp.asarray(drawn.astype(out[name].dtype))
    for name, factor in factors.items():
        out[name] = (out[name] * factor).astype(out[name].dtype)
    return out
```

```python
from contextlib import ExitStack

import concourse.bass as bass
from concourse import mybir

F32 = mybir.dt.float32
I32 = mybir.dt.int32
ALU = mybir.AluOpType
ACT = mybir.ActivationFunctionType
X = mybir.AxisListType.X

P = 128
B, T, D = 8, 512, 128
NT = T // P
LN_EPS = 1e-5

AH, ADH = 16, 8
GN_EPS = 0.00064
NPAIR = 4

G, NQ, NK = 4, 128, 64
H, DH = 8, 64
HP = H // 2
NKEY = NK + 1
PICKED = -3.0e38
ROUNDS_Q, ROUNDS_K = NQ // 8, NK // 8

SD = 8
E, TOPK = 5, 3
KINDS = 3
CW = H * DH
SCALE = DH ** -0.5
NCHUNK = NT * KINDS * E
NATT = NT * H

Z_LO, Z_HI = -88.7, 16.6355


N_LOADS = 18


class Banks:

    def __init__(self, banks, filled, freed, units):
        self.banks, self.filled_sem, self.freed = banks, filled, freed
        self.at = {name: n for n, (name, _) in enumerate(units)}
        self.reader = [reader for _, reader in units]

    def bank(self, name):
        return self.banks[self.at[name] % len(self.banks)]

    def filled(self, name):
        return self.filled_sem, self.at[name] + 1

    def _read(self, n):
        who = self.reader[n]
        return self.freed[who], sum(1 for r in self.reader[:n + 1] if r == who)

    def free_for(self, name):
        n = self.at[name] - len(self.banks)
        return self._read(n) if n >= 0 else None

    def free_sem(self, name):
        return self.freed[self.reader[self.at[name]]]

    def was_read(self, name):
        return self._read(self.at[name])


def chunk_kind(c):
    return c // (KINDS * E), c // E % KINDS, c % E


def l0_stages():
    out = [("lerp",), ("proj",), ("gather",)]
    out += [("wkv", 0), ("scores", 0), ("scores", 1), ("wkv", 1), ("scores", 2), ("scores", 3),
            ("soft",), ("wkv", 2), ("norm",), ("wkv", 3), ("null",), ("gn",)]
    out += [("mix", g) for g in range(G)] + [("join",)]
    return out


def l1_stages():
    out = [("head",), ("gates",)]
    out += [("chunk", c) for c in range(NCHUNK + 2)]
    Z_LAG, F_LAG = 14, 15
    for a in range(NATT + 2):
        out.append(("att", a))
        for t in range(NT - 1):
            if a == H * t + Z_LAG:
                out.append(("z", t))
            if a == H * t + F_LAG:
                out.append(("fin", t))
    for t in range(NT):
        if H * t + Z_LAG > NATT + 1:
            if ("z", t) not in out:
                out.append(("z", t))
        if ("fin", t) not in out and ("z", t) in out:
            out.append(("fin", t))
    return out


def spread(l1, l0):
    out, k = [], 0
    weight = []
    for s in l1:
        weight.append(2.0 if s[0] == "att" else 1.0)
    total = sum(weight)
    done = 0.0
    for s, w in zip(l1, weight):
        out.append(("l1",) + s)
        done += w
        while k < len(l0) and k < done / total * (len(l0) + 1) - 0.5:
            out.append(("l0",) + l0[k])
            k += 1
    return out + [("l0",) + s for s in l0[k:]]


def layers(nc, x, ddw, mixes, projw, gnw, gnb, qkr, wqn, wkn, wvn, won, nkT, nvT, null_token,
           winT, winT8, wcat, wg, wg8, bin_, bin8, bg, wout, wout9, wqkv, wsd, wor, out):
    ctx = ExitStack()
    with ctx:
        def sb(name, shape, dt=F32):
            return ctx.enter_context(nc.sbuf_tensor(name, shape, dt))

        def sem(name):
            return ctx.enter_context(nc.semaphore(name))

        xn_d = nc.dram_tensor("xn_scratch", (B, P, NT * D), F32, kind="Internal").ap()
        xT_d = nc.dram_tensor("xT_scratch", (B, P, T), F32, kind="Internal").ap()
        posT_d = nc.dram_tensor("posT_scratch", (B, P, NT * 2 * G), F32, kind="Internal").ap()
        pos_d = nc.dram_tensor("pos_scratch", (B, G * T), F32, kind="Internal").ap()
        v_d = nc.dram_tensor("v_scratch", (D, T), F32, kind="Internal").ap()
        r_d = nc.dram_tensor("r_scratch", (D, T), F32, kind="Internal").ap()

        ident = sb("ident", [P, P])
        iota1 = sb("iota1", [P, P])
        iotac = sb("iotac", [P, 1])
        ddw_s = sb("ddw_s", [P, D])
        mix_s = sb("mix_s", [P, 5])
        projw_s = sb("projw_s", [P, 5, D])
        oww_s = sb("oww_s", [P, D])
        gnw_s = sb("gnw_s", [P, D])
        gnb_s = sb("gnb_s", [P, D])
        null_s = sb("null_s", [P, D])
        qkr_s = sb("qkr_s", [P, 2 * G])
        A_s = sb("A_s", [P, G, 2, HP, P])
        M_s = sb("M_s", [P, G, 2, HP, P])
        u9_s = sb("u9_s", [P, G, H + 1])
        nvw_s = sb("nvw_s", [G * H, G, D])
        wqkv_s = sb("wqkv_s", [P, KINDS, E, CW])
        wsd_s = sb("wsd_s", [P, 2 * H * E])
        wsi_s = sb("wsi_s", [P, SD])
        wgt_s = sb("wgt_s", [P, SD])
        wfold_s = sb("wfold_s", [P, D])
        ws9_s = sb("ws9_s", [SD + 1, D])
        wor_s = sb("wor_s", [P, 3, D])
        bsi_s = sb("bsi_s", [SD, 1])
        bgt_s = sb("bgt_s", [SD, 1])
        rank0 = sb("rank0", [P, E])

        xr = sb("xr", [P, NT, D])
        xn = sb("xn", [P, NT, D])
        xTp = sb("xTp", [P, T + 1])
        dif = sb("dif", [P, T])
        th = sb("th", [P, T])
        aa = sb("aa", [P, T])
        lp = sb("lp", [P, 2, T])
        kf = sb("kf", [P, T])
        dec = sb("dec", [P, T])
        silu = dif
        vb = sb("vb", [P, 2, 2, T])
        rb = sb("rb", [P, 2, 2, T])
        vf = vb[:, 1, 0, :]
        rf = rb[:, 1, 0, :]
        sel = sb("sel", [P, G * H * NKEY])
        skeys = sel[:, 0:G * H * NK].rearrange("p (n k) -> p n k", k=NK)
        snull = sel[:, G * H * NK:G * H * NKEY]
        selT = sb("selT", [P, G, T])
        posT = sb("posT", [P, NT, 2, G])
        xq = sb("xq", [P, G * NQ])
        xk = sb("xk", [P, G * NK])
        ax = sb("ax", [P, 2, H * NK])
        pt0 = sb("pt0", [P, 2, HP, NQ])
        vw = sb("vw", [P, 2, HP, D])
        ptn = sb("ptn", [G * H, NQ])
        ob = aa[:, :].rearrange("p (g d) -> p g d", g=G)
        sm = sb("sm", [P, G * (H + 1) + G])
        smt = sb("smt", [P, G * (H + 1) + G])
        hmax = sb("hmax", [P, G * H])
        hsum = sb("hsum", [P, G * H])
        mu = sb("mu", [P, NT * AH])
        va = sb("va", [P, NT * AH])
        ya = sb("ya", [P, NT * AH])
        wa = sb("wa", [P, NT * AH])
        cnt4 = sb("cnt4", [P, NT, G])
        cnt = sb("cnt", [P, NT])
        rcnt = sb("rcnt", [P, NT])
        nz = sb("nz", [P, NT])

        x1 = sb("x1", [P, NT, D])
        xn2 = sb("xn2", [P, NT, D])
        x2T = sb("x2T", [P, T])
        zg = sb("zg", [P, NT * 2 * H * E])
        sg = sb("sg", [P, NT * 2 * H * E])
        wins = sb("wins", [P, NT * 2 * H * E])
        yg = sb("yg", [P, E * CW])
        qk = sb("qk", [P, 2, HP, T])
        vv = sb("vv", [P, NT, CW])
        pr = sb("pr", [P, 3, T])
        beat = pr[:, 1, 0:NT * 2 * H * (E - 1)]
        pt = sb("pt", [P, 2, NT, P])
        oo = sb("oo", [P, 2, CW])
        zT = sb("zT", [P, 3, P])
        nmax = sb("nmax", [P, NATT])
        den = sb("den", [P, NATT])
        rden = sb("rden", [P, NATT])
        st9 = sb("st9", [SD + 1, T])
        stats = sb("stats", [P, 4 * B, 6])
        mv = sb("mv", [P, 4 * B, 2])
        lv = sb("lv", [P, 4 * B])
        ly = sb("ly", [P, 4 * B])
        lw = sb("lw", [P, 4 * B])

        MAGIC = 0x5F3759DF

        bank = [ctx.enter_context(nc.psum_tensor(f"bank{k}", [P, 512], F32)) for k in range(8)]

        it_end = sem("it_end")
        it_go = sem("it_go")

        step_sems = []

        def ssem(name):
            s = sem(name)
            step_sems.append(s)
            return s

        out_sent = ssem("out_sent")
        p_ld = ssem("p_ld"); p_ldx = ssem("p_ldx"); p_ldw = ssem("p_ldw"); p_cst = ssem("p_cst")
        p_bn = ssem("p_bn"); p_nt = ssem("p_nt"); p_xn = ssem("p_xn"); p_wr = ssem("p_wr")
        p_fill = ssem("p_fill"); p_act = ssem("p_act"); p_dve = ssem("p_dve")
        p_top = ssem("p_top"); p_pos = ssem("p_pos"); p_posT = ssem("p_posT"); p_zero = ssem("p_zero")
        p_blk = ssem("p_blk"); p_log = ssem("p_log"); p_st = [ssem(f"p_st{s}") for s in range(2)]; p_misc = ssem("p_misc")
        p_ld2 = ssem("p_ld2")
        ld_x = ssem("ld_x"); ld_xn = ssem("ld_xn"); ld_xT = ssem("ld_xT")
        ld_posT = ssem("ld_posT"); ld_pos = ssem("ld_pos")
        dif_ready = ssem("dif_ready"); th_done = ssem("th_done"); e_done = ssem("e_done")
        af_ready = ssem("af_ready"); lerp_ready = ssem("lerp_ready")
        r_fill = ssem("r_fill"); r_act = ssem("r_act"); r_dve = ssem("r_dve")
        yT_fill = ssem("yT_fill"); yT_read = ssem("yT_read"); att_fill = ssem("att_fill")
        vr_sent = ssem("vr_sent"); tg_done = ssem("tg_done"); dec_ready = ssem("dec_ready")
        vb_in = [ssem(f"vb_in{s}") for s in range(2)]
        rb_in = [ssem(f"rb_in{s}") for s in range(2)]
        kv_done = ssem("kv_done"); scan_done = ssem("scan_done"); prod_done = ssem("prod_done")
        ot_done = ssem("ot_done")
        sel_ready = ssem("sel_ready"); selT_ready = ssem("selT_ready")
        smt_done = ssem("smt_done"); sig_ready = ssem("sig_ready")
        soft = ssem("soft"); e0_done = ssem("e0_done"); p0_ready = ssem("p0_ready")
        gn = ssem("gn"); sq_done = ssem("sq_done"); gnp = ssem("gnp"); y_ready = ssem("y_ready")
        cnt_s = ssem("cnt_s"); base_s = ssem("base_s"); join_s = ssem("join_s"); x1_new = ssem("x1_new")
        x1_copied = ssem("x1_copied"); ln_s = ssem("ln_s"); xn2_ready = ssem("xn2_ready")
        t_fill = ssem("t_fill"); t_act = ssem("t_act"); t_dve = ssem("t_dve")
        y_fill = ssem("y_fill"); y_act = ssem("y_act"); y_dve = ssem("y_dve")
        o_dve = ssem("o_dve")
        ex_s = ssem("ex_s"); rank_s = ssem("rank_s"); gates_ready = ssem("gates_ready")
        sc_s = ssem("sc_s"); st_ready = ssem("st_ready")
        v_add = ssem("v_add"); max_done = ssem("max_done"); rden_s = ssem("rden_s")
        tr_part = ssem("tr_part"); z_read = ssem("z_read"); pv_done = ssem("pv_done")
        zm_ready = ssem("zm_ready"); zt_done = ssem("zt_done"); fin_fill = ssem("fin_fill")
        lo_sem, hi_sem = step_sems[0].num, step_sems[-1].num
        assert [s.num for s in step_sems] == list(range(lo_sem, hi_sem + 1)), [s.num for s in step_sems]

        p_units = [(f"xT{b}", "act") for b in range(B)]
        p_units += [(f"fold{k}", "act") for k in range(4 * G)]
        p_units += [("u", "act"), ("nvw", "act"), ("wf", "act"), ("ws9", "act"), ("wmisc", "dve")]
        PB = Banks(bank[0:7], p_fill, {"act": p_act, "dve": p_dve}, p_units)
        LG = bank[7]

        r_units = [("dd", "act"), ("v", "act"), ("r", "act"), ("k", "act"), ("w", "act"), ("g", "dve"),
                   ("gq", "act"), ("gk", "act"), ("small", "dve")]
        for g in range(G):
            r_units += [(f"ax{g}", "act"), (f"s{g}", "dve")]
        r_units += [("ptn", "act")]
        for g in range(G):
            r_units += [(f"pt{g}", "act"), (f"vw{g}", "dve"), (f"o{g}", "act")]
        r_units += [("scat", "dve")]
        RB = Banks(bank[5:7], r_fill, {"act": r_act, "dve": r_dve}, r_units)
        NBK = bank[7]

        t_units = [("xT", "act"), ("gates", "dve")]
        t_units += [(f"qk{u}", "act") for u in range(2 * NT)]
        for s in l1_stages():
            if s[0] == "att" and 1 <= s[1] <= NATT:
                t_units.append((f"pt{s[1] - 1}", "act" if s[1] % 2 else "dve"))
            if s[0] == "z":
                t_units.append((f"z{s[1]}", "fin"))
        TB = Banks(bank[2:4], t_fill, {"act": t_act, "dve": t_dve, "fin": z_read}, t_units)
        y_units = [("si", "dve"), ("gt", "act")]
        y_units += [(f"y{c}", "dve") for c in range(NCHUNK)]
        y_units += [(f"s{a}", "act") for a in range(NATT)]
        YB = Banks(bank[0:2], y_fill, {"act": y_act, "dve": y_dve}, y_units)
        OB = Banks(bank[4:5], pv_done, {"dve": o_dve}, [(f"o{t}", "dve") for t in range(NT)])

        def qk_before(c):
            return sum(1 for k in range(c) if chunk_kind(k)[1] < 2)

        def v_before(c):
            return sum(1 for k in range(c) if chunk_kind(k)[1] == 2)

        def yg_slot(c):
            s = qk_before(c) % 3 if chunk_kind(c)[1] < 2 else 3 + v_before(c) % 2
            return yg[:, s * CW:(s + 1) * CW]

        stage = {}
        stage["wq"] = qk[:, :, :, :].rearrange("p a b c -> p (a b c)")[:, 0:2048].rearrange("p (g c f) -> p g c f", g=G, c=HP)
        stage["wk"] = qk[:, :, :, :].rearrange("p a b c -> p (a b c)")[:, 2048:4096].rearrange("p (g c f) -> p g c f", g=G, c=HP)
        stage["wv"] = vv[:, :, :].rearrange("p a b -> p (a b)").rearrange("p (g c f) -> p g c f", g=G, c=HP)
        stage["wo"] = yg[:, 0:2048].rearrange("p (g c f) -> p g c f", g=G, c=HP)
        nkt = rden[:, 0:16].rearrange("p (g c) -> p g c", g=G)
        nvt = rden[:, 16:32].rearrange("p (g c) -> p g c", g=G)
        nkb = den[:, 0:32].rearrange("p (g c a) -> p g c a", g=G, c=HP)
        nvb = pr[:, 0, :].rearrange("p (g n) -> p g n", g=G)
        xa = vb[:, :, :, :].rearrange("p a b c -> p (a b c)")
        xb = rb[:, :, :, :].rearrange("p a b c -> p (a b c)")
        xt_ev = ax
        wr_pad = lp[:, :, :].rearrange("p a b -> p (a b)")[:, 0:B * 64].rearrange("p (b n) -> p b n", b=B)
        lgw = aa[0:64, :]
        msk = dif[0:64, :]
        onesr = th[0:64, :]
        cum = kf[0:64, :]
        top8 = hmax[0:64, 0:8]
        posTb = x1[:, :, :].rearrange("p a b -> p (a b)")[:, 0:B * NT * 2 * G].rearrange("p (b t k g) -> p b t k g", b=B, t=NT, k=2)
        winT_s = x2T[:, 0:P]
        winT8_s = x2T[0:SD, P:2 * P]
        wg_s = x2T[:, 256:256 + SD]
        wg8_s = x2T[0:SD, 264:264 + SD]
        bin_s = x2T[:, 272:273]
        bin8_s = x2T[0:SD, 273:274]
        bg_s = x2T[0:SD, 274:275]
        bcol9 = x2T[:, 275:275 + SD + 1]
        wout_s = xn2[:, 0, :]
        wout9_s = xn2[0:SD + 1, 1, :]

        block = ctx.enter_context(nc.Block())

        def newton(eng, y, v, w, n, sem_, base):
            eng.tensor_scalar(w[:, 0:n].bitcast(I32), v[:, 0:n].bitcast(I32), 1, None,
                              ALU.logical_shift_right).then_inc(sem_, 1)
            eng.wait_ge(sem_, base + 1)
            eng.tensor_scalar(y[:, 0:n].bitcast(I32), w[:, 0:n].bitcast(I32), -1.0, float(MAGIC),
                              ALU.mult, ALU.add).then_inc(sem_, 1)
            eng.wait_ge(sem_, base + 2)
            for k in range(4):
                eng.scalar_tensor_tensor(out=w[:, 0:n], in0=y[:, 0:n], scalar=-0.5, in1=y[:, 0:n],
                                         op0=ALU.mult, op1=ALU.mult).then_inc(sem_, 1)
                eng.wait_ge(sem_, base + 3 * k + 3)
                eng.tensor_tensor(w[:, 0:n], w[:, 0:n], v[:, 0:n], ALU.mult).then_inc(sem_, 1)
                eng.wait_ge(sem_, base + 3 * k + 4)
                eng.scalar_tensor_tensor(out=y[:, 0:n], in0=w[:, 0:n], scalar=1.5, in1=y[:, 0:n],
                                         op0=ALU.add, op1=ALU.mult).then_inc(sem_, 1)
                eng.wait_ge(sem_, base + 3 * k + 5)
            return base + 14

        NEWTON = 14

        def step_over(eng, n):
            eng.drain().then_inc(it_end, 1)
            eng.wait_ge(it_go, n)

        def run(stages, names):
            for s in names:
                f = stages.get(s[0:2])
                if f is not None:
                    f(*s[2:])

        L0 = [("l0",) + s for s in l0_stages()]
        L1 = [("l1",) + s for s in l1_stages()]
        BODY = spread(l1_stages(), l0_stages())

        @block.sync
        def _(sp):
            sp.dma_start(qkr_s[:, :], qkr).then_inc(p_ldw, 16)
            for b in range(B):
                src, k = (xa, b) if b < 4 else (xb, b - 4)
                sp.dma_start(src[:, k * T:(k + 1) * T].rearrange("p (t d) -> p t d", t=NT),
                             x[b].rearrange("(t p) d -> p t d", p=P)).then_inc(p_ldx, 16)
            loads = [(stage["wq"], wqn), (stage["wk"], wkn), (stage["wv"], wvn), (stage["wo"], won),
                     (nkt, nkT), (nvt, nvT), (winT_s, winT), (winT8_s, winT8), (wg_s, wg), (wg8_s, wg8),
                     (bin_s, bin_), (bin8_s, bin8), (bg_s, bg), (wout_s, wout), (wout9_s, wout9),
                     (bsi_s[:, :], bin8), (gnw_s[:, :], gnw.partition_broadcast(P)), (gnb_s[:, :], gnb.partition_broadcast(P))]
            loads2 = [(wsi_s[:, :], wcat), (ddw_s[:, :], ddw), (mix_s[:, :], mixes), (projw_s[:, :, :], projw[:, 0:5, :]),
                     (oww_s[:, :], projw[:, 5, :]), (null_s[:, :], null_token.partition_broadcast(P)),
                     (wqkv_s[:, :, :, :], wqkv), (wsd_s[:, :], wsd), (wor_s[:, 0:2, :], wor[0:2].rearrange("c p m -> p c m")),
                     (wor_s[0:DH, 2, :], wor[2, 0:DH])]
            for dst, src in loads:
                sp.dma_start(dst, src, allow_slow_non_contiguous=True).then_inc(p_ld, 16)
            for dst, src in loads2:
                sp.dma_start(dst, src, allow_slow_non_contiguous=True).then_inc(p_ld2, 16)
            assert len(loads) == N_LOADS
            for b in range(B):
                src, k = (xa, b) if b < 4 else (xb, b - 4)
                sp.wait_ge(p_xn, NT * (b + 1))
                sp.dma_start(xn_d[b], src[:, k * T:(k + 1) * T]).then_inc(p_wr, 16)
                sp.wait_ge(p_act, PB.was_read(f"xT{b}")[1])
                sp.dma_start(xT_d[b], xt_ev[:, b % 2, :]).then_inc(p_st[b % 2], 16)
            sp.wait_ge(p_pos, 1)
            sp.dma_start(pos_d.rearrange("b (g t) -> (b g) t", g=G), cum[0:B * G, :]).then_inc(p_wr, 16)
            sp.wait_ge(p_pos, 2)
            sp.dma_start(posT_d.rearrange("b p n -> p b n"),
                         posTb.rearrange("p b t k g -> p b (t k g)")).then_inc(p_wr, 16)
            sp.wait_ge(p_wr, 16 * (B + 2))
            for s in p_st:
                sp.wait_ge(s, 16 * B // 2)
            sp.wait_ge(p_ld2, 16 * len(loads2))

            def next_step():
                sp.wait_ge(it_end, 4)
                sp.sem_clear(range(lo_sem, hi_sem + 1))
                sp.sem_clear(it_end)
                sp.sem_inc(it_go, 1)

            next_step()

            def stages_of(l0_b, l1_b):
                def l0_load():
                    one = bass.ds(l0_b, 1)
                    sp.dma_start(xTp[:, 1:T + 1], xT_d[one].rearrange("a p t -> (a p) t")).then_inc(ld_xT, 16)
                    sp.dma_start(xn[:, :, :].rearrange("p t d -> p (t d)"),
                                 xn_d[one].rearrange("a p t -> (a p) t")).then_inc(ld_xn, 16)
                    sp.dma_start(posT[:, :, :, :].rearrange("p t k g -> p (t k g)"),
                                 posT_d[one].rearrange("a p n -> (a p) n")).then_inc(ld_posT, 16)
                    sp.dma_start(selT[:, :, :].rearrange("p g t -> p (g t)"),
                                 pos_d[one].broadcast_to((P, G * T))).then_inc(ld_pos, 16)
                    if l1_b is not None:
                        sp.wait_ge(x1_copied, 1)
                        sp.wait_ge(xn2_ready, NT)
                    sp.dma_start(xr[:, :, :], x[one].rearrange("a (t p) d -> p (a t) d", p=P)).then_inc(ld_x, 16)

                def pair(dst, src, q, s):
                    for k in range(ADH):
                        sp.dma_start(dst[k:P:ADH, q % 2, :, :].rearrange("p j t -> p (j t)"),
                                     src.rearrange("(h q j) t -> q h (j t)", q=NPAIR, j=2)[q]).then_inc(s[q % 2], 16)

                def l0_proj():
                    sp.wait_ge(*RB.was_read("v"))
                    sp.dma_start(v_d, vf).then_inc(vr_sent, 16)
                    sp.wait_ge(*RB.was_read("r"))
                    sp.dma_start(r_d, rf).then_inc(vr_sent, 16)
                    sp.wait_ge(vr_sent, 32)
                    for q in range(2):
                        pair(vb, v_d, q, vb_in)
                        pair(rb, r_d, q, rb_in)

                def l0_wkv(q):
                    if q + 2 < NPAIR:
                        sp.wait_ge(ot_done, q + 1)
                        pair(vb, v_d, q + 2, vb_in)
                        pair(rb, r_d, q + 2, rb_in)

                def l1_store():
                    sp.wait_ge(*TB.was_read(f"z{NT - 1}"))
                    sp.dma_start(out[bass.ds(l1_b, 1)].rearrange("a (t p) d -> p (a t) d", p=P),
                                 x1[:, :, :]).then_inc(out_sent, 16)
                return l0_load, {("l0", "proj"): l0_proj, ("l0", "wkv"): l0_wkv}, l1_store

            load, st, _ = stages_of(0, None)
            load()
            run(st, L0)
            next_step()
            with sp.Fori(0, B - 1) as i:
                load, st, store = stages_of(i + 1, i)
                load()
                run(st, BODY)
                store()
                sp.wait_ge(out_sent, 16)
                next_step()
            _, st, store = stages_of(None, B - 1)
            store()
            sp.wait_ge(out_sent, 16)

        @block.gpsimd
        def _(gp):
            gp.memset(ident[:, :], 0.0).then_inc(p_cst, 1)
            gp.wait_ge(p_cst, 1)
            gp.affine_select(out=ident[:, :], in_=ident[:, :], compare_op=ALU.not_equal, fill=1.0, base=0,
                             pattern=[[-1, P]], channel_multiplier=1).then_inc(p_cst, 1)
            gp.iota(iota1[:, :], [[1, P]], base=1, channel_multiplier=0,
                    allow_small_or_imprecise_dtypes=True).then_inc(p_cst, 1)
            gp.iota(iotac[:, :], [[1, 1]], base=1, channel_multiplier=1,
                    allow_small_or_imprecise_dtypes=True).then_inc(p_cst, 1)
            gp.iota(rank0[:, :], [[1, E]], base=0, channel_multiplier=0,
                    allow_small_or_imprecise_dtypes=True).then_inc(p_cst, 1)
            gp.memset(xTp[:, 0:1], 0.0).then_inc(p_cst, 1)
            gp.memset(dec[:, 0:1], 0.0).then_inc(p_cst, 1)
            gp.memset(st9[:, :], 1.0).then_inc(p_cst, 1)
            gp.memset(onesr, 1.0).then_inc(p_cst, 1)
            step_over(gp, 1)

            def l0_lerp():
                gp.wait_ge(ld_xT, 16)
                gp.tensor_tensor(dif[:, :], xTp[:, 1:T + 1], xTp[:, 0:T], ALU.subtract).then_inc(dif_ready, 1)

            def l0_wkv(q):
                s = q % 2
                if q == 0:
                    gp.wait_ge(*RB.was_read("k"))
                gp.wait_ge(vb_in[s], 16 * ADH * (q // 2 + 1))
                gp.tensor_tensor(vb[:, s, :, :], vb[:, s, :, :],
                                 kf[:, :].unsqueeze(1).broadcast_to((P, 2, T)), ALU.mult).then_inc(kv_done, 1)
                gp.wait_ge(rb_in[s], 16 * ADH * (q // 2 + 1))
                gp.wait_ge(scan_done, 2 * q + 2)
                gp.tensor_tensor(vb[:, s, :, :], vb[:, s, :, :], rb[:, s, :, :], ALU.mult).then_inc(prod_done, 1)

            def l0_norm():
                gp.wait_ge(soft, 9)
                gp.tensor_tensor(skeys, skeys, hsum[:, :].unsqueeze(2).broadcast_to((P, G * H, NK)), ALU.mult)\
                  .then_inc(p0_ready, 1)
                gp.tensor_tensor(snull, snull, hsum[:, :], ALU.mult).then_inc(p0_ready, 1)

            def l0_gn():
                gp.wait_ge(gn, 2)
                gp.tensor_tensor(lp[:, 0, :], th[:, :], th[:, :], ALU.mult).then_inc(sq_done, 1)
                gp.wait_ge(gn, 5 + NEWTON)
                c = th[:, :].rearrange("p (t d) -> p t d", t=NT)
                gp.tensor_tensor(c, c, gnw_s[:, :].unsqueeze(1).broadcast_to((P, NT, D)), ALU.mult).then_inc(gnp, 1)
                gp.wait_ge(gnp, 1)
                gp.tensor_tensor(c, c, gnb_s[:, :].unsqueeze(1).broadcast_to((P, NT, D)), ALU.add).then_inc(gnp, 1)
                gp.wait_ge(gnp, 2)
                gp.wait_ge(*RB.was_read("g"))
                gp.tensor_tensor(th[:, :], th[:, :], silu[:, :], ALU.mult).then_inc(y_ready, 1)

            def l0_join():
                gp.wait_ge(cnt_s, 3)
                gp.wait_ge(ld_x, 16)
                gp.wait_ge(y_ready, 1)
                l3 = lp[:, 0, :].rearrange("p (t d) -> p t d", t=NT)
                gp.tensor_tensor(l3, null_s[:, :].unsqueeze(1).broadcast_to((P, NT, D)),
                                 nz[:, :].unsqueeze(2).broadcast_to((P, NT, D)), ALU.mult).then_inc(base_s, 1)
                gp.wait_ge(base_s, 1)
                gp.tensor_tensor(xr[:, :, :], xr[:, :, :], l3, ALU.add).then_inc(base_s, 1)
                gp.wait_ge(base_s, 2)
                gp.wait_ge(join_s, 1)
                gp.tensor_tensor(xr[:, :, :].rearrange("p t d -> p (t d)"),
                                 xr[:, :, :].rearrange("p t d -> p (t d)"), xq[:, :], ALU.add).then_inc(x1_new, 1)

            def l1_head():
                gp.tensor_copy(x1[:, :, :], xr[:, :, :]).then_inc(x1_copied, 1)

            def l1_chunk(n):
                c = n - 1
                if not 0 <= c < NCHUNK:
                    return
                t, kind, e = chunk_kind(c)
                if kind == 2 and e > 0:
                    m = v_before(c) - t - 1
                    gp.wait_ge(y_dve, YB.was_read(f"y{c}")[1])
                    if m > 0:
                        gp.wait_ge(v_add, m)
                    gp.tensor_tensor(vv[:, t, :], vv[:, t, :], yg_slot(c), ALU.add).then_inc(v_add, 1)

            def l1_att(a):
                if a >= H + 1 and (a - H - 1) % H == 0:
                    t = (a - H - 1) // H
                    gp.wait_ge(*OB.was_read(f"o{t}"))
                    if t > 0:
                        gp.wait_ge(*TB.filled(f"z{t - 1}"))
                    o4 = oo[:, t % 2, :].rearrange("p (h d) -> p h d", h=H)
                    m4 = wins[:, :].rearrange("p (t k h e) -> p t k h e", t=NT, k=2, h=H)[:, t, 1, :, :]
                    for half in range(2):
                        hs = slice(half * 4, half * 4 + 4)
                        gp.tensor_tensor(
                            yg[:, :].rearrange("p (h e d) -> p h e d", h=H, e=E)[:, hs],
                            o4[:, hs].unsqueeze(2).broadcast_to((P, 4, E, DH)),
                            m4[:, hs].unsqueeze(3).broadcast_to((P, 4, E, DH)), ALU.mult).then_inc(zm_ready, 1)

            st = {("l0", "lerp"): l0_lerp, ("l0", "wkv"): l0_wkv, ("l0", "norm"): l0_norm, ("l0", "gn"): l0_gn,
                  ("l0", "join"): l0_join, ("l1", "head"): l1_head, ("l1", "chunk"): l1_chunk, ("l1", "att"): l1_att}
            run(st, L0)
            step_over(gp, 2)
            with gp.Fori(0, B - 1) as i:
                run(st, BODY)
                step_over(gp, i + 3)
            run(st, L1)

        @block.scalar
        def _(act):
            act.preload_act_table_set("exp_and_others")
            for b in range(B):
                act.wait_ge(*PB.filled(f"xT{b}"))
                if b >= 2:
                    act.wait_ge(p_st[b % 2], 16 * (b // 2))
                    act.wait_ge(p_log, b - 1)
                act.activation(xt_ev[:, b % 2, :], PB.bank(f"xT{b}")[:, :], ACT.Copy).then_inc(p_act, 1)
            for k in range(4 * G):
                act.wait_ge(*PB.filled(f"fold{k}"))
                g, which = k // 4, k % 4
                dst, scale = (A_s, SCALE) if which < 2 else (M_s, 1.0)
                act.activation(dst[:, g, which % 2, :, :].rearrange("p a b -> p (a b)"), PB.bank(f"fold{k}")[:, :],
                               ACT.Copy, scale=scale).then_inc(p_act, 1)
            act.wait_ge(*PB.filled("u"))
            act.activation(u9_s[:, :, 0:H], PB.bank("u")[:, 0:G * H].rearrange("p (g h) -> p g h", g=G),
                           ACT.Copy, scale=SCALE).then_inc(p_act, 1)
            act.wait_ge(*PB.filled("nvw"))
            act.activation(nvw_s[:, :, :].rearrange("p g d -> p (g d)"), PB.bank("nvw")[0:G * H, :], ACT.Copy).then_inc(p_act, 1)
            act.wait_ge(*PB.filled("wf"))
            act.activation(wfold_s[:, :], PB.bank("wf")[:, 0:D], ACT.Copy).then_inc(p_act, 1)
            act.wait_ge(*PB.filled("ws9"))
            act.activation(ws9_s[:, :], PB.bank("ws9")[0:SD + 1, 0:D], ACT.Copy).then_inc(p_act, 1)
            step_over(act, 1)

            def copy(unit, banks, dst, src, scale=1.0):
                act.wait_ge(*banks.filled(unit))
                act.activation(dst, src, ACT.Copy, scale=scale).then_inc(banks.free_sem(unit), 1)

            def l0_lerp():
                act.wait_ge(*RB.filled("dd"))
                act.activation(th[:, :], RB.bank("dd")[:, :], ACT.Tanh).then_inc(r_act, 1)
                act.wait_ge(r_act, 1)
                act.activation(th[:, :], th[:, :], ACT.Tanh, scale=0.5).then_inc(th_done, 1)

            def l0_proj():
                copy("v", RB, vf, RB.bank("v")[:, :])
                copy("r", RB, rf, RB.bank("r")[:, :])
                copy("k", RB, kf[:, :], RB.bank("k")[:, :])
                act.wait_ge(*RB.filled("w"))
                act.activation(dec[:, 1:T], RB.bank("w")[:, 1:T], ACT.Tanh, scale=0.5).then_inc(r_act, 1)
                act.wait_ge(*RB.filled("g"))
                act.activation(silu[:, :], RB.bank("g")[:, :], ACT.Tanh, scale=0.5).then_inc(tg_done, 1)

            def l0_gather():
                copy("gq", RB, xq[:, :], RB.bank("gq")[:, :])
                copy("gk", RB, xk[:, :], RB.bank("gk")[:, 0:G * NK])

            def l0_scores(g):
                if g == 0:
                    act.wait_ge(*RB.was_read("small"))
                    act.activation(smt[:, :], sm[:, :], ACT.Tanh, scale=0.5).then_inc(smt_done, 1)
                else:
                    act.wait_ge(*RB.filled(f"s{g - 1}"))
                copy(f"ax{g}", RB, ax[:, g % 2, :], RB.bank(f"ax{g}")[:, :])

            def l0_soft():
                act.wait_ge(soft, 5)
                act.activation(sel[:, :], sel[:, :], ACT.Exp).then_inc(e0_done, 1)

            def l0_null():
                copy("ptn", RB, ptn[:, :], RB.bank("ptn")[0:G * H, 0:NQ])

            def l0_mix(g):
                if g >= 2:
                    act.wait_ge(*RB.filled(f"o{g - 2}"))
                copy(f"pt{g}", RB, pt0[:, g % 2, :, :].rearrange("p a b -> p (a b)"), RB.bank(f"pt{g}")[:, :])
                copy(f"o{g}", RB, ob[:, g, :], RB.bank(f"o{g}")[:, 0:D])

            def l0_gn():
                act.wait_ge(yT_fill, 1)
                act.activation(lp[:, 1, :], NBK[:, :], ACT.Copy).then_inc(yT_read, 1)

            def l1_head():
                copy("xT", TB, x2T[:, :], TB.bank("xT")[:, :])

            def l1_gates():
                act.wait_ge(*TB.was_read("gates"))
                act.activation(sg[:, :], zg[:, :], ACT.Exp, scale=-1.0).then_inc(ex_s, 1)
                act.wait_ge(*YB.filled("gt"))
                act.activation(xn2[0:SD, :, :].rearrange("p a b -> p (a b)"), YB.bank("gt")[0:SD, :], ACT.Tanh,
                               bias=bgt_s[:, 0:1], scale=0.5).then_inc(y_act, 1)

            def l1_chunk(n):
                c = n - 2
                if 0 <= c < NCHUNK:
                    t, kind, e = chunk_kind(c)
                    if kind < 2 and e == E - 1:
                        copy(f"qk{2 * t + kind}", TB, qk[:, kind, :, t * P:(t + 1) * P],
                             TB.bank(f"qk{2 * t + kind}")[:, :].rearrange("p (c n) -> p c n", c=HP))

            def l1_att(a):
                if a < NATT:
                    act.wait_ge(max_done, a + 1)
                    if a >= 3:
                        act.wait_ge(*TB.filled(f"pt{a - 3}"))
                    act.activation(pr[:, a % 3, :], YB.bank(f"s{a}")[:, :], ACT.Exp, bias=nmax[:, a:a + 1],
                                   accum_out=den[:, a:a + 1]).then_inc(y_act, 1)
                n = a - 1
                if 0 <= n < NATT and TB.reader[TB.at[f"pt{n}"]] == "act":
                    if n >= 2:
                        act.wait_ge(pv_done, n - 1)
                    copy(f"pt{n}", TB, pt[:, n % 2, :, :].rearrange("p a b -> p (a b)"), TB.bank(f"pt{n}")[:, :])

            def l1_z(t):
                act.wait_ge(*TB.filled(f"z{t}"))
                if t > 0:
                    act.wait_ge(fin_fill, t)
                act.activation(zT[:, 0:2, :].rearrange("p a b -> p (a b)"), TB.bank(f"z{t}")[:, 0:2 * P],
                               ACT.Copy).then_inc(zt_done, 1)
                act.activation(zT[0:DH, 2, :], TB.bank(f"z{t}")[0:DH, 2 * P:3 * P], ACT.Copy).then_inc(zt_done, 1)

            st = {("l0", "lerp"): l0_lerp, ("l0", "proj"): l0_proj, ("l0", "gather"): l0_gather,
                  ("l0", "scores"): l0_scores, ("l0", "soft"): l0_soft, ("l0", "null"): l0_null,
                  ("l0", "mix"): l0_mix, ("l0", "gn"): l0_gn, ("l1", "head"): l1_head, ("l1", "gates"): l1_gates,
                  ("l1", "chunk"): l1_chunk, ("l1", "att"): l1_att, ("l1", "z"): l1_z}
            run(st, L0)
            step_over(act, 2)
            with act.Fori(0, B - 1) as i:
                run(st, BODY)
                step_over(act, i + 3)
            run(st, L1)

        @block.tensor
        def _(pe):
            def open_(banks, unit):
                f = banks.free_for(unit)
                if f is not None:
                    pe.wait_ge(*f)
                return banks.bank(unit)

            def logits(b):
                pe.wait_ge(*PB.was_read(f"xT{b}"))
                pe.matmul(LG[0:64, :], wr_pad[:, b, :], xt_ev[:, b % 2, :], start=(b == 0), stop=(b == B - 1))\
                  .then_inc(p_log, 1)
            pe.wait_ge(p_blk, 1)
            pe.wait_ge(p_cst, 9)
            for b in range(B):
                bk = open_(PB, f"xT{b}")
                pe.wait_ge(p_xn, NT * (b + 1))
                src, k = (xa, b) if b < 4 else (xb, b - 4)
                for t in range(NT):
                    mm = pe.transpose(bk[:, t * P:(t + 1) * P], src[:, k * T + t * D:k * T + (t + 1) * D], ident[:, :])
                mm.then_inc(p_fill, 1)
                if b >= 1:
                    logits(b - 1)
            logits(B - 1)
            pe.wait_ge(p_ld, 16 * N_LOADS)
            for g in range(G):
                for which in range(4):
                    bk = open_(PB, f"fold{4 * g + which}")
                    hp = slice((which % 2) * DH, (which % 2) * DH + DH)
                    l, r = (stage["wk"], stage["wq"]) if which < 2 else (stage["wv"], stage["wo"])
                    for c in range(HP):
                        mm = pe.matmul(bk[:, c * P:(c + 1) * P], l[hp, g, c, :], r[hp, g, c, :], start=True, stop=True)
                    mm.then_inc(p_fill, 1)
            pe.wait_ge(p_blk, 4)
            bk = open_(PB, "u")
            for g in range(G):
                for c in range(HP):
                    mm = pe.matmul(bk[:, g * H + 2 * c:g * H + 2 * c + 2], stage["wq"][:, g, c, :], nkb[:, g, c, :],
                                   start=True, stop=True)
            mm.then_inc(p_fill, 1)
            bk = open_(PB, "nvw")
            for g in range(G):
                for c in range(HP):
                    mm = pe.matmul(bk[0:G * H, g * D:(g + 1) * D], nvb[:, g, c * 32:(c + 1) * 32], stage["wo"][:, g, c, :],
                                   start=(c == 0), stop=(c == HP - 1))
            mm.then_inc(p_fill, 1)
            bk = open_(PB, "wf")
            pe.matmul(bk[:, 0:D], winT_s, wout_s, start=True, stop=True).then_inc(p_fill, 1)
            bk = open_(PB, "ws9")
            pe.matmul(bk[0:SD + 1, 0:D], bcol9, wout_s, start=True, stop=False)
            pe.matmul(bk[0:SD + 1, 0:D], ident[0:SD + 1, 0:SD + 1], wout9_s, start=False, stop=True).then_inc(p_fill, 1)
            bk = open_(PB, "wmisc")
            pe.matmul(bk[:, 0:SD], winT_s, wg_s, start=True, stop=False)
            pe.matmul(bk[:, 0:SD], winT8_s, wg8_s, start=False, stop=True)
            pe.matmul(bk[0:SD, SD:SD + 1], wg_s, bin_s, start=True, stop=False)
            pe.matmul(bk[0:SD, SD:SD + 1], wg8_s, bin8_s, start=False, stop=True).then_inc(p_fill, 1)
            pe.wait_ge(p_pos, 1)
            for t in range(NT):
                mm = pe.transpose(LG[:, t * 64:(t + 1) * 64], cum[:, t * P:(t + 1) * P], ident[0:64, 0:64])
            mm.then_inc(p_posT, 1)
            step_over(pe, 1)

            def l0_lerp():
                pe.wait_ge(ld_xT, 16)
                bk = open_(RB, "dd")
                pe.matmul(bk[:, :], ddw_s[:, :], xTp[:, 0:T], start=True, stop=True).then_inc(r_fill, 1)

            def l0_proj():
                for m, u in enumerate("vrkw"):
                    bk = open_(RB, u)
                    pe.wait_ge(lerp_ready, m + 1)
                    pe.matmul(bk[:, :], projw_s[:, m, :], lp[:, m % 2, :], start=True, stop=True).then_inc(r_fill, 1)
                bk = open_(RB, "g")
                pe.wait_ge(lerp_ready, 5)
                for t in range(NT):
                    mm = pe.matmul(bk[:, t * P:(t + 1) * P], lp[:, 0, t * P:(t + 1) * P], projw_s[:, 4, :],
                                   start=True, stop=True)
                mm.then_inc(r_fill, 1)

            def l0_gather():
                pe.wait_ge(ld_xn, 16)
                for n, (u, w) in enumerate((("gq", NQ), ("gk", NK))):
                    bk = open_(RB, u)
                    pe.wait_ge(sel_ready, n + 1)
                    for t in range(NT):
                        mm = pe.matmul(bk[:, 0:G * w], xn[:, t, :], sel[:, t * G * w:(t + 1) * G * w],
                                       start=(t == 0), stop=(t == NT - 1))
                    mm.then_inc(r_fill, 1)
                bk = open_(RB, "small")
                pe.wait_ge(*RB.was_read("gk"))
                for g in range(G):
                    n = G * (H + 1) + g
                    pe.matmul(bk[:, g * (H + 1):(g + 1) * (H + 1)], xq[:, g * NQ:(g + 1) * NQ], u9_s[:, g, :],
                              start=True, stop=True)
                    pe.matmul(bk[0:NK, n:n + 1], xk[:, g * NK:(g + 1) * NK], qkr_s[:, G + g:G + g + 1],
                              start=True, stop=True)
                    mm = pe.matmul(bk[NK:2 * NK, n:n + 1], xk[:, g * NK:(g + 1) * NK], qkr_s[:, G + g:G + g + 1],
                                   start=True, stop=True)
                mm.then_inc(r_fill, 1)

            def l0_scores(g):
                bk = open_(RB, f"ax{g}")
                for h in range(H):
                    mm = pe.matmul(bk[:, h * NK:(h + 1) * NK], A_s[:, g, h % 2, h // 2, :], xk[:, g * NK:(g + 1) * NK],
                                   start=True, stop=True)
                mm.then_inc(r_fill, 1)
                bk = open_(RB, f"s{g}")
                pe.wait_ge(*RB.was_read(f"ax{g}"))
                pe.matmul(bk[:, :], xq[:, g * NQ:(g + 1) * NQ], ax[:, g % 2, :], start=True, stop=True).then_inc(r_fill, 1)

            def l0_wkv(q):
                bk = NBK
                pe.wait_ge(prod_done, q + 1)
                for j in range(2):
                    for t in range(NT):
                        first, last = q == 0 and j == 0 and t == 0, q == NPAIR - 1 and j == 1
                        mm = pe.matmul(bk[:, t * P:(t + 1) * P], vb[:, q % 2, j, t * P:(t + 1) * P], ident[:, :],
                                       is_transpose=True, start=first, stop=last, skip_group_check=True)
                mm.then_inc(ot_done, 1)

            def l0_gn():
                bk = NBK
                pe.wait_ge(gn, 2)
                pe.wait_ge(y_ready, 1)
                for t in range(NT):
                    mm = pe.transpose(bk[:, t * P:(t + 1) * P], th[:, t * P:(t + 1) * P], ident[:, :])
                mm.then_inc(yT_fill, 1)
                pe.wait_ge(yT_read, 1)
                for t in range(NT):
                    mm = pe.matmul(bk[:, t * P:(t + 1) * P], lp[:, 1, t * P:(t + 1) * P], oww_s[:, :], start=True, stop=True)
                mm.then_inc(att_fill, 1)

            def l0_null():
                bk = open_(RB, "ptn")
                pe.wait_ge(p0_ready, 2)
                pe.transpose(bk[0:G * H, 0:NQ], snull, ident[:, :]).then_inc(r_fill, 1)

            def l0_mix(g):
                bk = open_(RB, f"pt{g}")
                for c in range(HP):
                    mm = pe.transpose(bk[:, c * NQ:(c + 1) * NQ], sel[:, (g * HP + c) * P:(g * HP + c + 1) * P], ident[:, :])
                mm.then_inc(r_fill, 1)
                bk = open_(RB, f"vw{g}")
                for hp in range(2):
                    mm = pe.matmul(bk[hp * NK:(hp + 1) * NK, :], xk[:, g * NK:(g + 1) * NK],
                                   M_s[:, g, hp, :, :].rearrange("p a b -> p (a b)"), start=True, stop=True)
                mm.then_inc(r_fill, 1)
                bk = open_(RB, f"o{g}")
                pe.wait_ge(*RB.was_read(f"pt{g}"))
                pe.wait_ge(*RB.was_read(f"vw{g}"))
                for c in range(HP):
                    pe.matmul(bk[:, 0:D], pt0[:, g % 2, c, :], vw[:, g % 2, c, :], start=(c == 0), stop=False)
                pe.matmul(bk[:, 0:D], ptn[:, :], nvw_s[:, g, :], start=False, stop=True).then_inc(r_fill, 1)

            def l0_join():
                bk = open_(RB, "scat")
                pe.wait_ge(selT_ready, 1)
                pe.wait_ge(*RB.was_read(f"o{G - 1}"))
                for t in range(NT):
                    for g in range(G):
                        mm = pe.matmul(bk[:, t * P:(t + 1) * P], selT[:, g, t * P:(t + 1) * P], ob[:, g, :],
                                       start=(g == 0), stop=(g == G - 1))
                mm.then_inc(r_fill, 1)

            def l1_head():
                bk = open_(TB, "xT")
                for t in range(NT):
                    pe.wait_ge(xn2_ready, t + 1)
                    mm = pe.transpose(bk[:, t * P:(t + 1) * P], xn2[:, t, :], ident[:, :])
                mm.then_inc(t_fill, 1)

            def l1_gates():
                bk = open_(TB, "gates")
                pe.wait_ge(*TB.was_read("xT"))
                n = 2 * H * E
                for t in range(NT):
                    mm = pe.matmul(bk[:, t * n:(t + 1) * n], x2T[:, t * P:(t + 1) * P], wsd_s[:, :], start=True, stop=True)
                mm.then_inc(t_fill, 1)
                pe.matmul(YB.bank("si")[0:SD, :], wsi_s[:, :], x2T[:, :], start=True, stop=True).then_inc(y_fill, 1)
                pe.matmul(YB.bank("gt")[0:SD, :], wgt_s[:, :], x2T[:, :], start=True, stop=True).then_inc(y_fill, 1)

            def l1_chunk(n):
                if n < NCHUNK:
                    t, kind, e = chunk_kind(n)
                    bk = open_(YB, f"y{n}")
                    pe.matmul(bk[:, :], x2T[:, t * P:(t + 1) * P], wqkv_s[:, kind, e, :], start=True, stop=True)\
                      .then_inc(y_fill, 1)
                c = n - 2
                if 0 <= c < NCHUNK:
                    t, kind, e = chunk_kind(c)
                    if kind < 2:
                        u = f"qk{2 * t + kind}"
                        bk = open_(TB, u) if e == 0 else TB.bank(u)
                        pe.wait_ge(y_dve, YB.was_read(f"y{c}")[1])
                        src = yg_slot(c)
                        for p_ in range(HP):
                            mm = pe.matmul(bk[:, p_ * P:(p_ + 1) * P], src[:, p_ * P:(p_ + 1) * P], ident[:, :],
                                           is_transpose=True, start=(e == 0 and p_ == 0), stop=(e == E - 1),
                                           skip_group_check=True)
                        mm.then_inc(t_fill if e == E - 1 else tr_part, 1)

            def l1_att(a):
                if a < NATT:
                    t, h = a // H, a % H
                    hs = slice((h % 2) * DH, (h % 2) * DH + DH)
                    bk = open_(YB, f"s{a}")
                    if a == 0:
                        pe.wait_ge(*TB.was_read(f"qk{2 * NT - 1}"))
                    pe.matmul(bk[:, :], qk[hs, 0, h // 2, t * P:(t + 1) * P], qk[hs, 1, h // 2, :], start=True, stop=True)\
                      .then_inc(y_fill, 1)
                n = a - 1
                if 0 <= n < NATT:
                    bk = open_(TB, f"pt{n}")
                    pe.wait_ge(*YB.was_read(f"s{n}"))
                    for c in range(NT):
                        mm = pe.transpose(bk[:, c * P:(c + 1) * P], pr[:, n % 3, c * P:(c + 1) * P], ident[:, :])
                    mm.then_inc(t_fill, 1)
                n = a - 2
                if 0 <= n < NATT:
                    t, h = n // H, n % H
                    bk = open_(OB, f"o{t}") if h == 0 else OB.bank(f"o{t}")
                    if n == 0:
                        pe.wait_ge(v_add, NT * (E - 1))
                    pe.wait_ge(*TB.was_read(f"pt{n}"))
                    for c in range(NT):
                        mm = pe.matmul(bk[:, h * DH:(h + 1) * DH], pt[:, n % 2, c, :], vv[:, c, h * DH:(h + 1) * DH],
                                       start=(c == 0), stop=(c == NT - 1))
                    mm.then_inc(pv_done, 1)

            def l1_z(t):
                bk = open_(TB, f"z{t}")
                for h in range(H):
                    if h % 4 == 0:
                        pe.wait_ge(zm_ready, 2 * t + h // 4 + 1)
                    for c in range(3):
                        w = min(P, E * DH - c * P)
                        k = h * E * DH + c * P
                        mm = pe.matmul(bk[0:w, c * P:(c + 1) * P], yg[:, k:k + w], ident[:, :], is_transpose=True,
                                       start=(h == 0 and c == 0), stop=(h == H - 1), skip_group_check=True)
                mm.then_inc(t_fill, 1)

            def l1_fin(t):
                bk = TB.bank(f"z{t}")[:, 3 * P:4 * P]
                pe.wait_ge(zt_done, 2 * t + 2)
                ts = slice(t * P, (t + 1) * P)
                if t == 0:
                    pe.wait_ge(st_ready, 1)
                pe.matmul(bk, x2T[:, ts], wfold_s[:, :], start=True, stop=False)
                pe.matmul(bk, st9[:, ts], ws9_s[:, :], start=False, stop=False)
                pe.matmul(bk, zT[:, 0, :], wor_s[:, 0, :], start=False, stop=False)
                pe.matmul(bk, zT[:, 1, :], wor_s[:, 1, :], start=False, stop=False)
                pe.matmul(bk, zT[0:DH, 2, :], wor_s[0:DH, 2, :], start=False, stop=True).then_inc(fin_fill, 1)

            st = {("l0", "lerp"): l0_lerp, ("l0", "proj"): l0_proj, ("l0", "gather"): l0_gather,
                  ("l0", "scores"): l0_scores, ("l0", "wkv"): l0_wkv, ("l0", "gn"): l0_gn, ("l0", "null"): l0_null,
                  ("l0", "mix"): l0_mix, ("l0", "join"): l0_join, ("l1", "head"): l1_head, ("l1", "gates"): l1_gates,
                  ("l1", "chunk"): l1_chunk, ("l1", "att"): l1_att, ("l1", "z"): l1_z, ("l1", "fin"): l1_fin}
            run(st, L0)
            step_over(pe, 2)
            with pe.Fori(0, B - 1) as i:
                run(st, BODY)
                step_over(pe, i + 3)
            run(st, L1)

        @block.vector
        def _(dve):
            dve.memset(wr_pad, 0.0).then_inc(p_zero, 1)
            dve.memset(nkb, 0.0).then_inc(p_zero, 1)
            dve.memset(nvb, 0.0).then_inc(p_zero, 1)
            dve.wait_ge(p_zero, 3)
            dve.wait_ge(p_ldw, 16)
            for b in range(B):
                for k in range(2):
                    last = dve.tensor_copy(wr_pad[:, b, k * 32 + b * G:k * 32 + (b + 1) * G], qkr_s[:, k * G:(k + 1) * G])
            last.then_inc(p_blk, 1)
            dve.wait_ge(p_ldx, 16 * B)

            def batch(b):
                src, k = (xa, b) if b < 4 else (xb, b - 4)
                return src[:, k * T:(k + 1) * T]

            for b in range(B):
                for t in range(NT):
                    last = dve.bn_stats(stats[:, b * NT + t, :], batch(b)[:, t * D:(t + 1) * D])
            last.then_inc(p_bn, 1)
            dve.wait_ge(p_bn, 1)
            for n in range(B * NT):
                last = dve.bn_aggr(mv[:, n, :], stats[:, n, :])
            last.then_inc(p_bn, 1)
            dve.wait_ge(p_bn, 2)
            dve.tensor_scalar(lv[:, :], mv[:, :, 1], LN_EPS, None, ALU.add).then_inc(p_nt, 1)
            dve.wait_ge(p_nt, 1)
            newton(dve, ly, lv, lw, B * NT, p_nt, 1)
            for n in range(B * NT):
                xt = batch(n // NT)[:, (n % NT) * D:(n % NT + 1) * D]
                dve.tensor_scalar(xt, xt, mv[:, n, 0:1], ly[:, n:n + 1], ALU.subtract, ALU.mult).then_inc(p_xn, 1)
            dve.wait_ge(p_ld, 16 * N_LOADS)
            dve.memset(bcol9, 0.0).then_inc(p_zero, 1)
            dve.wait_ge(p_zero, 4)
            dve.tensor_copy(bcol9[:, SD:SD + 1], bin_s)
            for hp in range(2):
                ps = slice(hp * DH, (hp + 1) * DH)
                dve.tensor_copy(nkb[ps, :, :, hp], nkt[ps, :, :])
                for g in range(G):
                    first = g * H + hp
                    dve.tensor_copy(nvb[ps, g, first:first + 34 * (HP - 1) + 1:34], nvt[ps, g, :])
            dve.tensor_copy(u9_s[:, :, H], qkr_s[:, 0:G])
            dve.tensor_scalar(gnw_s[:, :], gnw_s[:, :], 0.5, None, ALU.mult)
            dve.tensor_scalar(gnb_s[:, :], gnb_s[:, :], 0.5, None, ALU.mult).then_inc(p_blk, 3)
            dve.wait_ge(p_cst, 9)
            dve.wait_ge(p_log, B)
            dve.tensor_copy(lgw, LG[0:64, :]).then_inc(p_top, 1)
            n = 1
            for k in range(ROUNDS_Q):
                rows = slice(0, 64 if k < ROUNDS_K else 32)
                dve.wait_ge(p_top, n)
                dve.max(top8[rows], lgw[rows]).then_inc(p_top, 1)
                dve.wait_ge(p_top, n + 1)
                dve.match_replace(lgw[rows], top8[rows], lgw[rows], PICKED).then_inc(p_top, 1)
                n += 2
            dve.wait_ge(p_top, n)
            dve.tensor_scalar(msk, lgw, PICKED, None, ALU.is_le).then_inc(p_top, 1)
            dve.wait_ge(p_top, n + 1)
            dve.tensor_tensor_scan(cum, onesr, msk, 0.0, ALU.mult, ALU.add).then_inc(p_top, 1)
            dve.wait_ge(p_top, n + 2)
            dve.tensor_tensor(cum, cum, msk, ALU.mult).then_inc(p_pos, 1)
            dve.wait_ge(p_posT, 1)
            for k in range(2):
                last = dve.tensor_copy(posTb[:, :, :, k, :],
                                       LG[:, 0:NT * 64].rearrange("p (t k b g) -> p k b t g", t=NT, k=2, b=B)[:, k])
            last.then_inc(p_pos, 1)
            dve.wait_ge(*PB.filled("wmisc"))
            wm = PB.bank("wmisc")
            dve.tensor_copy(wgt_s[:, :], wm[:, 0:SD])
            dve.tensor_scalar(bgt_s[:, :], wm[0:SD, SD:SD + 1], bg_s, 0.5, ALU.add, ALU.mult).then_inc(p_dve, 1)
            step_over(dve, 1)

            def l0_lerp():
                dve.wait_ge(th_done, 1)
                dve.wait_ge(dif_ready, 1)
                dve.scalar_tensor_tensor(out=th[:, :], in0=th[:, :], scalar=1.0, in1=dif[:, :],
                                         op0=ALU.add, op1=ALU.mult).then_inc(e_done, 1)
                dve.wait_ge(e_done, 1)
                dve.scalar_tensor_tensor(out=aa[:, :], in0=th[:, :], scalar=0.5, in1=xTp[:, 0:T],
                                         op0=ALU.mult, op1=ALU.add).then_inc(af_ready, 1)
                dve.scalar_tensor_tensor(out=dif[:, :], in0=th[:, :], scalar=-0.5, in1=dif[:, :],
                                         op0=ALU.mult, op1=ALU.add).then_inc(af_ready, 1)
                dve.wait_ge(af_ready, 2)

            def l0_proj():
                for m in range(5):
                    if m >= 2:
                        dve.wait_ge(*RB.filled("vrk"[m - 2]))
                    dve.scalar_tensor_tensor(out=lp[:, m % 2, :], in0=dif[:, :], scalar=mix_s[:, m:m + 1], in1=aa[:, :],
                                             op0=ALU.mult, op1=ALU.add).then_inc(lerp_ready, 1)
                half = 0.5 * 0.6065306597126334
                dve.wait_ge(*RB.was_read("w"))
                dve.tensor_scalar(dec[:, 1:T], dec[:, 1:T], half, half, ALU.mult, ALU.add).then_inc(dec_ready, 1)
                dve.wait_ge(tg_done, 1)
                dve.wait_ge(*RB.filled("g"))
                dve.scalar_tensor_tensor(out=silu[:, :], in0=silu[:, :], scalar=1.0, in1=RB.bank("g")[:, :],
                                         op0=ALU.add, op1=ALU.mult).then_inc(r_dve, 1)

            def l0_gather():
                dve.wait_ge(ld_posT, 16)
                dve.tensor_tensor(sel[:, 0:NT * G * NQ].rearrange("p (t g j) -> p t g j", t=NT, g=G),
                                  iota1[:, 0:NQ].unsqueeze(1).unsqueeze(1).broadcast_to((P, NT, G, NQ)),
                                  posT[:, :, 0, :].unsqueeze(3).broadcast_to((P, NT, G, NQ)), ALU.is_equal)\
                   .then_inc(sel_ready, 1)
                dve.tensor_scalar(cnt4[:, :, :], posT[:, :, 0, :], 0.5, None, ALU.is_gt).then_inc(cnt_s, 1)
                dve.wait_ge(cnt_s, 1)
                dve.tensor_reduce(cnt[:, :], cnt4[:, :, :], X, ALU.add).then_inc(cnt_s, 1)
                dve.wait_ge(cnt_s, 2)
                dve.tensor_scalar(nz[:, :], cnt[:, :], 0.5, None, ALU.is_lt).then_inc(cnt_s, 1)
                dve.tensor_scalar(rcnt[:, :], cnt[:, :], 1.0, None, ALU.max).then_inc(cnt_s, 1)
                dve.wait_ge(cnt_s, 4)
                dve.reciprocal(rcnt[:, :], rcnt[:, :]).then_inc(cnt_s, 1)
                dve.wait_ge(ld_pos, 16)
                dve.tensor_scalar(selT[:, :, :], selT[:, :, :], iotac[:, 0:1], None, ALU.is_equal).then_inc(selT_ready, 1)
                dve.wait_ge(*RB.filled("gq"))
                dve.tensor_tensor(sel[:, 0:NT * G * NK].rearrange("p (t g j) -> p t g j", t=NT, g=G),
                                  iota1[:, 0:NK].unsqueeze(1).unsqueeze(1).broadcast_to((P, NT, G, NK)),
                                  posT[:, :, 1, :].unsqueeze(3).broadcast_to((P, NT, G, NK)), ALU.is_equal)\
                   .then_inc(sel_ready, 1)

            def l0_wkv(q):
                dve.wait_ge(dec_ready, 1)
                dve.wait_ge(kv_done, q + 1)
                for j in range(2):
                    v1 = vb[:, q % 2, j, :]
                    dve.tensor_tensor_scan(v1, dec[:, :], v1, 0.0, ALU.mult, ALU.add).then_inc(scan_done, 1)

            def l0_scores(g):
                if g == 0:
                    dve.wait_ge(*RB.filled("small"))
                    dve.tensor_copy(sm[:, :], RB.bank("small")[:, 0:G * (H + 1) + G]).then_inc(r_dve, 1)
                    dve.wait_ge(*RB.was_read("small"))
                    dve.tensor_copy(snull.rearrange("p (g h) -> p g h", g=G),
                                    sm[:, 0:G * (H + 1)].rearrange("p (g n) -> p g n", g=G)[:, :, 0:H]).then_inc(soft, 1)
                    dve.wait_ge(smt_done, 1)
                    dve.tensor_scalar(smt[:, :], smt[:, :], 0.5, 0.5, ALU.mult, ALU.add).then_inc(sig_ready, 1)
                dve.wait_ge(*RB.filled(f"s{g}"))
                dve.tensor_copy(sel[:, g * H * NK:(g + 1) * H * NK], RB.bank(f"s{g}")[:, :]).then_inc(r_dve, 1)

            def l0_soft():
                dve.wait_ge(soft, 1)
                dve.wait_ge(*RB.was_read(f"s{G - 1}"))
                dve.tensor_reduce(hmax[:, :], skeys, X, ALU.max).then_inc(soft, 1)
                dve.wait_ge(soft, 2)
                dve.tensor_tensor(hmax[:, :], hmax[:, :], snull, ALU.max).then_inc(soft, 1)
                dve.wait_ge(soft, 3)
                dve.tensor_tensor(snull, snull, hmax[:, :], ALU.subtract).then_inc(soft, 1)
                dve.tensor_tensor(skeys, skeys, hmax[:, :].unsqueeze(2).broadcast_to((P, G * H, NK)), ALU.subtract)\
                   .then_inc(soft, 1)

            def l0_norm():
                dve.wait_ge(e0_done, 1)
                dve.tensor_reduce(hsum[:, :], skeys, X, ALU.add).then_inc(soft, 1)
                dve.wait_ge(soft, 6)
                dve.tensor_tensor(hsum[:, :], hsum[:, :], snull, ALU.add).then_inc(soft, 1)
                dve.wait_ge(soft, 7)
                dve.reciprocal(hsum[:, :], hsum[:, :]).then_inc(soft, 1)
                dve.wait_ge(soft, 8)
                dve.wait_ge(sig_ready, 1)
                dve.tensor_tensor(hsum[:, :].rearrange("p (g h) -> p g h", g=G),
                                  hsum[:, :].rearrange("p (g h) -> p g h", g=G),
                                  smt[:, 0:G * (H + 1)].rearrange("p (g n) -> p g n", g=G)[:, :, H:H + 1]
                                  .broadcast_to((P, G, H)), ALU.mult).then_inc(soft, 1)

            def l0_mix(g):
                dve.wait_ge(*RB.filled(f"vw{g}"))
                if g >= 2:
                    dve.wait_ge(*RB.filled(f"o{g - 2}"))
                n = G * (H + 1) + g
                dve.tensor_scalar(vw[:, g % 2, :, :].rearrange("p c d -> p (c d)"), RB.bank(f"vw{g}")[:, :],
                                  smt[:, n:n + 1], None, ALU.mult).then_inc(r_dve, 1)

            def l0_gn():
                dve.wait_ge(ot_done, NPAIR)
                o3 = NBK[:, :].rearrange("p (n k) -> p n k", k=ADH)
                c3 = th[:, :].rearrange("p (n k) -> p n k", k=ADH)
                n = NT * AH
                dve.tensor_reduce(mu[:, :], o3, X, ALU.add).then_inc(gn, 1)
                dve.wait_ge(gn, 1)
                dve.scalar_tensor_tensor(out=c3, in0=mu[:, :].unsqueeze(2).broadcast_to((P, n, ADH)), scalar=-1.0 / ADH,
                                         in1=o3, op0=ALU.mult, op1=ALU.add).then_inc(gn, 1)
                dve.wait_ge(sq_done, 1)
                dve.tensor_reduce(va[:, :], lp[:, 0, :].rearrange("p (n k) -> p n k", k=ADH), X, ALU.add).then_inc(gn, 1)
                dve.wait_ge(gn, 3)
                dve.tensor_scalar(va[:, :], va[:, :], 1.0 / ADH, GN_EPS, ALU.mult, ALU.add).then_inc(gn, 1)
                dve.wait_ge(gn, 4)
                newton(dve, ya, va, wa, n, gn, 4)
                dve.tensor_tensor(c3, c3, ya[:, :].unsqueeze(2).broadcast_to((P, n, ADH)), ALU.mult).then_inc(gn, 1)

            def l0_join():
                x3 = xq[:, :].rearrange("p (t d) -> p t d", t=NT)
                dve.wait_ge(*RB.filled("scat"))
                dve.wait_ge(cnt_s, 5)
                dve.tensor_tensor(x3, RB.bank("scat")[:, :].rearrange("p (t d) -> p t d", t=NT),
                                  rcnt[:, :].unsqueeze(2).broadcast_to((P, NT, D)), ALU.mult).then_inc(r_dve, 1)
                dve.wait_ge(*RB.was_read("scat"))
                dve.wait_ge(att_fill, 1)
                dve.tensor_tensor(xq[:, :], xq[:, :], NBK[:, :], ALU.add).then_inc(join_s, 1)

            def l1_head():
                for t in range(NT):
                    last = dve.bn_stats(stats[:, t, :], xr[:, t, :])
                last.then_inc(ln_s, 1)
                dve.wait_ge(ln_s, 1)
                for t in range(NT):
                    last = dve.bn_aggr(mv[:, t, :], stats[:, t, :])
                last.then_inc(ln_s, 1)
                dve.wait_ge(ln_s, 2)
                dve.tensor_scalar(lv[:, 0:NT], mv[:, 0:NT, 1], LN_EPS, None, ALU.add).then_inc(ln_s, 1)
                dve.wait_ge(ln_s, 3)
                newton(dve, ly, lv, lw, NT, ln_s, 3)
                for t in range(NT):
                    dve.tensor_scalar(xn2[:, t, :], xr[:, t, :], mv[:, t, 0:1], ly[:, t:t + 1],
                                      ALU.subtract, ALU.mult).then_inc(xn2_ready, 1)

            NG = NT * 2 * H
            z3 = zg[:, :].rearrange("p (n e) -> p n e", e=E)
            w3 = wins[:, :].rearrange("p (n e) -> p n e", e=E)

            def l1_gates():
                dve.wait_ge(*TB.filled("gates"))
                dve.tensor_scalar(zg[:, :], TB.bank("gates")[:, 0:NG * E], Z_HI, Z_LO, ALU.min, ALU.max).then_inc(t_dve, 1)
                dve.tensor_copy(w3, rank0[:, :].unsqueeze(1).broadcast_to((P, NG, E))).then_inc(rank_s, 1)
                dve.wait_ge(*TB.was_read("gates"))
                n = 1
                for d in range(1, E):
                    b3 = beat[:, 0:NG * (E - d)].rearrange("p (n e) -> p n e", e=E - d)
                    if d > 1:
                        dve.wait_ge(rank_s, n)
                    dve.tensor_tensor(b3, z3[:, :, 0:E - d], z3[:, :, d:E], ALU.is_ge).then_inc(rank_s, 1)
                    dve.wait_ge(rank_s, n + 1)
                    dve.tensor_tensor(w3[:, :, 0:E - d], w3[:, :, 0:E - d], b3, ALU.add).then_inc(rank_s, 1)
                    dve.wait_ge(rank_s, n + 2)
                    dve.tensor_tensor(w3[:, :, d:E], w3[:, :, d:E], b3, ALU.subtract).then_inc(rank_s, 1)
                    n += 3
                dve.wait_ge(rank_s, n)
                dve.tensor_scalar(wins[:, :], wins[:, :], E - TOPK - 0.5, None, ALU.is_gt).then_inc(rank_s, 1)
                dve.wait_ge(ex_s, 1)
                dve.tensor_scalar(sg[:, :], sg[:, :], 1.0, None, ALU.add).then_inc(rank_s, 1)
                dve.wait_ge(rank_s, n + 2)
                dve.reciprocal(sg[:, :], sg[:, :]).then_inc(rank_s, 1)
                dve.wait_ge(rank_s, n + 3)
                g4 = sg[:, :].rearrange("p (t k n) -> p t k n", t=NT, k=2)
                m4 = wins[:, :].rearrange("p (t k n) -> p t k n", t=NT, k=2)
                dve.tensor_tensor(g4[:, :, 0, :], g4[:, :, 0, :], m4[:, :, 0, :], ALU.mult).then_inc(gates_ready, 1)
                dve.scalar_tensor_tensor(out=g4[:, :, 1, :], in0=g4[:, :, 1, :], scalar=SCALE, in1=m4[:, :, 1, :],
                                         op0=ALU.mult, op1=ALU.mult).then_inc(gates_ready, 1)
                gate, inp = xn2[0:SD, :, :].rearrange("p a b -> p (a b)"), pr[0:SD, 0, :]
                dve.wait_ge(*YB.was_read("gt"))
                dve.tensor_scalar(inp, gate, -0.5, 0.5, ALU.mult, ALU.add).then_inc(sc_s, 1)
                dve.wait_ge(sc_s, 1)
                dve.tensor_scalar(gate, gate, 0.5, 0.5, ALU.mult, ALU.add).then_inc(sc_s, 1)
                dve.wait_ge(*YB.filled("si"))
                dve.scalar_tensor_tensor(out=inp, in0=YB.bank("si")[0:SD, :], scalar=bsi_s[:, 0:1], in1=inp,
                                         op0=ALU.add, op1=ALU.mult).then_inc(y_dve, 1)
                dve.wait_ge(sc_s, 2)
                dve.wait_ge(*YB.was_read("si"))
                dve.tensor_tensor_scan(st9[0:SD, :], gate, inp, 0.0, ALU.mult, ALU.add).then_inc(st_ready, 1)
                dve.wait_ge(gates_ready, 2)

            g5 = sg[:, :].rearrange("p (t k h e) -> p t k h e", t=NT, k=2, h=H)

            def l1_chunk(n):
                c = n - 1
                if not 0 <= c < NCHUNK:
                    return
                t, kind, e = chunk_kind(c)
                dst = vv[:, t, :] if kind == 2 and e == 0 else yg_slot(c)
                if kind < 2:
                    old = [k for k in range(c) if chunk_kind(k)[1] < 2]
                    if len(old) >= 3:
                        o = old[-3]
                        ot, ok, oe = chunk_kind(o)
                        if oe == E - 1:
                            dve.wait_ge(*TB.filled(f"qk{2 * ot + ok}"))
                        else:
                            dve.wait_ge(tr_part, sum(1 for k in old[:-2] if chunk_kind(k)[2] < E - 1))
                elif e > 0:
                    same = [k for k in range(c) if chunk_kind(k)[1] == 2 and chunk_kind(k)[2] > 0
                            and v_before(k) % 2 == v_before(c) % 2]
                    if same:
                        dve.wait_ge(v_add, sum(1 for k in range(same[-1] + 1)
                                               if chunk_kind(k)[1] == 2 and chunk_kind(k)[2] > 0))
                dve.wait_ge(*YB.filled(f"y{c}"))
                dve.tensor_tensor(dst.rearrange("p (h d) -> p h d", h=H),
                                  YB.bank(f"y{c}")[:, :].rearrange("p (h d) -> p h d", h=H),
                                  g5[:, t, 1 if kind == 0 else 0, :, e].unsqueeze(2).broadcast_to((P, H, DH)),
                                  ALU.mult).then_inc(y_dve, 1)

            def l1_att(a):
                if a < NATT:
                    dve.wait_ge(*YB.filled(f"s{a}"))
                    dve.tensor_reduce(nmax[:, a:a + 1], YB.bank(f"s{a}")[:, :], X, ALU.max, negate=True)\
                       .then_inc(max_done, 1)
                n = a - 1
                if 0 <= n < NATT and TB.reader[TB.at[f"pt{n}"]] == "dve":
                    if n >= 2:
                        dve.wait_ge(pv_done, n - 1)
                    dve.wait_ge(*TB.filled(f"pt{n}"))
                    dve.tensor_copy(pt[:, n % 2, :, :].rearrange("p a b -> p (a b)"), TB.bank(f"pt{n}")[:, :])\
                       .then_inc(t_dve, 1)
                if a >= H + 1 and (a - H - 1) % H == 0:
                    t = (a - H - 1) // H
                    hs = slice(t * H, (t + 1) * H)
                    dve.wait_ge(*YB.was_read(f"s{H * t + H - 1}"))
                    dve.reciprocal(rden[:, hs], den[:, hs]).then_inc(rden_s, 1)
                    dve.wait_ge(rden_s, t + 1)
                    if t >= 2:
                        dve.wait_ge(zm_ready, 2 * (t - 1))
                    dve.wait_ge(pv_done, H * (t + 1))
                    dve.tensor_tensor(oo[:, t % 2, :].rearrange("p (h d) -> p h d", h=H),
                                      OB.bank(f"o{t}")[:, :].rearrange("p (h d) -> p h d", h=H),
                                      rden[:, hs].unsqueeze(2).broadcast_to((P, H, DH)), ALU.mult).then_inc(o_dve, 1)

            def l1_fin(t):
                dve.wait_ge(fin_fill, t + 1)
                if t == 0:
                    dve.wait_ge(x1_copied, 1)
                dve.tensor_tensor(x1[:, t, :], x1[:, t, :], TB.bank(f"z{t}")[:, 3 * P:4 * P], ALU.add).then_inc(z_read, 1)

            st = {("l0", "lerp"): l0_lerp, ("l0", "proj"): l0_proj, ("l0", "gather"): l0_gather,
                  ("l0", "wkv"): l0_wkv, ("l0", "scores"): l0_scores, ("l0", "soft"): l0_soft, ("l0", "norm"): l0_norm,
                  ("l0", "mix"): l0_mix, ("l0", "gn"): l0_gn, ("l0", "join"): l0_join,
                  ("l1", "head"): l1_head, ("l1", "gates"): l1_gates, ("l1", "chunk"): l1_chunk,
                  ("l1", "att"): l1_att, ("l1", "fin"): l1_fin}
            run(st, L0)
            step_over(dve, 2)
            with dve.Fori(0, B - 1) as i:
                run(st, BODY)
                step_over(dve, i + 3)
            run(st, L1)


def kernel(**inputs):
    import numpy as np
    import concourse.bacc as _bacc
    from concourse import mybir as _mybir
    from concourse.bass_utils import run_bass_kernel_spmd as _run

    a = {k: np.asarray(v) for k, v in inputs.items()}
    heads = lambda w: w.reshape(G, HP, P, D).transpose(2, 0, 1, 3)
    wkv = a["L0_ffn_w_kv"]
    null = a["L0_ffn_null_kv"].reshape(2, G, HP, P).transpose(0, 3, 1, 2)
    wq5 = a["L1_ffn_Wq"].reshape(D, H, E, DH).transpose(0, 2, 1, 3).reshape(D, 1, E, CW)
    wkv5 = a["L1_ffn_Wkv"].reshape(D, 2, H, E, DH).transpose(0, 1, 3, 2, 4).reshape(D, 2, E, CW)
    wo5 = a["L1_ffn_Wo"].reshape(DH, E, D).transpose(1, 0, 2).reshape(E * DH, D)
    wor = np.zeros((3 * P, D), wo5.dtype)
    wor[:E * DH] = wo5
    win, bin_ = a["L1_attn_W_in"], a["L1_attn_b_in"]
    laid = {
        "x": a["L0_attn_x"],
        "ddw": a["L0_attn_ddlerp_w"].T,
        "mixes": np.stack([a[f"L0_attn_mix_{n}"] for n in "vrkwg"], axis=1),
        "projw": np.stack([a[f"L0_attn_{n}_w"].T for n in ("v", "r", "k", "w", "g", "out")], axis=1),
        "gnw": a["L0_attn_gn_weight"], "gnb": a["L0_attn_gn_bias"],
        "qkr": np.concatenate([a["L0_ffn_w_qr"], a["L0_ffn_w_kvr"]]).T,
        "wqn": heads(a["L0_ffn_w_q"]), "wkn": heads(wkv[:, :H * DH]), "wvn": heads(wkv[:, H * DH:]),
        "won": heads(a["L0_ffn_w_out"].transpose(0, 2, 1)),
        "nkT": null[0], "nvT": null[1], "null_token": a["L0_ffn_null_token"].reshape(D),
        "winT": win[:, :D].T, "winT8": win[:, D:].T, "wcat": win[:, D:],
        "wg": a["L1_attn_W_g"][:D], "wg8": a["L1_attn_W_g"][D:],
        "bin_": bin_[:D, None], "bin8": bin_[D:, None], "bg": a["L1_attn_b_g"][:, None],
        "wout": a["L1_attn_W_out"][:D],
        "wout9": np.concatenate([a["L1_attn_W_out"][D:], a["L1_attn_b_out"][None]]),
        "wqkv": np.concatenate([wq5, wkv5], axis=1),
        "wsd": np.concatenate([a["L1_ffn_Ws"], a["L1_ffn_Wd"]], axis=1),
        "wor": wor.reshape(3, P, D),
    }
    nc = _bacc.Bacc("TRN2", target_bir_lowering=False, num_devices=1)
    arrays, args = {}, []
    for name, arr in laid.items():
        arr = np.ascontiguousarray(arr)
        arrays[f"in_{name}_dram"] = arr
        args.append(nc.dram_tensor(f"in_{name}_dram", arr.shape, _mybir.dt.from_np(arr.dtype), kind="ExternalInput").ap())
    args.append(nc.dram_tensor("out_0_dram", (B, T, D), F32, kind="ExternalOutput").ap())
    layers(nc, *args)
    r = _run(nc, [arrays], core_ids=[0])
    return r.results[0]["out_0_dram"]
```

```python
from contextlib import ExitStack

import concourse.bass as bass
from concourse import mybir

F32 = mybir.dt.float32
I32 = mybir.dt.int32
ALU = mybir.AluOpType
ACT = mybir.ActivationFunctionType
X = mybir.AxisListType.X

P = 128
B, T, D = 8, 512, 128
NT = T // P
LN_EPS = 1e-5

AH, ADH = 16, 8
GN_EPS = 0.00064
NPAIR = 4

G, NQ, NK = 4, 128, 64
H, DH = 8, 64
HP = H // 2
NKEY = NK + 1
PICKED = -3.0e38
ROUNDS_Q, ROUNDS_K = NQ // 8, NK // 8

SD = 8
E, TOPK = 5, 3
KINDS = 3
CW = H * DH
SCALE = DH ** -0.5
NCHUNK = NT * KINDS * E
NATT = NT * H

Z_LO, Z_HI = -88.7, 16.6355


G_LAG, Q_LAG, S_LAG, K_LAG = 1, 3, 2, 5
PT_LAG, PV_LAG = 2, 3
HALF = H // 2
D_LAG = PV_LAG + H
M_LAG = D_LAG + 1
A_LAG, Z_LAG, F_LAG = D_LAG + 4, D_LAG + 5, D_LAG + 7

N_LOADS = 18


class Banks:

    def __init__(self, banks, filled, freed, units):
        self.banks, self.filled_sem, self.freed = banks, filled, freed
        self.at = {name: n for n, (name, _) in enumerate(units)}
        self.reader = [reader for _, reader in units]

    def bank(self, name):
        return self.banks[self.at[name] % len(self.banks)]

    def filled(self, name):
        return self.filled_sem, self.at[name] + 1

    def _read(self, n):
        who = self.reader[n]
        return self.freed[who], sum(1 for r in self.reader[:n + 1] if r == who)

    def free_for(self, name):
        n = self.at[name] - len(self.banks)
        return self._read(n) if n >= 0 else None

    def free_sem(self, name):
        return self.freed[self.reader[self.at[name]]]

    def was_read(self, name):
        return self._read(self.at[name])


def chunk_kind(c):
    return c // (KINDS * E), c // E % KINDS, c % E


def l0_slots():
    a = [[("dd",)], [("tanh",)], [("lerp",)], [("vr",)], [("vre",)], [("kw",)], [("kwe",)], [("g",)],
         [("ge",), ("selq",)], [("gq",)], [("gqe",)], [("gk",)], [("gke",), ("kv", 0)], [("small",), ("scan", 0)],
         [("smalle",), ("ax", 0), ("prod", 0)]]
    more = [[("kv", 1)], [("wsum", 0)], [("scan", 1)], [("prod", 1)], [("kv", 2)], [("wsum", 1)],
            [("scan", 2)], [("prod", 2)]]
    for g in range(G):
        a.append([("axe", g)] + more[2 * g] + ([("se", g - 1)] if g else []))
        a.append([("s", g)] + ([("ax", g + 1)] if g + 1 < G else []) + more[2 * g + 1])
    a += [[("se", G - 1), ("kv", 3)], [("soft",), ("wsum", 2), ("scan", 3)], [("shift",), ("prod", 3)],
          [("exp",)],
          [("sums",), ("wsum", 3)], [("norm",), ("gn1",)], [("ptn",), ("gnsq",)], [("ptne",), ("pt", 0), ("gn2",)],
          [("pte", 0), ("vw", 0)]]
    more = {0: [("gn3",)], 1: [("base",)], 4: [("yT",)], 5: [("yTe",)], 6: [("att",)]}
    for g in range(G):
        a.append([("vwe", g)] + more.get(4 * g, []))
        a.append([("o", g)] + ([("pt", g + 1)] if g + 1 < G else []) + more.get(4 * g + 1, []))
        a.append([("oe", g)] + ([("pte", g + 1)] if g + 1 < G else []) + more.get(4 * g + 2, []))
        if g + 1 < G:
            a.append([("vw", g + 1)] + more.get(4 * g + 3, []))
    return a + [[("scat",)], [("join",)], [("x1",)], [("ln",)]]


def l1_stages():
    out = [("xT",), ("xTe",), ("gates",)] + [("rank", d) for d in range(1, E)] + [("sig",)]
    out += [("chunk", c) for c in range(NCHUNK + K_LAG)]
    for a in range(NATT - H + F_LAG + 1):
        out += [("ze", t) for t in range(NT) if a == H * t + Z_LAG + 1]
        out.append(("att", a))
        for t in range(NT):
            if a == H * t + Z_LAG:
                out.append(("z", t))
            if a == H * t + F_LAG:
                out.append(("fin", t))
    return out


def spread(l1, l0):
    cost = {"att": 1.8, "gates": 2.0, "rank": 1.0, "sig": 2.0}
    out, k, done = [], 0, 0.0
    weight = [cost.get(s[0], 1.0) for s in l1]
    total = sum(weight)
    for s, w in zip(l1, weight):
        while k < len(l0) and k < done / total * len(l0) + 0.5:
            out += [("l0",) + u for u in l0[k]]
            k += 1
        out.append(("l1",) + s)
        done += w
    for u in l0[k:]:
        out += [("l0",) + v for v in u]
    return out


def layers(nc, x, ddw, mixes, projw, gnw, gnb, qkr, wqn, wkn, wvn, won, nkT, nvT, null_token,
           winT, winT8, wcat, wg, wg8, bin_, bin8, bg, wout, wout9, wqkv, wsd, wor, out):
    ctx = ExitStack()
    with ctx:
        def sb(name, shape, dt=F32):
            return ctx.enter_context(nc.sbuf_tensor(name, shape, dt))

        def sem(name):
            return ctx.enter_context(nc.semaphore(name))

        xn_d = nc.dram_tensor("xn_scratch", (B, P, NT * D), F32, kind="Internal").ap()
        xT_d = nc.dram_tensor("xT_scratch", (B + 1, P, T), F32, kind="Internal").ap()
        posT_d = nc.dram_tensor("posT_scratch", (B, P, NT * 2 * G), F32, kind="Internal").ap()
        pos_d = nc.dram_tensor("pos_scratch", (B, G * T), F32, kind="Internal").ap()
        v_d = nc.dram_tensor("v_scratch", (D, T), F32, kind="Internal").ap()
        r_d = nc.dram_tensor("r_scratch", (D, T), F32, kind="Internal").ap()

        ident = sb("ident", [P, P])
        iota1 = sb("iota1", [P, P])
        iotac = sb("iotac", [P, 1])
        ddw_s = sb("ddw_s", [P, D])
        mix_s = sb("mix_s", [P, 5])
        projw_s = sb("projw_s", [P, 5, D])
        oww_s = sb("oww_s", [P, D])
        gnw_s = sb("gnw_s", [P, D])
        gnb_s = sb("gnb_s", [P, D])
        null_s = sb("null_s", [P, D])
        qkr_s = sb("qkr_s", [P, 2 * G])
        A_s = sb("A_s", [P, G, 2, HP, P])
        M_s = sb("M_s", [P, G, 2, HP, P])
        u9_s = sb("u9_s", [P, G, H + 1])
        nvw_s = sb("nvw_s", [G * H, G, D])
        wqkv_s = sb("wqkv_s", [P, KINDS, E, CW])
        wsd_s = sb("wsd_s", [P, 2 * H * E])
        wsi_s = sb("wsi_s", [P, SD])
        wgt_s = sb("wgt_s", [P, SD])
        wfold_s = sb("wfold_s", [P, D])
        ws9_s = sb("ws9_s", [SD + 1, D])
        wor_s = sb("wor_s", [P, 3, D])
        bsi_s = sb("bsi_s", [SD, 1])
        bgt_s = sb("bgt_s", [SD, 1])
        rank0 = sb("rank0", [P, E])

        xr = sb("xr", [P, NT, D])
        xn = sb("xn", [P, NT, D])
        xTp = sb("xTp", [P, T + 1])
        dif = sb("dif", [P, T])
        th = sb("th", [P, T])
        aa = sb("aa", [P, T])
        lp = sb("lp", [P, 2, T])
        kf = sb("kf", [P, T])
        dec = sb("dec", [P, T])
        silu = dif
        vb = sb("vb", [P, 2, 2, T])
        rb = sb("rb", [P, 2, 2, T])
        vf = vb[:, 1, 0, :]
        rf = rb[:, 1, 0, :]
        sel = sb("sel", [P, G * H * NKEY])
        skeys = sel[:, 0:G * H * NK].rearrange("p (n k) -> p n k", k=NK)
        snull = sel[:, G * H * NK:G * H * NKEY]
        selT = sb("selT", [P, G, T])
        posT = sb("posT", [P, NT, 2, G])
        xq = sb("xq", [P, G * NQ])
        xk = sb("xk", [P, G * NK])
        ax = sb("ax", [P, 2, H * NK])
        pt0 = sb("pt0", [P, 2, HP, NQ])
        vw = sb("vw", [P, 2, HP, D])
        ptn = sb("ptn", [G * H, NQ])
        ob = aa[:, :].rearrange("p (g d) -> p g d", g=G)
        sm = sb("sm", [P, G * (H + 1) + G])
        smt = sb("smt", [P, G * (H + 1) + G])
        hmax = sb("hmax", [P, G * H])
        hsum = sb("hsum", [P, G * H])
        mu = sb("mu", [P, NT * AH])
        va = sb("va", [P, NT * AH])
        ya = sb("ya", [P, NT * AH])
        wa = sb("wa", [P, NT * AH])
        cnt4 = sb("cnt4", [P, NT, G])
        cnt = sb("cnt", [P, NT])
        rcnt = sb("rcnt", [P, NT])
        nz = sb("nz", [P, NT])

        x1 = sb("x1", [P, NT, D])
        xn2 = sb("xn2", [P, NT, D])
        x2T = sb("x2T", [P, T])
        zg = sb("zg", [P, NT * 2 * H * E])
        sg = sb("sg", [P, NT * 2 * H * E])
        wins = sb("wins", [P, NT * 2 * H * E])
        yg = sb("yg", [P, E * CW])
        qk = sb("qk", [P, 2, HP, T])
        vv = sb("vv", [P, NT, CW])
        pr = sb("pr", [P, 3, T])
        beat = pr[:, 1, 0:NT * 2 * H * (E - 1)]
        pt = sb("pt", [P, 2, NT, P])
        oo = sb("oo", [P, 2, CW])
        zT = sb("zT", [P, 3, P])
        nmax = sb("nmax", [P, NATT])
        den = sb("den", [P, NATT])
        rden = sb("rden", [P, NATT])
        st9 = sb("st9", [SD + 1, T])
        stats = sb("stats", [P, 4 * B, 6])
        mv = sb("mv", [P, 4 * B, 2])
        lv = sb("lv", [P, 4 * B])
        ly = sb("ly", [P, 4 * B])
        lw = sb("lw", [P, 4 * B])

        MAGIC = 0x5F3759DF

        bank = [ctx.enter_context(nc.psum_tensor(f"bank{k}", [P, 512], F32)) for k in range(8)]

        it_end = sem("it_end")
        it_go = sem("it_go")

        out_sent = sem("out_sent")

        step_sems = []

        def ssem(name):
            s = sem(name)
            step_sems.append(s)
            return s

        p_ld = ssem("p_ld"); p_ldx = ssem("p_ldx"); p_ldw = ssem("p_ldw"); p_cst = ssem("p_cst")
        p_bn = ssem("p_bn"); p_nt = ssem("p_nt"); p_xn = ssem("p_xn"); p_wr = ssem("p_wr")
        p_fill = ssem("p_fill"); p_act = ssem("p_act"); p_dve = ssem("p_dve")
        p_top = ssem("p_top"); p_pos = ssem("p_pos"); p_posT = ssem("p_posT"); p_zero = ssem("p_zero")
        p_blk = ssem("p_blk"); p_log = ssem("p_log"); p_st = [ssem(f"p_st{s}") for s in range(2)]; p_misc = ssem("p_misc")
        p_ld2 = ssem("p_ld2")
        ld_x = ssem("ld_x"); ld_xn = ssem("ld_xn"); x1_free = ssem("x1_free"); next_xT = ssem("next_xT")
        ld_posT = ssem("ld_posT"); ld_pos = ssem("ld_pos")
        dif_ready = ssem("dif_ready"); th_done = ssem("th_done"); e_done = ssem("e_done")
        af_ready = ssem("af_ready"); lerp_ready = ssem("lerp_ready")
        r_fill = ssem("r_fill"); r_act = ssem("r_act"); r_dve = ssem("r_dve")
        yT_fill = ssem("yT_fill"); yT_read = ssem("yT_read"); att_fill = ssem("att_fill")
        vr_sent = ssem("vr_sent"); tg_done = ssem("tg_done"); dec_ready = ssem("dec_ready")
        vb_in = [ssem(f"vb_in{s}") for s in range(2)]
        rb_in = [ssem(f"rb_in{s}") for s in range(2)]
        kv_done = ssem("kv_done"); scan_done = ssem("scan_done"); prod_done = ssem("prod_done")
        ot_done = ssem("ot_done")
        sel_ready = ssem("sel_ready"); selT_ready = ssem("selT_ready")
        smt_done = ssem("smt_done"); sig_ready = ssem("sig_ready")
        soft = ssem("soft"); e0_done = ssem("e0_done"); p0_ready = ssem("p0_ready")
        gn = ssem("gn"); sq_done = ssem("sq_done"); gnp = ssem("gnp"); y_ready = ssem("y_ready")
        cnt_s = ssem("cnt_s"); base_s = ssem("base_s"); join_s = ssem("join_s"); x1_new = ssem("x1_new")
        x1_copied = ssem("x1_copied"); ln_s = ssem("ln_s")
        t_fill = ssem("t_fill"); t_act = ssem("t_act"); t_dve = ssem("t_dve")
        y_fill = ssem("y_fill"); y_act = ssem("y_act"); y_dve = ssem("y_dve")
        s_fill = ssem("s_fill"); s_act = ssem("s_act")
        o_dve = ssem("o_dve")
        ex_s = ssem("ex_s"); rank_s = ssem("rank_s"); gates_ready = ssem("gates_ready")
        sc_s = ssem("sc_s"); st_ready = ssem("st_ready")
        sum_add = ssem("sum_add"); max_done = ssem("max_done"); rden_s = ssem("rden_s")
        tr_part = ssem("tr_part"); half_add = ssem("half_add"); pv_done = ssem("pv_done")
        zm_ready = ssem("zm_ready"); zt_done = ssem("zt_done")
        lo_sem, hi_sem = step_sems[0].num, step_sems[-1].num
        assert [s.num for s in step_sems] == list(range(lo_sem, hi_sem + 1)), [s.num for s in step_sems]

        p_units = [(f"xT{b}", "act") for b in range(B)]
        p_units += [(f"fold{k}", "act") for k in range(4 * G)]
        p_units += [("u", "act"), ("nvw", "act"), ("wf", "act"), ("ws9", "act"), ("wmisc", "dve")]
        PB = Banks(bank[0:7], p_fill, {"act": p_act, "dve": p_dve}, p_units)
        LG = bank[7]

        r_units = [("dd", "act"), ("v", "act"), ("r", "act"), ("k", "act"), ("w", "act"), ("g", "dve"),
                   ("gq", "act"), ("gk", "act"), ("small", "dve")]
        for g in range(G):
            r_units += [(f"ax{g}", "act"), (f"s{g}", "dve")]
        r_units += [("ptn", "act")]
        for g in range(G):
            r_units += [(f"pt{g}", "act"), (f"vw{g}", "dve"), (f"o{g}", "act")]
        r_units += [("scat", "dve")]
        RB = Banks(bank[5:7], r_fill, {"act": r_act, "dve": r_dve}, r_units)
        NBK = bank[7]

        t_units = [("xT", "act"), ("gates", "dve")]
        t_units += [(f"qk{u}", "act") for u in range(2 * NT)]
        for s in l1_stages():
            if s[0] == "att" and 0 <= s[1] - PT_LAG < NATT:
                t_units.append((f"pt{s[1] - PT_LAG}", "act"))
            if s[0] == "z":
                t_units.append((f"z{s[1]}", "act"))
            if s[0] == "fin":
                t_units.append((f"f{s[1]}", "dve"))
        TB = Banks(bank[2:4], t_fill, {"act": t_act, "dve": t_dve}, t_units)
        YB = Banks([bank[0], bank[1], bank[4]], y_fill, {"act": y_act, "dve": y_dve},
                   [("si", "dve"), ("gt", "act")] + [(f"y{c}", "dve") for c in range(NCHUNK)])
        SB = Banks(bank[0:2], s_fill, {"act": s_act}, [(f"s{a}", "act") for a in range(NATT)])
        OBK = bank[4]

        def q_before(c):
            return sum(1 for k in range(c) if chunk_kind(k)[1] == 0)

        def adds_before(c):
            return sum(1 for k in range(c) if chunk_kind(k)[1] > 0 and chunk_kind(k)[2] > 0)

        def gated(c):
            t, kind, e = chunk_kind(c)
            if kind == 0:
                s = q_before(c) % 3
                return yg[:, s * CW:(s + 1) * CW]
            if e == 0:
                return k_or_v_sum(t, kind)
            s = adds_before(c) % 3
            return pr[:, 2, :] if s == 2 else yg[:, (3 + s) * CW:(4 + s) * CW]

        def k_or_v_sum(t, kind):
            return oo[:, t % 2, :] if kind == 1 else vv[:, t, :]

        stage = {}
        stage["wq"] = qk[:, :, :, :].rearrange("p a b c -> p (a b c)")[:, 0:2048].rearrange("p (g c f) -> p g c f", g=G, c=HP)
        stage["wk"] = qk[:, :, :, :].rearrange("p a b c -> p (a b c)")[:, 2048:4096].rearrange("p (g c f) -> p g c f", g=G, c=HP)
        stage["wv"] = vv[:, :, :].rearrange("p a b -> p (a b)").rearrange("p (g c f) -> p g c f", g=G, c=HP)
        stage["wo"] = yg[:, 0:2048].rearrange("p (g c f) -> p g c f", g=G, c=HP)
        nkt = rden[:, 0:16].rearrange("p (g c) -> p g c", g=G)
        nvt = rden[:, 16:32].rearrange("p (g c) -> p g c", g=G)
        nkb = den[:, 0:32].rearrange("p (g c a) -> p g c a", g=G, c=HP)
        nvb = pr[:, 0, :].rearrange("p (g n) -> p g n", g=G)
        xa = vb[:, :, :, :].rearrange("p a b c -> p (a b c)")
        xb = rb[:, :, :, :].rearrange("p a b c -> p (a b c)")
        xt_ev = ax
        wr_pad = lp[:, :, :].rearrange("p a b -> p (a b)")[:, 0:B * 64].rearrange("p (b n) -> p b n", b=B)
        lgw = aa[0:64, :]
        msk = dif[0:64, :]
        onesr = th[0:64, :]
        cum = kf[0:64, :]
        top8 = hmax[0:64, 0:8]
        posTb = x1[:, :, :].rearrange("p a b -> p (a b)")[:, 0:B * NT * 2 * G].rearrange("p (b t k g) -> p b t k g", b=B, t=NT, k=2)
        winT_s = x2T[:, 0:P]
        winT8_s = x2T[0:SD, P:2 * P]
        wg_s = x2T[:, 256:256 + SD]
        wg8_s = x2T[0:SD, 264:264 + SD]
        bin_s = x2T[:, 272:273]
        bin8_s = x2T[0:SD, 273:274]
        bg_s = x2T[0:SD, 274:275]
        bcol9 = x2T[:, 275:275 + SD + 1]
        wout_s = xn2[:, 0, :]
        wout9_s = xn2[0:SD + 1, 1, :]

        block = ctx.enter_context(nc.Block())

        def newton(eng, y, v, w, n, sem_, base):
            eng.tensor_scalar(w[:, 0:n].bitcast(I32), v[:, 0:n].bitcast(I32), 1, None,
                              ALU.logical_shift_right).then_inc(sem_, 1)
            eng.wait_ge(sem_, base + 1)
            eng.tensor_scalar(y[:, 0:n].bitcast(I32), w[:, 0:n].bitcast(I32), -1.0, float(MAGIC),
                              ALU.mult, ALU.add).then_inc(sem_, 1)
            eng.wait_ge(sem_, base + 2)
            for k in range(4):
                eng.scalar_tensor_tensor(out=w[:, 0:n], in0=y[:, 0:n], scalar=-0.5, in1=y[:, 0:n],
                                         op0=ALU.mult, op1=ALU.mult).then_inc(sem_, 1)
                eng.wait_ge(sem_, base + 3 * k + 3)
                eng.tensor_tensor(w[:, 0:n], w[:, 0:n], v[:, 0:n], ALU.mult).then_inc(sem_, 1)
                eng.wait_ge(sem_, base + 3 * k + 4)
                eng.scalar_tensor_tensor(out=y[:, 0:n], in0=w[:, 0:n], scalar=1.5, in1=y[:, 0:n],
                                         op0=ALU.add, op1=ALU.mult).then_inc(sem_, 1)
                eng.wait_ge(sem_, base + 3 * k + 5)
            return base + 14

        NEWTON = 14

        def step_over(eng, n):
            eng.drain().then_inc(it_end, 1)
            eng.wait_ge(it_go, n)

        def run(stages, names):
            for s in names:
                f = stages.get(s[0:2])
                if f is not None:
                    f(*s[2:])

        L0 = [("l0",) + s for slot in l0_slots() for s in slot]
        L1 = [("l1",) + s for s in l1_stages()]
        BODY = spread(l1_stages(), l0_slots())

        @block.sync
        def _(sp):
            sp.dma_start(qkr_s[:, :], qkr).then_inc(p_ldw, 16)
            for b in range(B):
                src, k = (xa, b) if b < 4 else (xb, b - 4)
                sp.dma_start(src[:, k * T:(k + 1) * T].rearrange("p (t d) -> p t d", t=NT),
                             x[b].rearrange("(t p) d -> p t d", p=P)).then_inc(p_ldx, 16)
            loads = [(stage["wq"], wqn), (stage["wk"], wkn), (stage["wv"], wvn), (stage["wo"], won),
                     (nkt, nkT), (nvt, nvT), (winT_s, winT), (winT8_s, winT8), (wg_s, wg), (wg8_s, wg8),
                     (bin_s, bin_), (bin8_s, bin8), (bg_s, bg), (wout_s, wout), (wout9_s, wout9),
                     (bsi_s[:, :], bin8), (gnw_s[:, :], gnw.partition_broadcast(P)), (gnb_s[:, :], gnb.partition_broadcast(P))]
            loads2 = [(wsi_s[:, :], wcat), (ddw_s[:, :], ddw), (mix_s[:, :], mixes), (projw_s[:, :, :], projw[:, 0:5, :]),
                     (oww_s[:, :], projw[:, 5, :]), (null_s[:, :], null_token.partition_broadcast(P)),
                     (wqkv_s[:, :, :, :], wqkv), (wsd_s[:, :], wsd), (wor_s[:, 0:2, :], wor[0:2].rearrange("c p m -> p c m")),
                     (wor_s[0:DH, 2, :], wor[2, 0:DH])]
            for dst, src in loads:
                sp.dma_start(dst, src, allow_slow_non_contiguous=True).then_inc(p_ld, 16)
            for dst, src in loads2:
                sp.dma_start(dst, src, allow_slow_non_contiguous=True).then_inc(p_ld2, 16)
            assert len(loads) == N_LOADS
            for b in range(B):
                src, k = (xa, b) if b < 4 else (xb, b - 4)
                sp.wait_ge(p_xn, NT * (b + 1))
                sp.dma_start(xn_d[b], src[:, k * T:(k + 1) * T]).then_inc(p_wr, 16)
                sp.wait_ge(p_act, PB.was_read(f"xT{b}")[1])
                sp.dma_start(xT_d[b], xt_ev[:, b % 2, :]).then_inc(p_st[b % 2], 16)
                if b == 0:
                    sp.dma_start(xT_d[B], xt_ev[:, 0, :]).then_inc(p_st[0], 16)
            sp.wait_ge(p_pos, 1)
            sp.dma_start(pos_d.rearrange("b (g t) -> (b g) t", g=G), cum[0:B * G, :]).then_inc(p_wr, 16)
            sp.wait_ge(p_pos, 2)
            sp.dma_start(posT_d.rearrange("b p n -> p b n"),
                         posTb.rearrange("p b t k g -> p b (t k g)")).then_inc(p_wr, 16)
            sp.wait_ge(p_wr, 16 * (B + 2))
            sp.wait_ge(p_st[0], 16 * (B // 2 + 1))
            sp.wait_ge(p_st[1], 16 * B // 2)
            sp.dma_start(xTp[:, 1:T + 1], xT_d[0]).then_inc(next_xT, 16)
            sp.wait_ge(next_xT, 16)
            sp.wait_ge(p_ld2, 16 * len(loads2))

            def next_step():
                sp.wait_ge(it_end, 4)
                sp.sem_clear(range(lo_sem, hi_sem + 1))
                sp.sem_clear(it_end)
                sp.sem_inc(it_go, 1)

            next_step()

            def stages_of(l0_b, l1_b):
                def l0_load():
                    one = bass.ds(l0_b, 1)
                    sp.dma_start(xn[:, :, :].rearrange("p t d -> p (t d)"),
                                 xn_d[one].rearrange("a p t -> (a p) t")).then_inc(ld_xn, 16)
                    sp.dma_start(posT[:, :, :, :].rearrange("p t k g -> p (t k g)"),
                                 posT_d[one].rearrange("a p n -> (a p) n")).then_inc(ld_posT, 16)
                    sp.dma_start(selT[:, :, :].rearrange("p g t -> p (g t)"),
                                 pos_d[one].broadcast_to((P, G * T))).then_inc(ld_pos, 16)
                    if l1_b is not None:
                        x1_frees()
                        sp.wait_ge(x1_copied, 1)
                    sp.dma_start(xr[:, :, :], x[one].rearrange("a (t p) d -> p (a t) d", p=P)).then_inc(ld_x, 16)

                def l0_kwe():
                    sp.wait_ge(af_ready, 2)
                    sp.wait_ge(dif_ready, 1)
                    sp.wait_ge(*RB.filled("dd"))
                    sp.dma_start(xTp[:, 1:T + 1], xT_d[bass.ds(l0_b + 1, 1)].rearrange("a p t -> (a p) t")).then_inc(next_xT, 16)

                def pair(dst, src, q, s):
                    two = src.rearrange("(h q j) t -> q h (j t)", q=NPAIR, j=2)[q]
                    sp.dma_start(dst[:, q % 2, :, :].rearrange("p j t -> p (j t)"),
                                 two.unsqueeze(1).broadcast_to((AH, ADH, 2 * T))).then_inc(s[q % 2], 16)

                def l0_vre():
                    sp.wait_ge(*RB.was_read("v"))
                    sp.dma_start(v_d, vf).then_inc(vr_sent, 16)
                    sp.wait_ge(*RB.was_read("r"))
                    sp.dma_start(r_d, rf).then_inc(vr_sent, 16)
                    sp.wait_ge(vr_sent, 32)
                    for q in range(2):
                        pair(vb, v_d, q, vb_in)
                        pair(rb, r_d, q, rb_in)

                def l0_wsum(q):
                    if q + 2 < NPAIR:
                        sp.wait_ge(ot_done, q + 1)
                        pair(vb, v_d, q + 2, vb_in)
                        pair(rb, r_d, q + 2, rb_in)

                def l1_store():
                    sp.wait_ge(*TB.was_read(f"f{NT - 1}"))
                    sp.dma_start(out[bass.ds(l1_b, 1)].rearrange("a (t p) d -> p (a t) d", p=P),
                                 x1[:, :, :]).then_inc(out_sent, 16)
                return l0_load, {("l0", "vre"): l0_vre, ("l0", "kwe"): l0_kwe, ("l0", "wsum"): l0_wsum}, l1_store

            def x1_frees():
                sp.wait_ge(out_sent, 16)
                sp.sem_clear(out_sent)
                sp.sem_inc(x1_free, 1)

            load, st, _ = stages_of(0, None)
            load()
            run(st, L0)
            sp.wait_ge(next_xT, 16)
            next_step()
            sp.sem_inc(out_sent, 16)
            with sp.Fori(0, B - 1) as i:
                load, st, store = stages_of(i + 1, i)
                load()
                run(st, BODY)
                store()
                sp.wait_ge(next_xT, 16)
                next_step()
            _, st, store = stages_of(None, B - 1)
            x1_frees()
            store()
            sp.wait_ge(out_sent, 16)

        @block.gpsimd
        def _(gp):
            gp.memset(ident[:, :], 0.0).then_inc(p_cst, 1)
            gp.wait_ge(p_cst, 1)
            gp.affine_select(out=ident[:, :], in_=ident[:, :], compare_op=ALU.not_equal, fill=1.0, base=0,
                             pattern=[[-1, P]], channel_multiplier=1).then_inc(p_cst, 1)
            gp.iota(iota1[:, :], [[1, P]], base=1, channel_multiplier=0,
                    allow_small_or_imprecise_dtypes=True).then_inc(p_cst, 1)
            gp.iota(iotac[:, :], [[1, 1]], base=1, channel_multiplier=1,
                    allow_small_or_imprecise_dtypes=True).then_inc(p_cst, 1)
            gp.iota(rank0[:, :], [[1, E]], base=0, channel_multiplier=0,
                    allow_small_or_imprecise_dtypes=True).then_inc(p_cst, 1)
            gp.memset(xTp[:, 0:1], 0.0).then_inc(p_cst, 1)
            gp.memset(dec[:, 0:1], 0.0).then_inc(p_cst, 1)
            gp.memset(st9[:, :], 1.0).then_inc(p_cst, 1)
            gp.memset(onesr, 1.0).then_inc(p_cst, 1)
            step_over(gp, 1)

            def l0_dd():
                gp.tensor_tensor(dif[:, :], xTp[:, 1:T + 1], xTp[:, 0:T], ALU.subtract).then_inc(dif_ready, 1)

            def l0_kv(q):
                if q == 0:
                    gp.wait_ge(*RB.was_read("k"))
                gp.wait_ge(vb_in[q % 2], 16 * (q // 2 + 1))
                gp.tensor_tensor(vb[:, q % 2, :, :], vb[:, q % 2, :, :],
                                 kf[:, :].unsqueeze(1).broadcast_to((P, 2, T)), ALU.mult).then_inc(kv_done, 1)

            def l0_prod(q):
                gp.wait_ge(rb_in[q % 2], 16 * (q // 2 + 1))
                gp.wait_ge(scan_done, 2 * q + 2)
                gp.tensor_tensor(vb[:, q % 2, :, :], vb[:, q % 2, :, :], rb[:, q % 2, :, :], ALU.mult).then_inc(prod_done, 1)

            def l0_norm():
                gp.wait_ge(soft, 9)
                gp.tensor_tensor(skeys, skeys, hsum[:, :].unsqueeze(2).broadcast_to((P, G * H, NK)), ALU.mult)\
                  .then_inc(p0_ready, 1)
                gp.tensor_tensor(snull, snull, hsum[:, :], ALU.mult).then_inc(p0_ready, 1)

            def l0_gnsq():
                gp.wait_ge(gn, 2)
                gp.tensor_tensor(lp[:, 0, :], th[:, :], th[:, :], ALU.mult).then_inc(sq_done, 1)

            def l0_gn3():
                gp.wait_ge(gn, 5 + NEWTON)
                c = th[:, :].rearrange("p (t d) -> p t d", t=NT)
                gp.tensor_tensor(c, c, gnw_s[:, :].unsqueeze(1).broadcast_to((P, NT, D)), ALU.mult).then_inc(gnp, 1)
                gp.wait_ge(gnp, 1)
                gp.tensor_tensor(c, c, gnb_s[:, :].unsqueeze(1).broadcast_to((P, NT, D)), ALU.add).then_inc(gnp, 1)
                gp.wait_ge(gnp, 2)
                gp.wait_ge(*RB.was_read("g"))
                gp.tensor_tensor(th[:, :], th[:, :], silu[:, :], ALU.mult).then_inc(y_ready, 1)

            def l0_base():
                gp.wait_ge(cnt_s, 3)
                gp.wait_ge(ld_x, 16)
                gp.wait_ge(y_ready, 1)
                l3 = lp[:, 0, :].rearrange("p (t d) -> p t d", t=NT)
                gp.tensor_tensor(l3, null_s[:, :].unsqueeze(1).broadcast_to((P, NT, D)),
                                 nz[:, :].unsqueeze(2).broadcast_to((P, NT, D)), ALU.mult).then_inc(base_s, 1)
                gp.wait_ge(base_s, 1)
                gp.tensor_tensor(xr[:, :, :], xr[:, :, :], l3, ALU.add).then_inc(base_s, 1)

            def l0_x1():
                gp.wait_ge(base_s, 2)
                gp.wait_ge(join_s, 1)
                gp.tensor_tensor(xr[:, :, :].rearrange("p t d -> p (t d)"),
                                 xr[:, :, :].rearrange("p t d -> p (t d)"), xq[:, :], ALU.add).then_inc(x1_new, 1)

            def l1_xT():
                gp.wait_ge(x1_free, 1)
                gp.tensor_copy(x1[:, :, :], xr[:, :, :]).then_inc(x1_copied, 1)

            def l1_chunk(n):
                c = n - S_LAG
                if not 0 <= c < NCHUNK:
                    return
                t, kind, e = chunk_kind(c)
                if kind > 0 and e > 0:
                    gp.wait_ge(y_dve, YB.was_read(f"y{c}")[1])
                    if e > 1:
                        gp.wait_ge(sum_add, adds_before(c))
                    dst = k_or_v_sum(t, kind)
                    gp.tensor_tensor(dst, dst, gated(c), ALU.add).then_inc(sum_add, 1)

            def l1_att(a):
                t, r = divmod(a - M_LAG, H)
                if r == 0 and 0 <= t < NT:
                    gp.wait_ge(o_dve, t + 1)
                    if t > 0:
                        gp.wait_ge(*TB.filled(f"z{t - 1}"))
                    for half in range(2):
                        hs = slice(half * HALF, (half + 1) * HALF)
                        m4 = wins[:, :].rearrange("p (t k h e) -> p t k h e", t=NT, k=2, h=H)[:, t, 1, hs, :]
                        gp.tensor_tensor(
                            yg[:, :].rearrange("p (h e d) -> p h e d", h=H, e=E)[:, hs],
                            oo[:, t % 2, :].rearrange("p (h d) -> p h d", h=H)[:, hs].unsqueeze(2).broadcast_to((P, HALF, E, DH)),
                            m4.unsqueeze(3).broadcast_to((P, HALF, E, DH)), ALU.mult).then_inc(zm_ready, 1)

            st = {("l0", "dd"): l0_dd, ("l0", "kv"): l0_kv, ("l0", "prod"): l0_prod, ("l0", "norm"): l0_norm,
                  ("l0", "gnsq"): l0_gnsq, ("l0", "gn3"): l0_gn3, ("l0", "base"): l0_base, ("l0", "x1"): l0_x1,
                  ("l1", "xT"): l1_xT, ("l1", "chunk"): l1_chunk, ("l1", "att"): l1_att}
            run(st, L0)
            step_over(gp, 2)
            with gp.Fori(0, B - 1) as i:
                run(st, BODY)
                step_over(gp, i + 3)
            run(st, L1)

        @block.scalar
        def _(act):
            act.preload_act_table_set("exp_and_others")
            for b in range(B):
                act.wait_ge(*PB.filled(f"xT{b}"))
                if b >= 2:
                    act.wait_ge(p_st[b % 2], 16 * (b // 2 + (b % 2 == 0)))
                    act.wait_ge(p_log, b - 1)
                act.activation(xt_ev[:, b % 2, :], PB.bank(f"xT{b}")[:, :], ACT.Copy).then_inc(p_act, 1)
            for k in range(4 * G):
                act.wait_ge(*PB.filled(f"fold{k}"))
                g, which = k // 4, k % 4
                dst, scale = (A_s, SCALE) if which < 2 else (M_s, 1.0)
                act.activation(dst[:, g, which % 2, :, :].rearrange("p a b -> p (a b)"), PB.bank(f"fold{k}")[:, :],
                               ACT.Copy, scale=scale).then_inc(p_act, 1)
            act.wait_ge(*PB.filled("u"))
            act.activation(u9_s[:, :, 0:H], PB.bank("u")[:, 0:G * H].rearrange("p (g h) -> p g h", g=G),
                           ACT.Copy, scale=SCALE).then_inc(p_act, 1)
            act.wait_ge(*PB.filled("nvw"))
            act.activation(nvw_s[:, :, :].rearrange("p g d -> p (g d)"), PB.bank("nvw")[0:G * H, :], ACT.Copy).then_inc(p_act, 1)
            act.wait_ge(*PB.filled("wf"))
            act.activation(wfold_s[:, :], PB.bank("wf")[:, 0:D], ACT.Copy).then_inc(p_act, 1)
            act.wait_ge(*PB.filled("ws9"))
            act.activation(ws9_s[:, :], PB.bank("ws9")[0:SD + 1, 0:D], ACT.Copy).then_inc(p_act, 1)
            step_over(act, 1)

            def copy(unit, banks, dst, src, scale=1.0):
                act.wait_ge(*banks.filled(unit))
                act.activation(dst, src, ACT.Copy, scale=scale).then_inc(banks.free_sem(unit), 1)

            def l0_tanh():
                act.wait_ge(*RB.filled("dd"))
                act.activation(th[:, :], RB.bank("dd")[:, :], ACT.Tanh).then_inc(r_act, 1)
                act.wait_ge(r_act, 1)
                act.activation(th[:, :], th[:, :], ACT.Tanh, scale=0.5).then_inc(th_done, 1)

            def l0_vre():
                copy("v", RB, vf, RB.bank("v")[:, :])
                copy("r", RB, rf, RB.bank("r")[:, :])

            def l0_kwe():
                copy("k", RB, kf[:, :], RB.bank("k")[:, :])
                act.wait_ge(*RB.filled("w"))
                act.activation(dec[:, 1:T], RB.bank("w")[:, 1:T], ACT.Tanh, scale=0.5).then_inc(r_act, 1)

            def l0_ge():
                act.wait_ge(*RB.filled("g"))
                act.activation(silu[:, :], RB.bank("g")[:, :], ACT.Tanh, scale=0.5).then_inc(tg_done, 1)

            def l0_gqe():
                copy("gq", RB, xq[:, :], RB.bank("gq")[:, :])

            def l0_gke():
                copy("gk", RB, xk[:, :], RB.bank("gk")[:, 0:G * NK])

            def l0_smalle():
                act.wait_ge(*RB.was_read("small"))
                act.activation(smt[:, :], sm[:, :], ACT.Tanh, scale=0.5).then_inc(smt_done, 1)

            def l0_axe(g):
                copy(f"ax{g}", RB, ax[:, g % 2, :], RB.bank(f"ax{g}")[:, :])

            def l0_exp():
                act.wait_ge(soft, 5)
                act.activation(sel[:, :], sel[:, :], ACT.Exp).then_inc(e0_done, 1)

            def l0_ptne():
                copy("ptn", RB, ptn[:, :], RB.bank("ptn")[0:G * H, 0:NQ])

            def l0_pte(g):
                copy(f"pt{g}", RB, pt0[:, g % 2, :, :].rearrange("p a b -> p (a b)"), RB.bank(f"pt{g}")[:, :])

            def l0_oe(g):
                copy(f"o{g}", RB, ob[:, g, :], RB.bank(f"o{g}")[:, 0:D])

            def l0_yTe():
                act.wait_ge(yT_fill, 1)
                act.activation(lp[:, 1, :], NBK[:, :], ACT.Copy).then_inc(yT_read, 1)

            def l1_xTe():
                copy("xT", TB, x2T[:, :], TB.bank("xT")[:, :])

            def l1_gates():
                act.wait_ge(*TB.was_read("gates"))
                act.activation(sg[:, :], zg[:, :], ACT.Exp, scale=-1.0).then_inc(ex_s, 1)
                act.wait_ge(*YB.filled("gt"))
                act.activation(xn2[0:SD, :, :].rearrange("p a b -> p (a b)"), YB.bank("gt")[0:SD, :], ACT.Tanh,
                               bias=bgt_s[:, 0:1], scale=0.5).then_inc(y_act, 1)

            def l1_chunk(n):
                for kind, lag in enumerate((Q_LAG, K_LAG)):
                    c = n - lag
                    if 0 <= c < NCHUNK and chunk_kind(c)[1:] == (kind, E - 1):
                        t = chunk_kind(c)[0]
                        copy(f"qk{2 * t + kind}", TB, qk[:, kind, :, t * P:(t + 1) * P],
                             TB.bank(f"qk{2 * t + kind}")[:, :].rearrange("p (c n) -> p c n", c=HP))

            def l1_att(a):
                if a < NATT:
                    act.wait_ge(max_done, a + 1)
                    if a == 2:
                        act.wait_ge(sum_add, adds_before(NCHUNK))
                    if a >= 3:
                        act.wait_ge(*TB.filled(f"pt{a - 3}"))
                    act.activation(pr[:, a % 3, :], SB.bank(f"s{a}")[:, :], ACT.Exp, bias=nmax[:, a:a + 1],
                                   accum_out=den[:, a:a + 1]).then_inc(s_act, 1)
                n = a - PT_LAG
                if 0 <= n < NATT:
                    if n >= 2:
                        act.wait_ge(pv_done, n - 1)
                    copy(f"pt{n}", TB, pt[:, n % 2, :, :].rearrange("p a b -> p (a b)"), TB.bank(f"pt{n}")[:, :])

            def l1_ze(t):
                act.wait_ge(*TB.filled(f"z{t}"))
                act.activation(zT[:, 0:2, :].rearrange("p a b -> p (a b)"), TB.bank(f"z{t}")[:, 0:2 * P],
                               ACT.Copy).then_inc(zt_done, 1)
                act.activation(zT[0:DH, 2, :], TB.bank(f"z{t}")[0:DH, 2 * P:3 * P], ACT.Copy).then_inc(t_act, 1)

            st = {("l0", "tanh"): l0_tanh, ("l0", "vre"): l0_vre, ("l0", "kwe"): l0_kwe, ("l0", "ge"): l0_ge,
                  ("l0", "gqe"): l0_gqe, ("l0", "gke"): l0_gke, ("l0", "smalle"): l0_smalle, ("l0", "axe"): l0_axe,
                  ("l0", "exp"): l0_exp, ("l0", "ptne"): l0_ptne, ("l0", "pte"): l0_pte, ("l0", "oe"): l0_oe,
                  ("l0", "yTe"): l0_yTe, ("l1", "xTe"): l1_xTe, ("l1", "gates"): l1_gates,
                  ("l1", "chunk"): l1_chunk, ("l1", "att"): l1_att, ("l1", "ze"): l1_ze}
            run(st, L0)
            step_over(act, 2)
            with act.Fori(0, B - 1) as i:
                run(st, BODY)
                step_over(act, i + 3)
            run(st, L1)

        @block.tensor
        def _(pe):
            def open_(banks, unit):
                f = banks.free_for(unit)
                if f is not None:
                    pe.wait_ge(*f)
                return banks.bank(unit)

            def logits(b):
                pe.wait_ge(*PB.was_read(f"xT{b}"))
                pe.matmul(LG[0:64, :], wr_pad[:, b, :], xt_ev[:, b % 2, :], start=(b == 0), stop=(b == B - 1))\
                  .then_inc(p_log, 1)
            pe.wait_ge(p_blk, 1)
            pe.wait_ge(p_cst, 9)
            for b in range(B):
                bk = open_(PB, f"xT{b}")
                pe.wait_ge(p_xn, NT * (b + 1))
                src, k = (xa, b) if b < 4 else (xb, b - 4)
                for t in range(NT):
                    mm = pe.transpose(bk[:, t * P:(t + 1) * P], src[:, k * T + t * D:k * T + (t + 1) * D], ident[:, :])
                mm.then_inc(p_fill, 1)
                if b >= 1:
                    logits(b - 1)
            logits(B - 1)
            pe.wait_ge(p_ld, 16 * N_LOADS)
            for g in range(G):
                for which in range(4):
                    bk = open_(PB, f"fold{4 * g + which}")
                    hp = slice((which % 2) * DH, (which % 2) * DH + DH)
                    l, r = (stage["wk"], stage["wq"]) if which < 2 else (stage["wv"], stage["wo"])
                    for c in range(HP):
                        mm = pe.matmul(bk[:, c * P:(c + 1) * P], l[hp, g, c, :], r[hp, g, c, :], start=True, stop=True)
                    mm.then_inc(p_fill, 1)
            pe.wait_ge(p_blk, 4)
            bk = open_(PB, "u")
            for g in range(G):
                for c in range(HP):
                    mm = pe.matmul(bk[:, g * H + 2 * c:g * H + 2 * c + 2], stage["wq"][:, g, c, :], nkb[:, g, c, :],
                                   start=True, stop=True)
            mm.then_inc(p_fill, 1)
            bk = open_(PB, "nvw")
            for g in range(G):
                for c in range(HP):
                    mm = pe.matmul(bk[0:G * H, g * D:(g + 1) * D], nvb[:, g, c * 32:(c + 1) * 32], stage["wo"][:, g, c, :],
                                   start=(c == 0), stop=(c == HP - 1))
            mm.then_inc(p_fill, 1)
            bk = open_(PB, "wf")
            pe.matmul(bk[:, 0:D], winT_s, wout_s, start=True, stop=True).then_inc(p_fill, 1)
            bk = open_(PB, "ws9")
            pe.matmul(bk[0:SD + 1, 0:D], bcol9, wout_s, start=True, stop=False)
            pe.matmul(bk[0:SD + 1, 0:D], ident[0:SD + 1, 0:SD + 1], wout9_s, start=False, stop=True).then_inc(p_fill, 1)
            bk = open_(PB, "wmisc")
            pe.matmul(bk[:, 0:SD], winT_s, wg_s, start=True, stop=False)
            pe.matmul(bk[:, 0:SD], winT8_s, wg8_s, start=False, stop=True)
            pe.matmul(bk[0:SD, SD:SD + 1], wg_s, bin_s, start=True, stop=False)
            pe.matmul(bk[0:SD, SD:SD + 1], wg8_s, bin8_s, start=False, stop=True).then_inc(p_fill, 1)
            pe.wait_ge(p_pos, 1)
            for t in range(NT):
                mm = pe.transpose(LG[:, t * 64:(t + 1) * 64], cum[:, t * P:(t + 1) * P], ident[0:64, 0:64])
            mm.then_inc(p_posT, 1)
            step_over(pe, 1)

            def l0_dd():
                bk = open_(RB, "dd")
                pe.matmul(bk[:, :], ddw_s[:, :], xTp[:, 0:T], start=True, stop=True).then_inc(r_fill, 1)

            def project(m):
                bk = open_(RB, "vrkw"[m])
                pe.wait_ge(lerp_ready, m + 1)
                pe.matmul(bk[:, :], projw_s[:, m, :], lp[:, m % 2, :], start=True, stop=True).then_inc(r_fill, 1)

            def l0_vr():
                project(0)
                project(1)

            def l0_kw():
                project(2)
                project(3)

            def l0_g():
                bk = open_(RB, "g")
                pe.wait_ge(lerp_ready, 5)
                for t in range(NT):
                    mm = pe.matmul(bk[:, t * P:(t + 1) * P], lp[:, 0, t * P:(t + 1) * P], projw_s[:, 4, :],
                                   start=True, stop=True)
                mm.then_inc(r_fill, 1)

            def gather(n, u, w):
                bk = open_(RB, u)
                pe.wait_ge(sel_ready, n)
                for t in range(NT):
                    mm = pe.matmul(bk[:, 0:G * w], xn[:, t, :], sel[:, t * G * w:(t + 1) * G * w],
                                   start=(t == 0), stop=(t == NT - 1))
                mm.then_inc(r_fill, 1)

            def l0_gq():
                pe.wait_ge(ld_xn, 16)
                gather(1, "gq", NQ)

            def l0_gk():
                gather(2, "gk", NK)

            def l0_small():
                bk = open_(RB, "small")
                pe.wait_ge(*RB.was_read("gk"))
                for g in range(G):
                    n = G * (H + 1) + g
                    pe.matmul(bk[:, g * (H + 1):(g + 1) * (H + 1)], xq[:, g * NQ:(g + 1) * NQ], u9_s[:, g, :],
                              start=True, stop=True)
                    pe.matmul(bk[0:NK, n:n + 1], xk[:, g * NK:(g + 1) * NK], qkr_s[:, G + g:G + g + 1],
                              start=True, stop=True)
                    mm = pe.matmul(bk[NK:2 * NK, n:n + 1], xk[:, g * NK:(g + 1) * NK], qkr_s[:, G + g:G + g + 1],
                                   start=True, stop=True)
                mm.then_inc(r_fill, 1)

            def l0_ax(g):
                bk = open_(RB, f"ax{g}")
                for h in range(H):
                    mm = pe.matmul(bk[:, h * NK:(h + 1) * NK], A_s[:, g, h % 2, h // 2, :], xk[:, g * NK:(g + 1) * NK],
                                   start=True, stop=True)
                mm.then_inc(r_fill, 1)

            def l0_s(g):
                bk = open_(RB, f"s{g}")
                pe.wait_ge(*RB.was_read(f"ax{g}"))
                pe.matmul(bk[:, :], xq[:, g * NQ:(g + 1) * NQ], ax[:, g % 2, :], start=True, stop=True).then_inc(r_fill, 1)

            def l0_wsum(q):
                bk = NBK
                pe.wait_ge(prod_done, q + 1)
                for j in range(2):
                    for t in range(NT):
                        first, last = q == 0 and j == 0 and t == 0, q == NPAIR - 1 and j == 1
                        mm = pe.matmul(bk[:, t * P:(t + 1) * P], vb[:, q % 2, j, t * P:(t + 1) * P], ident[:, :],
                                       is_transpose=True, start=first, stop=last, skip_group_check=True)
                mm.then_inc(ot_done, 1)

            def l0_yT():
                pe.wait_ge(gn, 2)
                pe.wait_ge(y_ready, 1)
                for t in range(NT):
                    mm = pe.transpose(NBK[:, t * P:(t + 1) * P], th[:, t * P:(t + 1) * P], ident[:, :])
                mm.then_inc(yT_fill, 1)

            def l0_att():
                pe.wait_ge(yT_read, 1)
                for t in range(NT):
                    mm = pe.matmul(NBK[:, t * P:(t + 1) * P], lp[:, 1, t * P:(t + 1) * P], oww_s[:, :], start=True, stop=True)
                mm.then_inc(att_fill, 1)

            def l0_ptn():
                bk = open_(RB, "ptn")
                pe.wait_ge(p0_ready, 2)
                pe.transpose(bk[0:G * H, 0:NQ], snull, ident[:, :]).then_inc(r_fill, 1)

            def l0_pt(g):
                bk = open_(RB, f"pt{g}")
                for c in range(HP):
                    mm = pe.transpose(bk[:, c * NQ:(c + 1) * NQ], sel[:, (g * HP + c) * P:(g * HP + c + 1) * P], ident[:, :])
                mm.then_inc(r_fill, 1)

            def l0_vw(g):
                bk = open_(RB, f"vw{g}")
                for hp in range(2):
                    mm = pe.matmul(bk[hp * NK:(hp + 1) * NK, :], xk[:, g * NK:(g + 1) * NK],
                                   M_s[:, g, hp, :, :].rearrange("p a b -> p (a b)"), start=True, stop=True)
                mm.then_inc(r_fill, 1)

            def l0_o(g):
                bk = open_(RB, f"o{g}")
                pe.wait_ge(*RB.was_read(f"pt{g}"))
                pe.wait_ge(*RB.was_read(f"vw{g}"))
                for c in range(HP):
                    pe.matmul(bk[:, 0:D], pt0[:, g % 2, c, :], vw[:, g % 2, c, :], start=(c == 0), stop=False)
                pe.matmul(bk[:, 0:D], ptn[:, :], nvw_s[:, g, :], start=False, stop=True).then_inc(r_fill, 1)

            def l0_scat():
                bk = open_(RB, "scat")
                pe.wait_ge(selT_ready, 1)
                pe.wait_ge(*RB.was_read(f"o{G - 1}"))
                for t in range(NT):
                    for g in range(G):
                        mm = pe.matmul(bk[:, t * P:(t + 1) * P], selT[:, g, t * P:(t + 1) * P], ob[:, g, :],
                                       start=(g == 0), stop=(g == G - 1))
                mm.then_inc(r_fill, 1)

            def l1_xT():
                bk = open_(TB, "xT")
                for t in range(NT):
                    mm = pe.transpose(bk[:, t * P:(t + 1) * P], xn2[:, t, :], ident[:, :])
                mm.then_inc(t_fill, 1)

            def l1_gates():
                bk = open_(TB, "gates")
                pe.wait_ge(*TB.was_read("xT"))
                n = 2 * H * E
                for t in range(NT):
                    mm = pe.matmul(bk[:, t * n:(t + 1) * n], x2T[:, t * P:(t + 1) * P], wsd_s[:, :], start=True, stop=True)
                mm.then_inc(t_fill, 1)
                pe.matmul(YB.bank("si")[0:SD, :], wsi_s[:, :], x2T[:, :], start=True, stop=True).then_inc(y_fill, 1)
                pe.matmul(YB.bank("gt")[0:SD, :], wgt_s[:, :], x2T[:, :], start=True, stop=True).then_inc(y_fill, 1)

            def l1_chunk(n):
                if n < NCHUNK:
                    t, kind, e = chunk_kind(n)
                    bk = open_(YB, f"y{n}")
                    pe.matmul(bk[:, :], x2T[:, t * P:(t + 1) * P], wqkv_s[:, kind, e, :], start=True, stop=True)\
                      .then_inc(y_fill, 1)
                c = n - Q_LAG
                if 0 <= c < NCHUNK and chunk_kind(c)[1] == 0:
                    t, _, e = chunk_kind(c)
                    u = f"qk{2 * t}"
                    bk = open_(TB, u) if e == 0 else TB.bank(u)
                    pe.wait_ge(y_dve, YB.was_read(f"y{c}")[1])
                    src = gated(c)
                    for p_ in range(HP):
                        mm = pe.matmul(bk[:, p_ * P:(p_ + 1) * P], src[:, p_ * P:(p_ + 1) * P], ident[:, :],
                                       is_transpose=True, start=(e == 0 and p_ == 0), stop=(e == E - 1),
                                       skip_group_check=True)
                    mm.then_inc(t_fill if e == E - 1 else tr_part, 1)
                c = n - K_LAG
                if 0 <= c < NCHUNK and chunk_kind(c)[1:] == (1, E - 1):
                    t = chunk_kind(c)[0]
                    bk = open_(TB, f"qk{2 * t + 1}")
                    pe.wait_ge(sum_add, adds_before(c + 1))
                    for p_ in range(HP):
                        mm = pe.transpose(bk[:, p_ * P:(p_ + 1) * P], k_or_v_sum(t, 1)[:, p_ * P:(p_ + 1) * P], ident[:, :])
                    mm.then_inc(t_fill, 1)

            def l1_att(a):
                if a < NATT:
                    t, h = a // H, a % H
                    hs = slice((h % 2) * DH, (h % 2) * DH + DH)
                    bk = open_(SB, f"s{a}")
                    if a == 0:
                        pe.wait_ge(*TB.was_read(f"qk{2 * NT - 1}"))
                        pe.wait_ge(*YB.was_read(f"y{NCHUNK - 1}"))
                    pe.matmul(bk[:, :], qk[hs, 0, h // 2, t * P:(t + 1) * P], qk[hs, 1, h // 2, :], start=True, stop=True)\
                      .then_inc(s_fill, 1)
                n = a - PT_LAG
                if 0 <= n < NATT:
                    bk = open_(TB, f"pt{n}")
                    pe.wait_ge(*SB.was_read(f"s{n}"))
                    for c in range(NT):
                        mm = pe.transpose(bk[:, c * P:(c + 1) * P], pr[:, n % 3, c * P:(c + 1) * P], ident[:, :])
                    mm.then_inc(t_fill, 1)
                n = a - PV_LAG
                if 0 <= n < NATT:
                    t, h = n // H, n % H
                    if n == 0:
                        pe.wait_ge(sum_add, adds_before(NCHUNK))
                    if t > 0 and h == 0:
                        pe.wait_ge(o_dve, t)
                    pe.wait_ge(*TB.was_read(f"pt{n}"))
                    for c in range(NT):
                        mm = pe.matmul(OBK[:, h * DH:(h + 1) * DH], pt[:, n % 2, c, :], vv[:, c, h * DH:(h + 1) * DH],
                                       start=(c == 0), stop=(c == NT - 1))
                    mm.then_inc(pv_done, 1)

            def l1_z(t):
                bk = open_(TB, f"z{t}")
                pe.wait_ge(half_add, t + 1)
                for h in range(HALF):
                    for c in range(3):
                        w = min(P, E * DH - c * P)
                        k = h * E * DH + c * P
                        mm = pe.matmul(bk[0:w, c * P:(c + 1) * P], yg[:, k:k + w], ident[:, :], is_transpose=True,
                                       start=(h == 0 and c == 0), stop=(h == HALF - 1), skip_group_check=True)
                mm.then_inc(t_fill, 1)

            def l1_fin(t):
                bk = open_(TB, f"f{t}")[:, 0:D]
                ts = slice(t * P, (t + 1) * P)
                if t == 0:
                    pe.wait_ge(st_ready, 1)
                pe.matmul(bk, x2T[:, ts], wfold_s[:, :], start=True, stop=False)
                pe.matmul(bk, st9[:, ts], ws9_s[:, :], start=False, stop=False)
                pe.wait_ge(zt_done, t + 1)
                pe.wait_ge(*TB.was_read(f"z{t}"))
                pe.matmul(bk, zT[:, 0, :], wor_s[:, 0, :], start=False, stop=False)
                pe.matmul(bk, zT[:, 1, :], wor_s[:, 1, :], start=False, stop=False)
                pe.matmul(bk, zT[0:DH, 2, :], wor_s[0:DH, 2, :], start=False, stop=True).then_inc(t_fill, 1)

            st = {("l0", "dd"): l0_dd, ("l0", "vr"): l0_vr, ("l0", "kw"): l0_kw, ("l0", "g"): l0_g, ("l0", "gq"): l0_gq,
                  ("l0", "gk"): l0_gk, ("l0", "small"): l0_small, ("l0", "ax"): l0_ax, ("l0", "s"): l0_s,
                  ("l0", "wsum"): l0_wsum, ("l0", "yT"): l0_yT, ("l0", "att"): l0_att, ("l0", "ptn"): l0_ptn,
                  ("l0", "pt"): l0_pt, ("l0", "vw"): l0_vw, ("l0", "o"): l0_o, ("l0", "scat"): l0_scat,
                  ("l1", "xT"): l1_xT, ("l1", "gates"): l1_gates, ("l1", "chunk"): l1_chunk,
                  ("l1", "att"): l1_att, ("l1", "z"): l1_z, ("l1", "fin"): l1_fin}
            run(st, L0)
            step_over(pe, 2)
            with pe.Fori(0, B - 1) as i:
                run(st, BODY)
                step_over(pe, i + 3)
            run(st, L1)

        @block.vector
        def _(dve):
            dve.memset(wr_pad, 0.0).then_inc(p_zero, 1)
            dve.memset(nkb, 0.0).then_inc(p_zero, 1)
            dve.memset(nvb, 0.0).then_inc(p_zero, 1)
            dve.wait_ge(p_zero, 3)
            dve.wait_ge(p_ldw, 16)
            for b in range(B):
                for k in range(2):
                    last = dve.tensor_copy(wr_pad[:, b, k * 32 + b * G:k * 32 + (b + 1) * G], qkr_s[:, k * G:(k + 1) * G])
            last.then_inc(p_blk, 1)
            dve.wait_ge(p_ldx, 16 * B)

            def batch(b):
                src, k = (xa, b) if b < 4 else (xb, b - 4)
                return src[:, k * T:(k + 1) * T]

            for b in range(B):
                for t in range(NT):
                    last = dve.bn_stats(stats[:, b * NT + t, :], batch(b)[:, t * D:(t + 1) * D])
            last.then_inc(p_bn, 1)
            dve.wait_ge(p_bn, 1)
            for n in range(B * NT):
                last = dve.bn_aggr(mv[:, n, :], stats[:, n, :])
            last.then_inc(p_bn, 1)
            dve.wait_ge(p_bn, 2)
            dve.tensor_scalar(lv[:, :], mv[:, :, 1], LN_EPS, None, ALU.add).then_inc(p_nt, 1)
            dve.wait_ge(p_nt, 1)
            newton(dve, ly, lv, lw, B * NT, p_nt, 1)
            for n in range(B * NT):
                xt = batch(n // NT)[:, (n % NT) * D:(n % NT + 1) * D]
                dve.tensor_scalar(xt, xt, mv[:, n, 0:1], ly[:, n:n + 1], ALU.subtract, ALU.mult).then_inc(p_xn, 1)
            dve.wait_ge(p_ld, 16 * N_LOADS)
            dve.memset(bcol9, 0.0).then_inc(p_zero, 1)
            dve.wait_ge(p_zero, 4)
            dve.tensor_copy(bcol9[:, SD:SD + 1], bin_s)
            for hp in range(2):
                ps = slice(hp * DH, (hp + 1) * DH)
                dve.tensor_copy(nkb[ps, :, :, hp], nkt[ps, :, :])
                for g in range(G):
                    first = g * H + hp
                    dve.tensor_copy(nvb[ps, g, first:first + 34 * (HP - 1) + 1:34], nvt[ps, g, :])
            dve.tensor_copy(u9_s[:, :, H], qkr_s[:, 0:G])
            dve.tensor_scalar(gnw_s[:, :], gnw_s[:, :], 0.5, None, ALU.mult)
            dve.tensor_scalar(gnb_s[:, :], gnb_s[:, :], 0.5, None, ALU.mult).then_inc(p_blk, 3)
            dve.wait_ge(p_cst, 9)
            dve.wait_ge(p_log, B)
            dve.tensor_copy(lgw, LG[0:64, :]).then_inc(p_top, 1)
            n = 1
            for k in range(ROUNDS_Q):
                rows = slice(0, 64 if k < ROUNDS_K else 32)
                dve.wait_ge(p_top, n)
                dve.max(top8[rows], lgw[rows]).then_inc(p_top, 1)
                dve.wait_ge(p_top, n + 1)
                dve.match_replace(lgw[rows], top8[rows], lgw[rows], PICKED).then_inc(p_top, 1)
                n += 2
            dve.wait_ge(p_top, n)
            dve.tensor_scalar(msk, lgw, PICKED, None, ALU.is_le).then_inc(p_top, 1)
            dve.wait_ge(p_top, n + 1)
            dve.tensor_tensor_scan(cum, onesr, msk, 0.0, ALU.mult, ALU.add).then_inc(p_top, 1)
            dve.wait_ge(p_top, n + 2)
            dve.tensor_tensor(cum, cum, msk, ALU.mult).then_inc(p_pos, 1)
            dve.wait_ge(p_posT, 1)
            for k in range(2):
                last = dve.tensor_copy(posTb[:, :, :, k, :],
                                       LG[:, 0:NT * 64].rearrange("p (t k b g) -> p k b t g", t=NT, k=2, b=B)[:, k])
            last.then_inc(p_pos, 1)
            dve.wait_ge(*PB.filled("wmisc"))
            wm = PB.bank("wmisc")
            dve.tensor_copy(wgt_s[:, :], wm[:, 0:SD])
            dve.tensor_scalar(bgt_s[:, :], wm[0:SD, SD:SD + 1], bg_s, 0.5, ALU.add, ALU.mult).then_inc(p_dve, 1)
            step_over(dve, 1)

            def l0_lerp():
                dve.wait_ge(th_done, 1)
                dve.wait_ge(dif_ready, 1)
                dve.scalar_tensor_tensor(out=th[:, :], in0=th[:, :], scalar=1.0, in1=dif[:, :],
                                         op0=ALU.add, op1=ALU.mult).then_inc(e_done, 1)
                dve.wait_ge(e_done, 1)
                dve.scalar_tensor_tensor(out=aa[:, :], in0=th[:, :], scalar=0.5, in1=xTp[:, 0:T],
                                         op0=ALU.mult, op1=ALU.add).then_inc(af_ready, 1)
                dve.scalar_tensor_tensor(out=dif[:, :], in0=th[:, :], scalar=-0.5, in1=dif[:, :],
                                         op0=ALU.mult, op1=ALU.add).then_inc(af_ready, 1)
                dve.wait_ge(af_ready, 2)

                for m in range(2):
                    lerp(m)

            def lerp(m):
                dve.scalar_tensor_tensor(out=lp[:, m % 2, :], in0=dif[:, :], scalar=mix_s[:, m:m + 1], in1=aa[:, :],
                                         op0=ALU.mult, op1=ALU.add).then_inc(lerp_ready, 1)

            def l0_vre():
                for m in range(2, 4):
                    dve.wait_ge(*RB.filled("vr"[m - 2]))
                    lerp(m)

            def l0_kwe():
                dve.wait_ge(*RB.filled("k"))
                lerp(4)

            def l0_ge():
                half = 0.5 * 0.6065306597126334
                dve.wait_ge(*RB.was_read("w"))
                dve.tensor_scalar(dec[:, 1:T], dec[:, 1:T], half, half, ALU.mult, ALU.add).then_inc(dec_ready, 1)
                dve.wait_ge(tg_done, 1)
                dve.wait_ge(*RB.filled("g"))
                dve.scalar_tensor_tensor(out=silu[:, :], in0=silu[:, :], scalar=1.0, in1=RB.bank("g")[:, :],
                                         op0=ALU.add, op1=ALU.mult).then_inc(r_dve, 1)

            def selection(k, w):
                dve.tensor_tensor(sel[:, 0:NT * G * w].rearrange("p (t g j) -> p t g j", t=NT, g=G),
                                  iota1[:, 0:w].unsqueeze(1).unsqueeze(1).broadcast_to((P, NT, G, w)),
                                  posT[:, :, k, :].unsqueeze(3).broadcast_to((P, NT, G, w)), ALU.is_equal)\
                   .then_inc(sel_ready, 1)

            def l0_selq():
                dve.wait_ge(ld_posT, 16)
                selection(0, NQ)

            def l0_gqe():
                dve.wait_ge(*RB.filled("gq"))
                selection(1, NK)
                dve.tensor_scalar(cnt4[:, :, :], posT[:, :, 0, :], 0.5, None, ALU.is_gt).then_inc(cnt_s, 1)
                dve.wait_ge(cnt_s, 1)
                dve.tensor_reduce(cnt[:, :], cnt4[:, :, :], X, ALU.add).then_inc(cnt_s, 1)
                dve.wait_ge(cnt_s, 2)
                dve.tensor_scalar(nz[:, :], cnt[:, :], 0.5, None, ALU.is_lt).then_inc(cnt_s, 1)
                dve.tensor_scalar(rcnt[:, :], cnt[:, :], 1.0, None, ALU.max).then_inc(cnt_s, 1)
                dve.wait_ge(cnt_s, 4)
                dve.reciprocal(rcnt[:, :], rcnt[:, :]).then_inc(cnt_s, 1)

            def l0_gke():
                dve.wait_ge(ld_pos, 16)
                dve.tensor_scalar(selT[:, :, :], selT[:, :, :], iotac[:, 0:1], None, ALU.is_equal).then_inc(selT_ready, 1)

            def l0_scan(q):
                if q == 0:
                    dve.wait_ge(dec_ready, 1)
                dve.wait_ge(kv_done, q + 1)
                for j in range(2):
                    v1 = vb[:, q % 2, j, :]
                    dve.tensor_tensor_scan(v1, dec[:, :], v1, 0.0, ALU.mult, ALU.add).then_inc(scan_done, 1)

            def l0_smalle():
                dve.wait_ge(*RB.filled("small"))
                dve.tensor_copy(sm[:, :], RB.bank("small")[:, 0:G * (H + 1) + G]).then_inc(r_dve, 1)
                dve.wait_ge(*RB.was_read("small"))
                dve.tensor_copy(snull.rearrange("p (g h) -> p g h", g=G),
                                sm[:, 0:G * (H + 1)].rearrange("p (g n) -> p g n", g=G)[:, :, 0:H]).then_inc(soft, 1)

            def l0_se(g):
                dve.wait_ge(*RB.filled(f"s{g}"))
                dve.tensor_copy(sel[:, g * H * NK:(g + 1) * H * NK], RB.bank(f"s{g}")[:, :]).then_inc(r_dve, 1)

            def l0_soft():
                dve.wait_ge(soft, 1)
                dve.wait_ge(*RB.was_read(f"s{G - 1}"))
                dve.tensor_reduce(hmax[:, :], skeys, X, ALU.max).then_inc(soft, 1)
                dve.wait_ge(soft, 2)
                dve.tensor_tensor(hmax[:, :], hmax[:, :], snull, ALU.max).then_inc(soft, 1)

            def l0_shift():
                dve.wait_ge(soft, 3)
                dve.tensor_tensor(snull, snull, hmax[:, :], ALU.subtract).then_inc(soft, 1)
                dve.tensor_tensor(skeys, skeys, hmax[:, :].unsqueeze(2).broadcast_to((P, G * H, NK)), ALU.subtract)\
                   .then_inc(soft, 1)

            def l0_sums():
                dve.wait_ge(smt_done, 1)
                dve.tensor_scalar(smt[:, :], smt[:, :], 0.5, 0.5, ALU.mult, ALU.add).then_inc(sig_ready, 1)
                dve.wait_ge(e0_done, 1)
                dve.tensor_reduce(hsum[:, :], skeys, X, ALU.add).then_inc(soft, 1)
                dve.wait_ge(soft, 6)
                dve.tensor_tensor(hsum[:, :], hsum[:, :], snull, ALU.add).then_inc(soft, 1)
                dve.wait_ge(soft, 7)
                dve.reciprocal(hsum[:, :], hsum[:, :]).then_inc(soft, 1)
                dve.wait_ge(soft, 8)
                dve.wait_ge(sig_ready, 1)
                dve.tensor_tensor(hsum[:, :].rearrange("p (g h) -> p g h", g=G),
                                  hsum[:, :].rearrange("p (g h) -> p g h", g=G),
                                  smt[:, 0:G * (H + 1)].rearrange("p (g n) -> p g n", g=G)[:, :, H:H + 1]
                                  .broadcast_to((P, G, H)), ALU.mult).then_inc(soft, 1)

            def l0_vwe(g):
                dve.wait_ge(*RB.filled(f"vw{g}"))
                n = G * (H + 1) + g
                dve.tensor_scalar(vw[:, g % 2, :, :].rearrange("p c d -> p (c d)"), RB.bank(f"vw{g}")[:, :],
                                  smt[:, n:n + 1], None, ALU.mult).then_inc(r_dve, 1)

            def l0_gn1():
                dve.wait_ge(ot_done, NPAIR)
                o3 = NBK[:, :].rearrange("p (n k) -> p n k", k=ADH)
                c3 = th[:, :].rearrange("p (n k) -> p n k", k=ADH)
                n = NT * AH
                dve.tensor_reduce(mu[:, :], o3, X, ALU.add).then_inc(gn, 1)
                dve.wait_ge(gn, 1)
                dve.scalar_tensor_tensor(out=c3, in0=mu[:, :].unsqueeze(2).broadcast_to((P, n, ADH)), scalar=-1.0 / ADH,
                                         in1=o3, op0=ALU.mult, op1=ALU.add).then_inc(gn, 1)

            def l0_gn2():
                c3 = th[:, :].rearrange("p (n k) -> p n k", k=ADH)
                n = NT * AH
                dve.wait_ge(sq_done, 1)
                dve.tensor_reduce(va[:, :], lp[:, 0, :].rearrange("p (n k) -> p n k", k=ADH), X, ALU.add).then_inc(gn, 1)
                dve.wait_ge(gn, 3)
                dve.tensor_scalar(va[:, :], va[:, :], 1.0 / ADH, GN_EPS, ALU.mult, ALU.add).then_inc(gn, 1)
                dve.wait_ge(gn, 4)
                newton(dve, ya, va, wa, n, gn, 4)
                dve.tensor_tensor(c3, c3, ya[:, :].unsqueeze(2).broadcast_to((P, n, ADH)), ALU.mult).then_inc(gn, 1)

            def l0_join():
                x3 = xq[:, :].rearrange("p (t d) -> p t d", t=NT)
                dve.wait_ge(*RB.filled("scat"))
                dve.wait_ge(cnt_s, 5)
                dve.tensor_tensor(x3, RB.bank("scat")[:, :].rearrange("p (t d) -> p t d", t=NT),
                                  rcnt[:, :].unsqueeze(2).broadcast_to((P, NT, D)), ALU.mult).then_inc(r_dve, 1)
                dve.wait_ge(*RB.was_read("scat"))
                dve.wait_ge(att_fill, 1)
                dve.tensor_tensor(xq[:, :], xq[:, :], NBK[:, :], ALU.add).then_inc(join_s, 1)

            def l0_ln():
                dve.wait_ge(x1_new, 1)
                for t in range(NT):
                    last = dve.bn_stats(stats[:, t, :], xr[:, t, :])
                last.then_inc(ln_s, 1)
                dve.wait_ge(ln_s, 1)
                for t in range(NT):
                    last = dve.bn_aggr(mv[:, t, :], stats[:, t, :])
                last.then_inc(ln_s, 1)
                dve.wait_ge(ln_s, 2)
                dve.tensor_scalar(lv[:, 0:NT], mv[:, 0:NT, 1], LN_EPS, None, ALU.add).then_inc(ln_s, 1)
                dve.wait_ge(ln_s, 3)
                newton(dve, ly, lv, lw, NT, ln_s, 3)
                for t in range(NT):
                    dve.tensor_scalar(xn2[:, t, :], xr[:, t, :], mv[:, t, 0:1], ly[:, t:t + 1],
                                      ALU.subtract, ALU.mult)

            NG = NT * 2 * H
            z3 = zg[:, :].rearrange("p (n e) -> p n e", e=E)
            w3 = wins[:, :].rearrange("p (n e) -> p n e", e=E)

            def l1_gates():
                dve.wait_ge(*TB.filled("gates"))
                dve.tensor_scalar(zg[:, :], TB.bank("gates")[:, 0:NG * E], Z_HI, Z_LO, ALU.min, ALU.max).then_inc(t_dve, 1)
                dve.tensor_copy(w3, rank0[:, :].unsqueeze(1).broadcast_to((P, NG, E))).then_inc(rank_s, 1)
                dve.wait_ge(*TB.was_read("gates"))

            def l1_rank(d):
                n = 1 + 3 * (d - 1)
                b3 = beat[:, 0:NG * (E - d)].rearrange("p (n e) -> p n e", e=E - d)
                if d > 1:
                    dve.wait_ge(rank_s, n)
                dve.tensor_tensor(b3, z3[:, :, 0:E - d], z3[:, :, d:E], ALU.is_ge).then_inc(rank_s, 1)
                dve.wait_ge(rank_s, n + 1)
                dve.tensor_tensor(w3[:, :, 0:E - d], w3[:, :, 0:E - d], b3, ALU.add).then_inc(rank_s, 1)
                dve.wait_ge(rank_s, n + 2)
                dve.tensor_tensor(w3[:, :, d:E], w3[:, :, d:E], b3, ALU.subtract).then_inc(rank_s, 1)

            def l1_sig():
                n = 1 + 3 * (E - 1)
                dve.wait_ge(rank_s, n)
                dve.tensor_scalar(wins[:, :], wins[:, :], E - TOPK - 0.5, None, ALU.is_gt).then_inc(rank_s, 1)
                dve.wait_ge(ex_s, 1)
                dve.tensor_scalar(sg[:, :], sg[:, :], 1.0, None, ALU.add).then_inc(rank_s, 1)
                dve.wait_ge(rank_s, n + 2)
                dve.reciprocal(sg[:, :], sg[:, :]).then_inc(rank_s, 1)
                dve.wait_ge(rank_s, n + 3)
                g4 = sg[:, :].rearrange("p (t k n) -> p t k n", t=NT, k=2)
                m4 = wins[:, :].rearrange("p (t k n) -> p t k n", t=NT, k=2)
                dve.tensor_tensor(g4[:, :, 0, :], g4[:, :, 0, :], m4[:, :, 0, :], ALU.mult).then_inc(gates_ready, 1)
                dve.scalar_tensor_tensor(out=g4[:, :, 1, :], in0=g4[:, :, 1, :], scalar=SCALE, in1=m4[:, :, 1, :],
                                         op0=ALU.mult, op1=ALU.mult).then_inc(gates_ready, 1)
                gate, inp = xn2[0:SD, :, :].rearrange("p a b -> p (a b)"), pr[0:SD, 0, :]
                dve.wait_ge(*YB.was_read("gt"))
                dve.tensor_scalar(inp, gate, -0.5, 0.5, ALU.mult, ALU.add).then_inc(sc_s, 1)
                dve.wait_ge(sc_s, 1)
                dve.tensor_scalar(gate, gate, 0.5, 0.5, ALU.mult, ALU.add).then_inc(sc_s, 1)
                dve.wait_ge(*YB.filled("si"))
                dve.scalar_tensor_tensor(out=inp, in0=YB.bank("si")[0:SD, :], scalar=bsi_s[:, 0:1], in1=inp,
                                         op0=ALU.add, op1=ALU.mult).then_inc(y_dve, 1)
                dve.wait_ge(sc_s, 2)
                dve.wait_ge(*YB.was_read("si"))
                dve.tensor_tensor_scan(st9[0:SD, :], gate, inp, 0.0, ALU.mult, ALU.add).then_inc(st_ready, 1)
                dve.wait_ge(gates_ready, 2)
                dve.wait_ge(st_ready, 1)

            g5 = sg[:, :].rearrange("p (t k h e) -> p t k h e", t=NT, k=2, h=H)

            def l1_chunk(n):
                c = n - G_LAG
                if not 0 <= c < NCHUNK:
                    return
                t, kind, e = chunk_kind(c)
                if kind == 0:
                    old = [k for k in range(c) if chunk_kind(k)[1] == 0]
                    if len(old) >= 3:
                        ot, _, oe = chunk_kind(old[-3])
                        if oe == E - 1:
                            dve.wait_ge(*TB.filled(f"qk{2 * ot}"))
                        else:
                            dve.wait_ge(tr_part, sum(1 for k in old[:-2] if chunk_kind(k)[2] < E - 1))
                elif e == 0:
                    if kind == 1 and t >= 2:
                        dve.wait_ge(*TB.filled(f"qk{2 * (t - 2) + 1}"))
                elif adds_before(c) >= 3:
                    dve.wait_ge(sum_add, adds_before(c) - 2)
                dve.wait_ge(*YB.filled(f"y{c}"))
                dve.tensor_tensor(gated(c).rearrange("p (h d) -> p h d", h=H),
                                  YB.bank(f"y{c}")[:, :].rearrange("p (h d) -> p h d", h=H),
                                  g5[:, t, 1 if kind == 0 else 0, :, e].unsqueeze(2).broadcast_to((P, H, DH)),
                                  ALU.mult).then_inc(y_dve, 1)

            def l1_att(a):
                t, r = divmod(a - D_LAG, H)
                if r == 0 and 0 <= t < NT:
                    hs = slice(t * H, (t + 1) * H)
                    dve.wait_ge(*SB.was_read(f"s{H * t + H - 1}"))
                    dve.reciprocal(rden[:, hs], den[:, hs]).then_inc(rden_s, 1)
                    dve.wait_ge(rden_s, t + 1)
                    if t >= 2:
                        dve.wait_ge(zm_ready, 2 * (t - 1))
                    dve.wait_ge(pv_done, H * (t + 1))
                    dve.tensor_tensor(oo[:, t % 2, :].rearrange("p (h d) -> p h d", h=H),
                                      OBK[:, :].rearrange("p (h d) -> p h d", h=H),
                                      rden[:, hs].unsqueeze(2).broadcast_to((P, H, DH)), ALU.mult).then_inc(o_dve, 1)
                if a < NATT:
                    dve.wait_ge(*SB.filled(f"s{a}"))
                    dve.tensor_reduce(nmax[:, a:a + 1], SB.bank(f"s{a}")[:, :], X, ALU.max, negate=True)\
                       .then_inc(max_done, 1)
                t, r = divmod(a - A_LAG, H)
                if r == 0 and 0 <= t < NT:
                    n = HALF * E * DH
                    dve.wait_ge(zm_ready, 2 * t + 2)
                    dve.tensor_tensor(yg[:, 0:n], yg[:, 0:n], yg[:, n:2 * n], ALU.add).then_inc(half_add, 1)

            def l1_fin(t):
                dve.wait_ge(*TB.filled(f"f{t}"))
                if t == 0:
                    dve.wait_ge(x1_copied, 1)
                dve.tensor_tensor(x1[:, t, :], x1[:, t, :], TB.bank(f"f{t}")[:, 0:D], ALU.add).then_inc(t_dve, 1)

            st = {("l0", "lerp"): l0_lerp, ("l0", "vre"): l0_vre, ("l0", "kwe"): l0_kwe, ("l0", "ge"): l0_ge,
                  ("l0", "selq"): l0_selq, ("l0", "gqe"): l0_gqe, ("l0", "gke"): l0_gke, ("l0", "scan"): l0_scan,
                  ("l0", "smalle"): l0_smalle, ("l0", "se"): l0_se, ("l0", "soft"): l0_soft, ("l0", "sums"): l0_sums,
                  ("l0", "vwe"): l0_vwe, ("l0", "gn1"): l0_gn1, ("l0", "gn2"): l0_gn2, ("l0", "join"): l0_join,
                  ("l0", "shift"): l0_shift, ("l0", "ln"): l0_ln,
                  ("l1", "gates"): l1_gates, ("l1", "rank"): l1_rank, ("l1", "sig"): l1_sig, ("l1", "chunk"): l1_chunk,
                  ("l1", "att"): l1_att, ("l1", "fin"): l1_fin}
            run(st, L0)
            step_over(dve, 2)
            with dve.Fori(0, B - 1) as i:
                run(st, BODY)
                step_over(dve, i + 3)
            run(st, L1)


def kernel(**inputs):
    import numpy as np
    import concourse.bacc as _bacc
    from concourse import mybir as _mybir
    from concourse.bass_utils import run_bass_kernel_spmd as _run

    a = {k: np.asarray(v) for k, v in inputs.items()}
    heads = lambda w: w.reshape(G, HP, P, D).transpose(2, 0, 1, 3)
    wkv = a["L0_ffn_w_kv"]
    null = a["L0_ffn_null_kv"].reshape(2, G, HP, P).transpose(0, 3, 1, 2)
    wq5 = a["L1_ffn_Wq"].reshape(D, H, E, DH).transpose(0, 2, 1, 3).reshape(D, 1, E, CW)
    wkv5 = a["L1_ffn_Wkv"].reshape(D, 2, H, E, DH).transpose(0, 1, 3, 2, 4).reshape(D, 2, E, CW)
    wo5 = a["L1_ffn_Wo"].reshape(DH, E, D).transpose(1, 0, 2).reshape(E * DH, D)
    wor = np.zeros((3 * P, D), wo5.dtype)
    wor[:E * DH] = wo5
    win, bin_ = a["L1_attn_W_in"], a["L1_attn_b_in"]
    laid = {
        "x": a["L0_attn_x"],
        "ddw": a["L0_attn_ddlerp_w"].T,
        "mixes": np.stack([a[f"L0_attn_mix_{n}"] for n in "vrkwg"], axis=1),
        "projw": np.stack([a[f"L0_attn_{n}_w"].T for n in ("v", "r", "k", "w", "g", "out")], axis=1),
        "gnw": a["L0_attn_gn_weight"], "gnb": a["L0_attn_gn_bias"],
        "qkr": np.concatenate([a["L0_ffn_w_qr"], a["L0_ffn_w_kvr"]]).T,
        "wqn": heads(a["L0_ffn_w_q"]), "wkn": heads(wkv[:, :H * DH]), "wvn": heads(wkv[:, H * DH:]),
        "won": heads(a["L0_ffn_w_out"].transpose(0, 2, 1)),
        "nkT": null[0], "nvT": null[1], "null_token": a["L0_ffn_null_token"].reshape(D),
        "winT": win[:, :D].T, "winT8": win[:, D:].T, "wcat": win[:, D:],
        "wg": a["L1_attn_W_g"][:D], "wg8": a["L1_attn_W_g"][D:],
        "bin_": bin_[:D, None], "bin8": bin_[D:, None], "bg": a["L1_attn_b_g"][:, None],
        "wout": a["L1_attn_W_out"][:D],
        "wout9": np.concatenate([a["L1_attn_W_out"][D:], a["L1_attn_b_out"][None]]),
        "wqkv": np.concatenate([wq5, wkv5], axis=1),
        "wsd": np.concatenate([a["L1_ffn_Ws"], a["L1_ffn_Wd"]], axis=1),
        "wor": wor.reshape(3, P, D),
    }
    nc = _bacc.Bacc("TRN2", target_bir_lowering=False, num_devices=1)
    arrays, args = {}, []
    for name, arr in laid.items():
        arr = np.ascontiguousarray(arr)
        arrays[f"in_{name}_dram"] = arr
        args.append(nc.dram_tensor(f"in_{name}_dram", arr.shape, _mybir.dt.from_np(arr.dtype), kind="ExternalInput").ap())
    args.append(nc.dram_tensor("out_0_dram", (B, T, D), F32, kind="ExternalOutput").ap())
    layers(nc, *args)
    r = _run(nc, [arrays], core_ids=[0])
    return r.results[0]["out_0_dram"]
```

```python
from contextlib import ExitStack

import concourse.bass as bass
from concourse import mybir

F32 = mybir.dt.float32
I32 = mybir.dt.int32
ALU = mybir.AluOpType
ACT = mybir.ActivationFunctionType
X = mybir.AxisListType.X

P = 128
B, T, D = 8, 512, 128
NT = T // P
LN_EPS = 1e-5

AH, ADH = 16, 8
GN_EPS = 0.00064
NPAIR = 4

G, NQ, NK = 4, 128, 64
H, DH = 8, 64
HP = H // 2
NKEY = NK + 1
PICKED = -3.0e38
ROUNDS_Q, ROUNDS_K = NQ // 8, NK // 8

GT_ROW = 96
SD = 8
E, TOPK = 5, 3
KINDS = 3
QUERY, KEY, VALUE = range(KINDS)
CW = H * DH
SCALE = DH ** -0.5
TAKES = (1, 2, 3, 4)
TURNED = tuple(e for e in range(E) if e + 1 not in TAKES)
NCHUNK = NT * KINDS * E
NATT = NT * H

Z_LO, Z_HI = -88.7, 16.6355


G_LAG, Q_LAG, S_LAG, K_LAG = 1, 3, 2, 5
A_KNOTS = ((0.0, 10.9), (0.438, 65.2), (0.458, 69.0), (1.0, 139.6))
W_KNOTS = ((0.0, 24.0), (0.41, 69.7), (0.44, 74.9), (1.0, 136.2))
PT_LAG, PV_LAG = 2, 3
HALF = H // 2
D_LAG = PV_LAG + H
T_LAG, M_LAG = D_LAG + 1, D_LAG + 2
A_LAG, Z_LAG, F_LAG = (D_LAG + 5, D_LAG + 6, D_LAG + 7), D_LAG + 8, D_LAG + 10

N_LOADS, N_LOADS_M = 18, 5


class Banks:

    def __init__(self, banks, filled, freed, units):
        self.banks, self.filled_sem, self.freed = banks, filled, freed
        self.at = {u[0]: n for n, u in enumerate(units)}
        self.reader = [u[1] for u in units]
        self.where = [u[2] if len(u) > 2 else n % len(banks) for n, u in enumerate(units)]

    def bank(self, name):
        return self.banks[self.where[self.at[name]]]

    def filled(self, name):
        return self.filled_sem, self.at[name] + 1

    def _read(self, n):
        who = self.reader[n]
        return self.freed[who], sum(1 for r in self.reader[:n + 1] if r == who)

    def free_for(self, name):
        n = self.at[name]
        before = [m for m in range(n) if self.where[m] == self.where[n]]
        return self._read(before[-1]) if before else None

    def free_sem(self, name):
        return self.freed[self.reader[self.at[name]]]

    def was_read(self, name):
        return self._read(self.at[name])


def chunk_kind(c):
    return c // (KINDS * E), (KEY, QUERY, VALUE)[c // E % KINDS], c % E


def l0_slots():
    early = [(-0.1, ("dd",)), (0.9, ("tanh",)), (1.9, ("lerp",)), (4.1, ("vr",)), (4.6, ("vre",))]
    a = [[("lerp2",)], [("kw",)], [("kwe",)], [("g",)], [("ge",)], [("selq", 0)], [("selq", 1)], [("gq",)], [("gqe",)],
         [("gk",)], [("gke",)], [("small",)], [("smalle",), ("ax", 0)]]
    for g in range(G):
        a.append([("axe", g)] + ([("se", g - 1)] if g else []))
        a.append([("s", g)] + ([("ax", g + 1)] if g + 1 < G else []))
    a += [[("se", G - 1)], [("soft", 0)], [("soft", 1)], [("shift", 0)], [("shift", 1)], [("exp",)], [("sums", 0)],
          [("sums", 1)], [("norm",)], [], [("ptn",)], [("ptne",), ("pt", 0)], [("pte", 0), ("vw", 0)]]
    for g in range(G):
        a.append([("vwe", g)])
        a.append([("o", g)] + ([("pt", g + 1)] if g + 1 < G else []))
        a.append([("oe", g)] + ([("pte", g + 1)] if g + 1 < G else []))
        if g + 1 < G:
            a.append([("vw", g + 1)])
    w = [[("kv", 0)], [("scan", 0)], [("kv", 1)], [("prod", 0)], [("scan", 1)], [("wsum", 0)], [("prod", 1)], [("kv", 2)],
         [("wsum", 1)], [("scan", 2)], [("kv", 3)], [("prod", 2)], [("scan", 3)], [("wsum", 2)], [("prod", 3)],
         [("wsum", 3)], [("gn1",)], [("gnsq",)], [("gn2",)], [("root", 0)], [("root", 1)], [("root", 2)], [("gn3",)], [("yT",)], [("yTe",)], [("att",)],
         [("base",)], [("x0",)]]
    tail = [(LAST_TURN + 0.1, ("scat",)), (LAST_TURN + 0.2, ("join",)), (LAST_FIN + 0.1, ("ln",))]
    out = early + tail
    for slots, knots in ((a, A_KNOTS), (w, W_KNOTS)):
        for k, slot in enumerate(slots):
            share = k / (len(slots) - 1)
            (s0, t0), (s1, t1) = [pair for pair in zip(knots, knots[1:]) if share <= pair[1][0]][0]
            out += [(t0 + (t1 - t0) * (share - s0) / (s1 - s0), u) for u in slot]
    return sorted(out, key=lambda u: u[0])


def l1_slots():
    out, now = [], 0.0

    def add(cost, *stage):
        nonlocal now
        out.append((now, stage))
        now += cost

    add(1.0, "xT")
    add(1.0, "xTe")
    add(2.5, "gates")
    for d in range(1, E):
        add(0.7, "rank", d)
    add(2.5, "sig")

    def att(a):
        for t in range(NT):
            if a == H * t + Z_LAG + 1:
                add(0.0, "ze", t)
        add(1.8, "att", a)
        for t in range(NT):
            if a == H * t + T_LAG:
                add(0.5, "turn", t)
        for t in range(NT):
            if a == H * t + Z_LAG:
                add(0.5, "z", t)
            if a == H * t + F_LAG:
                add(0.5, "fin", t)

    for n in range(NCHUNK + S_LAG):
        add(1.0, "chunk", n)
        if n == 4:
            add(0.5, "state")
        if n >= NCHUNK - 2:
            att(n - NCHUNK + 2)
    for a in range(S_LAG + 2, NATT - H + F_LAG + 1):
        att(a)
    return out


def first_stages():
    l0 = [u for _, u in l0_slots()]
    early = [(2.0, "dd"), (3.0, "tanh"), (5.0, "lerp"), (7.5, "vr"), (8.5, "vre"), (11.0, "lerp2"), (14.0, "kw"),
             (15.0, "kwe"), (20.0, "g")]
    timed = [(when, ("l0", u)) for when, u in early]
    end = 1.0 + 1.6 * ROUNDS_Q
    timed += [(1.0 + 1.6 * k, ("p", "round", k)) for k in range(ROUNDS_Q)] + [(end, ("p", "picked"))]
    timed += [(2.8 * (k - 1), ("p", "fold", k)) for k in range(2 * G)]
    timed += [(2.8 * (k - 1) + 1.5, ("p", "foldc", k)) for k in range(2 * G)]
    timed += [(1.9, ("p", "xT")), (end + 1.0, ("p", "nulls"))]
    out = [u for _, u in sorted(timed, key=lambda u: u[0])]
    after = {("gqe",): 0, ("gke",): 1, ("axe", 0): 2, ("axe", 1): 3, ("axe", 2): 4, ("axe", 3): 5, ("se", 3): 6, ("soft", 0): 7}
    for u in l0:
        if ("l0",) + u not in out:
            out.append(("l0",) + u)
        if u in after:
            k = 2 * G + after[u]
            out += [("p", "foldc", k - 1)] * (k > 2 * G) + [("p", "fold", k)]
        if u == ("soft", 1):
            out += [("p", "foldc", 4 * G - 1), ("p", "scan_weights")]
    return out


LAST_TURN = dict((s, when) for when, s in l1_slots())[("turn", NT - 1)]
LAST_FIN = dict((s, when) for when, s in l1_slots())[("fin", NT - 2)]


def layers(nc, x, ddw, mixes, projw, gnw, gnb, qkr, wqn, wkn, wvn, won, nkT, nvT, null_token,
           winT, winT8, wcat, wg, wg8, bin_, bin8, bg, wout, wout9, wqkv, wsd, wor, out):
    ctx = ExitStack()
    with ctx:
        def sb(name, shape, dt=F32):
            return ctx.enter_context(nc.sbuf_tensor(name, shape, dt))

        def sem(name):
            return ctx.enter_context(nc.semaphore(name))

        xn_d = nc.dram_tensor("xn_scratch", (B, P, NT * D), F32, kind="Internal").ap()
        xT_d = nc.dram_tensor("xT_scratch", (B + 1, P, T), F32, kind="Internal").ap()
        posT_d = nc.dram_tensor("posT_scratch", (B, P, NT * 2 * G), F32, kind="Internal").ap()
        pos_d = nc.dram_tensor("pos_scratch", (B, G * T), F32, kind="Internal").ap()
        v_d = nc.dram_tensor("v_scratch", (D, T), F32, kind="Internal").ap()
        r_d = nc.dram_tensor("r_scratch", (D, T), F32, kind="Internal").ap()

        ST_ROWS, LAST_ROWS = slice(DH, DH + SD), slice(DH, DH + SD + 1)

        ident = sb("ident", [P, P])
        iota1 = sb("iota1", [P, P])
        iotac = sb("iotac", [P, 1])
        ddw_s = sb("ddw_s", [P, D])
        mix_s = sb("mix_s", [P, 5])
        projw_s = sb("projw_s", [P, 5, D])
        oww_s = sb("oww_s", [P, D])
        gnw_s = sb("gnw_s", [P, D])
        gnb_s = sb("gnb_s", [P, D])
        null_s = sb("null_s", [P, D])
        qkr_s = sb("qkr_s", [P, 2 * G])
        A_s = sb("A_s", [P, G, 2, HP, P])
        M_s = sb("M_s", [P, G, 2, HP, P])
        u9_s = sb("u9_s", [P, G, H + 1])
        nvw_s = sb("nvw_s", [G * H, G, D])
        wqkv_s = sb("wqkv_s", [P, KINDS, E, CW])
        wsd_s = sb("wsd_s", [P, 2 * H * E])
        wst_s = sb("wst_s", [P, GT_ROW + SD])
        wsi_s, wgt_s = wst_s[:, DH:DH + SD], wst_s[:, GT_ROW:GT_ROW + SD]
        wfold_s = sb("wfold_s", [P, D])
        wor_s = sb("wor_s", [P, 3, D])
        bsi_s = sb("bsi_s", [P, 1])[ST_ROWS]
        bgt_s = sb("bgt_s", [P, 1])[ST_ROWS]
        rank0 = sb("rank0", [P, E])

        xr = sb("xr", [P, NT, D])
        xn = sb("xn", [P, NT, D])
        xTp = sb("xTp", [P, T + 1])
        dif = sb("dif", [P, T])
        th = sb("th", [P, T])
        aa = sb("aa", [P, T])
        lp = sb("lp", [P, 2, T])
        kf = sb("kf", [P, T])
        dec = sb("dec", [P, T])
        silu = dif
        vb = sb("vb", [P, 2, 2, T])
        rb = sb("rb", [P, 2, 2, T])
        vf = vb[:, 1, 0, :]
        rf = rb[:, 1, 0, :]
        sel = sb("sel", [P, G * H * NKEY])
        skeys = sel[:, 0:G * H * NK].rearrange("p (n k) -> p n k", k=NK)
        snull = sel[:, G * H * NK:G * H * NKEY]
        selT = sb("selT", [P, G, T])
        posT = sb("posT", [P, NT, 2, G])
        xq = sb("xq", [P, G * NQ])
        xk = sb("xk", [P, G * NK])
        ax = sb("ax", [P, 2, H * NK])
        pt0 = sb("pt0", [P, 2, HP, NQ])
        vw = sb("vw", [P, 2, HP, D])
        ptn = sb("ptn", [G * H, NQ])
        ob = aa[:, :].rearrange("p (g d) -> p g d", g=G)
        sm = sb("sm", [P, G * (H + 1) + G])
        smt = sb("smt", [P, G * (H + 1) + G])
        hmax = sb("hmax", [P, G * H])
        hsum = sb("hsum", [P, G * H])
        mu = sb("mu", [P, NT * AH])
        va = sb("va", [P, NT * AH])
        ya = sb("ya", [P, NT * AH])
        wa = sb("wa", [P, NT * AH])
        cnt4 = sb("cnt4", [P, NT, G])
        cnt = sb("cnt", [P, NT])
        rcnt = sb("rcnt", [P, NT])
        nz = sb("nz", [P, NT])

        x1 = sb("x1", [P, NT, D])
        xn2 = sb("xn2", [P, NT, D])
        x2T = sb("x2T", [P, T])
        zg = sb("zg", [P, NT * 2 * H * E])
        sg = sb("sg", [P, NT * 2 * H * E])
        wins = sb("wins", [P, NT * 2 * H * E])
        yg = sb("yg", [P, E * CW])
        qk = sb("qk", [P, 2, HP, T])
        vv = sb("vv", [P, NT, CW])
        pr = sb("pr", [P, 3, T])
        beat = pr[:, 1:3, :].rearrange("p a b -> p (a b)")
        pt = sb("pt", [P, 3, NT, P])
        oo = sb("oo", [P, 2, CW])
        zT = sb("zT", [P, 2, P])
        nmax = sb("nmax", [P, NATT])
        den = sb("den", [P, NATT])
        rden = sb("rden", [P, NATT])
        zst = sb("zst", [DH + SD + 1, T])
        stats = sb("stats", [P, 4 * B, 6])
        mv = sb("mv", [P, 4 * B, 2])
        lv = sb("lv", [P, 4 * B])
        ly = sb("ly", [P, 4 * B])
        lw = sb("lw", [P, 4 * B])

        MAGIC = 0x5F3759DF

        bank = [ctx.enter_context(nc.psum_tensor(f"bank{k}", [P, 512], F32)) for k in range(8)]

        it_end = sem("it_end")
        it_go = sem("it_go")

        out_sent = sem("out_sent")

        step_sems = []

        def ssem(name):
            s = sem(name)
            step_sems.append(s)
            return s

        p_ld = ssem("p_ld"); p_ldx = [ssem(f"p_ldx{k}") for k in range(2)]; p_ldw = ssem("p_ldw"); p_cst = ssem("p_cst")
        p_bn = ssem("p_bn"); p_nt = ssem("p_nt"); p_xn = ssem("p_xn"); p_wr = ssem("p_wr")
        p_fill = ssem("p_fill"); p_act = ssem("p_act"); p_dve = ssem("p_dve")
        p_top = ssem("p_top"); p_pos = ssem("p_pos"); p_posT = ssem("p_posT"); p_zero = ssem("p_zero")
        p_blk = ssem("p_blk"); p_log = ssem("p_log"); p_st = [ssem(f"p_st{s}") for s in range(2)]
        p_ld2 = ssem("p_ld2"); p_ldm = ssem("p_ldm"); ld_xT = ssem("ld_xT")
        ld_x = ssem("ld_x"); ld_xn = ssem("ld_xn"); x1_free = ssem("x1_free"); next_xT = ssem("next_xT")
        ld_posT = ssem("ld_posT"); ld_pos = ssem("ld_pos")
        dif_ready = ssem("dif_ready"); th_done = ssem("th_done"); e_done = ssem("e_done")
        af_ready = ssem("af_ready"); mixed = ssem("mixed"); lerp_ready = ssem("lerp_ready")
        r_fill = ssem("r_fill"); r_act = ssem("r_act"); r_dve = ssem("r_dve")
        yT_fill = ssem("yT_fill"); yT_read = ssem("yT_read"); att_fill = ssem("att_fill")
        vr_sent = ssem("vr_sent"); tg_done = ssem("tg_done"); dec_ready = ssem("dec_ready")
        vb_in = [ssem(f"vb_in{s}") for s in range(2)]
        rb_in = [ssem(f"rb_in{s}") for s in range(2)]
        kv_done = ssem("kv_done"); scan_done = ssem("scan_done"); prod_done = ssem("prod_done")
        ot_done = ssem("ot_done")
        sel_ready = ssem("sel_ready"); selT_ready = ssem("selT_ready")
        smt_done = ssem("smt_done"); sig_ready = ssem("sig_ready")
        soft = ssem("soft"); e0_done = ssem("e0_done"); p0_ready = ssem("p0_ready")
        gn = ssem("gn"); sq_done = ssem("sq_done"); gnp = ssem("gnp"); y_ready = ssem("y_ready")
        cnt_s = ssem("cnt_s"); base_s = ssem("base_s"); x0_new = ssem("x0_new"); x1_new = ssem("x1_new")
        x1_copied = ssem("x1_copied"); ln_s = ssem("ln_s")
        t_fill = ssem("t_fill"); t_act = ssem("t_act"); t_dve = ssem("t_dve")
        y_fill = ssem("y_fill"); y_act = ssem("y_act"); y_dve = ssem("y_dve")
        si_read = ssem("si_read")
        o_read = ssem("o_read")
        ex_s = ssem("ex_s"); rank_s = ssem("rank_s"); sig_s = ssem("sig_s"); gt_read = ssem("gt_read"); gates_ready = ssem("gates_ready")
        sc_s = ssem("sc_s"); st_ready = ssem("st_ready")
        sum_add = ssem("sum_add"); q_add = ssem("q_add"); max_done = ssem("max_done"); rden_s = ssem("rden_s")
        tr_part = ssem("tr_part"); half_add = ssem("half_add"); zm_dve = ssem("zm_dve"); pv_done = ssem("pv_done")
        zm_ready = ssem("zm_ready"); zt_done = ssem("zt_done")
        lo_sem, hi_sem = step_sems[0].num, step_sems[-1].num
        assert [s.num for s in step_sems] == list(range(lo_sem, hi_sem + 1)), [s.num for s in step_sems]

        p_units = [(f"xT{b}", "act") for b in range(B)]
        p_units += [(f"fold{k}", "act") for k in range(2 * G)] + [("u", "act")]
        p_units += [(f"fold{k}", "act") for k in range(2 * G, 4 * G)] + [("nvw", "act"), ("wf", "act"), ("ws9", "act"), ("wmisc", "dve")]
        PB = Banks(bank[0:4], p_fill, {"act": p_act, "dve": p_dve}, p_units)
        LG = bank[4]

        r_units = [("dd", "act"), ("v", "act"), ("r", "act"), ("k", "act"), ("w", "act"), ("g", "dve"),
                   ("gq", "act"), ("gk", "act"), ("small", "dve")]
        for g in range(G):
            r_units += [(f"ax{g}", "act"), (f"s{g}", "dve")]
        r_units += [("ptn", "act")]
        for g in range(G):
            r_units += [(f"pt{g}", "act"), (f"vw{g}", "dve"), (f"o{g}", "act")]
        r_units += [("scat", "dve")]
        RB = Banks(bank[5:7], r_fill, {"act": r_act, "dve": r_dve}, r_units)
        NBK = bank[7]

        t_units = [("xT", "act"), ("gates", "dve"), ("si", "si")]
        y_units = []
        for _, s in l1_slots():
            k = s[1] if len(s) > 1 else None
            if s[0] == "chunk" and k < NCHUNK:
                y_units.append((f"y{k}", "dve", k % 3 if k + 1 < NCHUNK else 0))
            if s[0] == "chunk" and 0 <= k - Q_LAG < NCHUNK and chunk_kind(k - Q_LAG)[1:] == (QUERY, E - 1):
                t_units.append((f"q{chunk_kind(k - Q_LAG)[0]}", "act", 0))
            if s[0] == "chunk" and 0 <= k - K_LAG < NCHUNK and chunk_kind(k - K_LAG)[1:] == (KEY, E - 1):
                t_units.append((f"k{chunk_kind(k - K_LAG)[0]}", "act", 1))
            if s[0] == "att" and k < NATT:
                y_units.append((f"s{k}", "act", k % 2 if k > 0 else 2))
            if s[0] == "att" and 0 <= k - PT_LAG < NATT:
                t_units.append((f"pt{k - PT_LAG}", "act"))
            if s[0] == "turn":
                t_units.append((f"o{k}", "dve"))
            if s[0] == "z":
                t_units.append((f"z{k}", "act"))
            if s[0] == "fin":
                t_units.append((f"f{k}", "dve"))
        TB = Banks(bank[2:4], t_fill, {"act": t_act, "dve": t_dve, "si": si_read}, t_units)
        YB = Banks([bank[0], bank[1], bank[4]], y_fill, {"act": y_act, "dve": y_dve}, y_units)
        OBK = bank[4]

        def q_before(c):
            return sum(1 for k in range(c) if chunk_kind(k)[1] == QUERY)

        def takes_before(c):
            return sum(1 for k in range(c) if chunk_kind(k)[1] == QUERY and chunk_kind(k)[2] in TAKES)

        def adds_before(c):
            return sum(1 for k in range(c) if chunk_kind(k)[1] != QUERY and chunk_kind(k)[2] > 0)

        def gated(c):
            t, kind, e = chunk_kind(c)
            if kind == QUERY:
                s = q_before(c) % 3
                return yg[:, s * CW:(s + 1) * CW]
            if e == 0:
                return k_or_v_sum(t, kind)
            s = adds_before(c) % 3
            return pr[:, 2, :] if s == 2 else yg[:, (3 + s) * CW:(4 + s) * CW]

        def k_or_v_sum(t, kind):
            return oo[:, t % 2, :] if kind == KEY else vv[:, t, :]

        stage = {}
        stage["wq"] = qk[:, :, :, :].rearrange("p a b c -> p (a b c)")[:, 0:2048].rearrange("p (g c f) -> p g c f", g=G, c=HP)
        stage["wk"] = qk[:, :, :, :].rearrange("p a b c -> p (a b c)")[:, 2048:4096].rearrange("p (g c f) -> p g c f", g=G, c=HP)
        stage["wv"] = vv[:, :, :].rearrange("p a b -> p (a b)").rearrange("p (g c f) -> p g c f", g=G, c=HP)
        stage["wo"] = yg[:, 0:2048].rearrange("p (g c f) -> p g c f", g=G, c=HP)
        nkt = rden[:, 0:16].rearrange("p (g c) -> p g c", g=G)
        nvt = rden[:, 16:32].rearrange("p (g c) -> p g c", g=G)
        nkb = den[:, 0:32].rearrange("p (g c a) -> p g c a", g=G, c=HP)
        nvb = pr[:, 0, :].rearrange("p (g n) -> p g n", g=G)
        xa = vb[:, :, :, :].rearrange("p a b c -> p (a b c)")
        xb = rb[:, :, :, :].rearrange("p a b c -> p (a b c)")
        xt_ev = ax
        wr_pad = lp[:, :, :].rearrange("p a b -> p (a b)")[:, 0:B * 64].rearrange("p (b n) -> p b n", b=B)
        lgw, msk, onesr = (pt[0:64, k, :, :].rearrange("p a b -> p (a b)") for k in range(3))
        cum = oo[0:64, 0, :]
        top8 = hmax[0:64, 0:8]
        posTb = x1[:, :, :].rearrange("p a b -> p (a b)")[:, 0:B * NT * 2 * G].rearrange("p (b t k g) -> p b t k g", b=B, t=NT, k=2)
        winT_s = x2T[:, 0:P]
        winT8_s = x2T[0:SD, P:2 * P]
        wg_s = x2T[:, 256:256 + SD]
        wg8_s = x2T[0:SD, 264:264 + SD]
        bin_s = x2T[:, 272:273]
        bin8_s = x2T[0:SD, 273:274]
        bg_s = x2T[ST_ROWS, 274:275]
        bcol9 = x2T[:, 275:275 + SD + 1]
        wout_s = xn2[:, 0, :]
        wout9_s = xn2[0:SD + 1, 1, :]

        block = ctx.enter_context(nc.Block())

        def newton(eng, y, v, w, n, sem_, base):
            newton_start(eng, y, v, w, n, sem_, base)
            for k in range(3):
                newton_step(eng, y, v, w, n, sem_, base, k)
            return base + NEWTON

        def newton_start(eng, y, v, w, n, sem_, base):
            eng.tensor_scalar(w[:, 0:n].bitcast(I32), v[:, 0:n].bitcast(I32), 1, None,
                              ALU.logical_shift_right).then_inc(sem_, 1)
            eng.wait_ge(sem_, base + 1)
            eng.tensor_scalar(y[:, 0:n].bitcast(I32), w[:, 0:n].bitcast(I32), -1.0, float(MAGIC),
                              ALU.mult, ALU.add).then_inc(sem_, 1)
            eng.wait_ge(sem_, base + 2)

        def newton_step(eng, y, v, w, n, sem_, base, k):
            eng.scalar_tensor_tensor(out=w[:, 0:n], in0=y[:, 0:n], scalar=-0.5, in1=y[:, 0:n],
                                     op0=ALU.mult, op1=ALU.mult).then_inc(sem_, 1)
            eng.wait_ge(sem_, base + 3 * k + 3)
            eng.tensor_tensor(w[:, 0:n], w[:, 0:n], v[:, 0:n], ALU.mult).then_inc(sem_, 1)
            eng.wait_ge(sem_, base + 3 * k + 4)
            eng.scalar_tensor_tensor(out=y[:, 0:n], in0=w[:, 0:n], scalar=1.5, in1=y[:, 0:n],
                                     op0=ALU.add, op1=ALU.mult).then_inc(sem_, 1)
            eng.wait_ge(sem_, base + 3 * k + 5)

        NEWTON = 11

        def step_over(eng, n):
            eng.drain().then_inc(it_end, 1)
            eng.wait_ge(it_go, n)

        def masked(eng, t, half, done):
            hs = slice(half * HALF, (half + 1) * HALF)
            m4 = wins[:, :].rearrange("p (t k h e) -> p t k h e", t=NT, k=2, h=H)[:, t, 1, hs, :]
            eng.tensor_tensor(
                yg[:, :].rearrange("p (h e d) -> p h e d", h=H, e=E)[:, hs],
                oo[:, 0, :].rearrange("p (h d) -> p h d", h=H)[:, hs].unsqueeze(2).broadcast_to((P, HALF, E, DH)),
                m4.unsqueeze(3).broadcast_to((P, HALF, E, DH)), ALU.mult).then_inc(done, 1)

        def run(stages, names):
            for s in names:
                f = stages.get(s[0:2])
                if f is not None:
                    f(*s[2:])

        first = [(when, ("l0",) + s) for when, s in l0_slots()]
        second = [(when, ("l1",) + s) for when, s in l1_slots()]
        FIRST = first_stages()
        L1 = [s for _, s in second]
        BODY = [s for _, s in sorted(first + second, key=lambda u: u[0])]

        @block.sync
        def _(sp):
            sp.dma_start(qkr_s[:, :], qkr).then_inc(p_ldw, 16)
            for b in range(B):
                src, k = (xa, b) if b < 4 else (xb, b - 4)
                sp.dma_start(src[:, k * T:(k + 1) * T].rearrange("p (t d) -> p t d", t=NT),
                             x[b].rearrange("(t p) d -> p t d", p=P)).then_inc(p_ldx[b * 2 // B], 16)
            loads = [(stage["wq"], wqn), (stage["wk"], wkn), (stage["wv"], wvn), (stage["wo"], won),
                     (nkt, nkT), (nvt, nvT), (winT_s, winT), (winT8_s, winT8), (wg_s, wg), (wg8_s, wg8),
                     (bin_s, bin_), (bin8_s, bin8), (bg_s, bg), (wout_s, wout), (wout9_s, wout9),
                     (bsi_s[:, :], bin8), (gnw_s[:, :], gnw.partition_broadcast(P)), (gnb_s[:, :], gnb.partition_broadcast(P))]
            loads_m = [(ddw_s[:, :], ddw), (mix_s[:, :], mixes), (projw_s[:, :, :], projw[:, 0:5, :]),
                       (oww_s[:, :], projw[:, 5, :]), (null_s[:, :], null_token.partition_broadcast(P))]
            loads2 = [(wsi_s, wcat), (wqkv_s[:, :, :, :], wqkv), (wsd_s[:, :], wsd), (wor_s[:, 0:2, :], wor[0:2].rearrange("c p m -> p c m")),
                     (wor_s[0:DH, 2, :], wor[2, 0:DH])]
            for dst, src in loads_m:
                sp.dma_start(dst, src, allow_slow_non_contiguous=True).then_inc(p_ldm, 16)
            for dst, src in loads:
                sp.dma_start(dst, src, allow_slow_non_contiguous=True).then_inc(p_ld, 16)
            assert len(loads) == N_LOADS and len(loads_m) == N_LOADS_M
            for b in range(B):
                src, k = (xa, b) if b < 4 else (xb, b - 4)
                sp.wait_ge(p_xn, NT * (b + 1))
                sp.dma_start(xn_d[b], src[:, k * T:(k + 1) * T]).then_inc(p_wr, 16)
                sp.wait_ge(p_act, PB.was_read(f"xT{b}")[1])
                sp.dma_start(xT_d[b], xt_ev[:, b % 2, :]).then_inc(p_st[b % 2], 16)
                if b == 0:
                    sp.dma_start(xT_d[B], xt_ev[:, 0, :]).then_inc(p_st[0], 16)
            sp.wait_ge(p_wr, 16 * B)
            sp.wait_ge(p_st[0], 16 * (B // 2 + 1))
            sp.wait_ge(p_st[1], 16 * B // 2)
            sp.dma_start(xTp[:, 1:T + 1], xT_d[0]).then_inc(ld_xT, 16)
            for dst, src in loads2:
                sp.dma_start(dst, src, allow_slow_non_contiguous=True).then_inc(p_ld2, 16)

            def p_picked():
                sp.wait_ge(p_pos, 1)
                sp.dma_start(pos_d.rearrange("b (g t) -> (b g) t", g=G), cum[0:B * G, :]).then_inc(p_wr, 16)
                sp.wait_ge(p_pos, 2)
                sp.dma_start(posT_d.rearrange("b p n -> p b n"),
                             posTb.rearrange("p b t k g -> p b (t k g)")).then_inc(p_wr, 16)
                sp.wait_ge(p_wr, 16 * (B + 2))
                load()

            def next_step():
                sp.wait_ge(it_end, 4)
                sp.sem_clear(range(lo_sem, hi_sem + 1))
                sp.sem_clear(it_end)
                sp.sem_inc(it_go, 1)

            def stages_of(l0_b, l1_b):
                def l0_load():
                    one = bass.ds(l0_b, 1)
                    sp.dma_start(xn[:, :, :].rearrange("p t d -> p (t d)"),
                                 xn_d[one].rearrange("a p t -> (a p) t")).then_inc(ld_xn, 16)
                    sp.dma_start(posT[:, :, :, :].rearrange("p t k g -> p (t k g)"),
                                 posT_d[one].rearrange("a p n -> (a p) n")).then_inc(ld_posT, 16)
                    sp.dma_start(selT[:, :, :].rearrange("p g t -> p (g t)"),
                                 pos_d[one].broadcast_to((P, G * T))).then_inc(ld_pos, 16)
                    if l1_b is not None:
                        x1_frees()
                        sp.wait_ge(x1_copied, 1)
                    sp.dma_start(xr[:, :, :], x[one].rearrange("a (t p) d -> p (a t) d", p=P)).then_inc(ld_x, 16)

                def l0_kwe():
                    sp.wait_ge(af_ready, 2)
                    sp.wait_ge(dif_ready, 1)
                    sp.wait_ge(*RB.filled("dd"))
                    sp.dma_start(xTp[:, 1:T + 1], xT_d[bass.ds(l0_b + 1, 1)].rearrange("a p t -> (a p) t")).then_inc(next_xT, 16)

                def pair(dst, src, q, s):
                    two = src.rearrange("(h q j) t -> q h (j t)", q=NPAIR, j=2)[q]
                    sp.dma_start(dst[:, q % 2, :, :].rearrange("p j t -> p (j t)"),
                                 two.unsqueeze(1).broadcast_to((AH, ADH, 2 * T))).then_inc(s[q % 2], 16)

                def l0_vre():
                    sp.wait_ge(*RB.was_read("v"))
                    sp.dma_start(v_d, vf).then_inc(vr_sent, 16)
                    sp.wait_ge(*RB.was_read("r"))
                    sp.dma_start(r_d, rf).then_inc(vr_sent, 16)
                    sp.wait_ge(vr_sent, 32)
                    for q in range(2):
                        pair(vb, v_d, q, vb_in)
                        pair(rb, r_d, q, rb_in)

                def l0_wsum(q):
                    if q + 2 < NPAIR:
                        sp.wait_ge(ot_done, q + 1)
                        pair(vb, v_d, q + 2, vb_in)
                        pair(rb, r_d, q + 2, rb_in)

                def l1_store():
                    sp.wait_ge(*TB.was_read(f"f{NT - 1}"))
                    sp.dma_start(out[bass.ds(l1_b, 1)].rearrange("a (t p) d -> p (a t) d", p=P),
                                 x1[:, :, :]).then_inc(out_sent, 16)
                return l0_load, {("l0", "vre"): l0_vre, ("l0", "kwe"): l0_kwe, ("l0", "wsum"): l0_wsum}, l1_store

            def x1_frees():
                sp.wait_ge(out_sent, 16)
                sp.sem_clear(out_sent)
                sp.sem_inc(x1_free, 1)

            load, st, _ = stages_of(0, None)
            run({**st, ("p", "picked"): p_picked}, FIRST)
            sp.wait_ge(next_xT, 16)
            sp.wait_ge(p_ld2, 16 * len(loads2))
            next_step()
            sp.sem_inc(out_sent, 16)
            with sp.Fori(0, B - 1) as i:
                load, st, store = stages_of(i + 1, i)
                load()
                run(st, BODY)
                store()
                sp.wait_ge(next_xT, 16)
                next_step()
            _, st, store = stages_of(None, B - 1)
            x1_frees()
            store()
            sp.wait_ge(out_sent, 16)

        @block.gpsimd
        def _(gp):
            gp.memset(ident[:, :], 0.0).then_inc(p_cst, 1)
            gp.wait_ge(p_cst, 1)
            gp.affine_select(out=ident[:, :], in_=ident[:, :], compare_op=ALU.not_equal, fill=1.0, base=0,
                             pattern=[[-1, P]], channel_multiplier=1).then_inc(p_cst, 1)
            gp.iota(iota1[:, :], [[1, P]], base=1, channel_multiplier=0,
                    allow_small_or_imprecise_dtypes=True).then_inc(p_cst, 1)
            gp.iota(iotac[:, :], [[1, 1]], base=1, channel_multiplier=1,
                    allow_small_or_imprecise_dtypes=True).then_inc(p_cst, 1)
            gp.iota(rank0[:, :], [[1, E]], base=0, channel_multiplier=0,
                    allow_small_or_imprecise_dtypes=True).then_inc(p_cst, 1)
            gp.memset(xTp[:, 0:1], 0.0).then_inc(p_cst, 1)
            gp.memset(dec[:, 0:1], 0.0).then_inc(p_cst, 1)
            gp.wait_ge(p_cst, 7)
            gp.memset(zst[LAST_ROWS, :], 1.0).then_inc(p_cst, 1)
            gp.wait_ge(p_cst, 8)
            gp.memset(wst_s[:, 0:DH], 0.0).then_inc(p_cst, 1)
            gp.memset(wst_s[:, DH + SD:GT_ROW], 0.0).then_inc(p_cst, 1)
            gp.memset(onesr, 1.0).then_inc(p_cst, 1)
            gp.wait_ge(p_cst, 11)
            gp.wait_ge(p_blk, 4)
            gp.wait_ge(p_ldm, 16 * N_LOADS_M)

            def p_xT():
                gp.wait_ge(ld_xT, 16)


            def l0_dd():
                gp.tensor_tensor(dif[:, :], xTp[:, 1:T + 1], xTp[:, 0:T], ALU.subtract).then_inc(dif_ready, 1)

            def lerp(m):
                gp.wait_ge(mixed, m + 1)
                gp.tensor_tensor(lp[:, m % 2, :], lp[:, m % 2, :], aa[:, :], ALU.add).then_inc(lerp_ready, 1)

            def l0_lerp():
                for m in range(2):
                    lerp(m)

            def l0_lerp2():
                for m in range(2, 4):
                    lerp(m)

            def l0_kwe():
                lerp(4)

            def l0_kv(q):
                if q == 0:
                    gp.wait_ge(*RB.was_read("k"))
                gp.wait_ge(vb_in[q % 2], 16 * (q // 2 + 1))
                gp.tensor_tensor(vb[:, q % 2, :, :], vb[:, q % 2, :, :],
                                 kf[:, :].unsqueeze(1).broadcast_to((P, 2, T)), ALU.mult).then_inc(kv_done, 1)

            def l0_prod(q):
                gp.wait_ge(rb_in[q % 2], 16 * (q // 2 + 1))
                gp.wait_ge(scan_done, 2 * q + 2)
                gp.tensor_tensor(vb[:, q % 2, :, :], vb[:, q % 2, :, :], rb[:, q % 2, :, :], ALU.mult).then_inc(prod_done, 1)

            def l0_norm():
                gp.wait_ge(soft, 12)
                gp.tensor_tensor(skeys, skeys, hsum[:, :].unsqueeze(2).broadcast_to((P, G * H, NK)), ALU.mult)\
                  .then_inc(p0_ready, 1)
                gp.tensor_tensor(snull, snull, hsum[:, :], ALU.mult).then_inc(p0_ready, 1)

            def l0_gnsq():
                gp.wait_ge(gn, 2)
                gp.tensor_tensor(lp[:, 0, :], th[:, :], th[:, :], ALU.mult).then_inc(sq_done, 1)

            def l0_gn3():
                gp.wait_ge(gn, 5 + NEWTON)
                c = th[:, :].rearrange("p (t d) -> p t d", t=NT)
                gp.tensor_tensor(c, c, gnw_s[:, :].unsqueeze(1).broadcast_to((P, NT, D)), ALU.mult).then_inc(gnp, 1)
                gp.wait_ge(gnp, 1)
                gp.tensor_tensor(c, c, gnb_s[:, :].unsqueeze(1).broadcast_to((P, NT, D)), ALU.add).then_inc(gnp, 1)
                gp.wait_ge(gnp, 2)
                gp.wait_ge(*RB.was_read("g"))
                gp.tensor_tensor(th[:, :], th[:, :], silu[:, :], ALU.mult).then_inc(y_ready, 1)

            def l0_base():
                gp.wait_ge(cnt_s, 3)
                gp.wait_ge(ld_x, 16)
                gp.wait_ge(y_ready, 1)
                l3 = lp[:, 0, :].rearrange("p (t d) -> p t d", t=NT)
                gp.tensor_tensor(l3, null_s[:, :].unsqueeze(1).broadcast_to((P, NT, D)),
                                 nz[:, :].unsqueeze(2).broadcast_to((P, NT, D)), ALU.mult).then_inc(base_s, 1)
                gp.wait_ge(base_s, 1)
                gp.tensor_tensor(xr[:, :, :], xr[:, :, :], l3, ALU.add).then_inc(base_s, 1)

            def l1_chunk(n):
                c = n - S_LAG
                if not 0 <= c < NCHUNK:
                    return
                t, kind, e = chunk_kind(c)
                if kind != QUERY and e > 0:
                    gp.wait_ge(y_dve, YB.was_read(f"y{c}")[1])
                    if e > 1:
                        gp.wait_ge(sum_add, adds_before(c))
                    dst = k_or_v_sum(t, kind)
                    gp.tensor_tensor(dst, dst, gated(c), ALU.add).then_inc(sum_add, 1)

            def l1_att(a):
                t, r = divmod(a - M_LAG, H)
                if r == 0 and 0 <= t < NT:
                    gp.wait_ge(*TB.was_read(f"o{t}"))
                    if t > 0:
                        gp.wait_ge(*TB.filled(f"z{t - 1}"))
                    masked(gp, t, 0, zm_ready)
                    if t + 1 < NT:
                        masked(gp, t, 1, zm_ready)

            st = {("l0", "dd"): l0_dd, ("l0", "lerp"): l0_lerp, ("l0", "lerp2"): l0_lerp2, ("l0", "kwe"): l0_kwe,
                  ("l0", "kv"): l0_kv, ("l0", "prod"): l0_prod, ("l0", "norm"): l0_norm,
                  ("l0", "gnsq"): l0_gnsq, ("l0", "gn3"): l0_gn3, ("l0", "base"): l0_base,
                  ("l1", "chunk"): l1_chunk, ("l1", "att"): l1_att}
            run({**st, ("p", "xT"): p_xT}, FIRST)
            step_over(gp, 1)
            with gp.Fori(0, B - 1) as i:
                run(st, BODY)
                step_over(gp, i + 2)
            run(st, L1)

        @block.scalar
        def _(act):
            act.preload_act_table_set("exp_and_others")
            for b in range(B):
                act.wait_ge(*PB.filled(f"xT{b}"))
                if b >= 2:
                    act.wait_ge(p_st[b % 2], 16 * (b // 2 + (b % 2 == 0)))
                    act.wait_ge(p_log, b - 1)
                act.activation(xt_ev[:, b % 2, :], PB.bank(f"xT{b}")[:, :], ACT.Copy).then_inc(p_act, 1)
            def p_foldc(k):
                act.wait_ge(*PB.filled(f"fold{k}"))
                g, hp = k // 2 % G, k % 2
                dst, scale = (A_s, SCALE) if k < 2 * G else (M_s, 1.0)
                act.activation(dst[:, g, hp, :, :].rearrange("p a b -> p (a b)"), PB.bank(f"fold{k}")[:, :],
                               ACT.Copy, scale=scale).then_inc(p_act, 1)

            def p_nulls():
                act.wait_ge(*PB.filled("u"))
                act.activation(u9_s[:, :, 0:H], PB.bank("u")[:, 0:G * H].rearrange("p (g h) -> p g h", g=G),
                               ACT.Copy, scale=SCALE).then_inc(p_act, 1)

            def p_scan_weights():
                act.wait_ge(*PB.filled("nvw"))
                act.activation(nvw_s[:, :, :].rearrange("p g d -> p (g d)"), PB.bank("nvw")[0:G * H, :], ACT.Copy).then_inc(p_act, 1)
                act.wait_ge(*PB.filled("wf"))
                act.activation(wfold_s[:, :], PB.bank("wf")[:, 0:D], ACT.Copy).then_inc(p_act, 1)
                act.wait_ge(*PB.filled("ws9"))
                act.activation(wor_s[LAST_ROWS, 2, :], PB.bank("ws9")[LAST_ROWS, 0:D], ACT.Copy).then_inc(p_act, 1)

            act.wait_ge(p_ldm, 16 * N_LOADS_M)

            def copy(unit, banks, dst, src, scale=1.0):
                act.wait_ge(*banks.filled(unit))
                act.activation(dst, src, ACT.Copy, scale=scale).then_inc(banks.free_sem(unit), 1)

            def l0_tanh():
                act.wait_ge(*RB.filled("dd"))
                act.activation(th[:, :], RB.bank("dd")[:, :], ACT.Tanh).then_inc(r_act, 1)
                act.wait_ge(r_act, 1)
                act.activation(th[:, :], th[:, :], ACT.Tanh, scale=0.5).then_inc(th_done, 1)

            def mix(m):
                act.activation(lp[:, m % 2, :], dif[:, :], ACT.Copy, scale=mix_s[:, m:m + 1]).then_inc(mixed, 1)

            def l0_lerp():
                act.wait_ge(af_ready, 2)
                for m in range(2):
                    mix(m)

            def l0_lerp2():
                for m in range(2, 4):
                    act.wait_ge(*RB.filled("vr"[m - 2]))
                    mix(m)

            def l0_vre():
                copy("v", RB, vf, RB.bank("v")[:, :])
                copy("r", RB, rf, RB.bank("r")[:, :])

            def l0_kwe():
                act.wait_ge(*RB.filled("k"))
                mix(4)
                copy("k", RB, kf[:, :], RB.bank("k")[:, :])
                act.wait_ge(*RB.filled("w"))
                act.activation(dec[:, 1:T], RB.bank("w")[:, 1:T], ACT.Tanh, scale=0.5).then_inc(r_act, 1)

            def l0_ge():
                act.wait_ge(*RB.filled("g"))
                act.activation(silu[:, :], RB.bank("g")[:, :], ACT.Tanh, scale=0.5).then_inc(tg_done, 1)

            def l0_gqe():
                copy("gq", RB, xq[:, :], RB.bank("gq")[:, :])

            def l0_gke():
                copy("gk", RB, xk[:, :], RB.bank("gk")[:, 0:G * NK])

            def l0_smalle():
                act.wait_ge(*RB.was_read("small"))
                act.activation(smt[:, :], sm[:, :], ACT.Tanh, scale=0.5).then_inc(smt_done, 1)

            def l0_axe(g):
                copy(f"ax{g}", RB, ax[:, g % 2, :], RB.bank(f"ax{g}")[:, :])

            def l0_exp():
                act.wait_ge(soft, 7)
                for cols in (slice(0, G * H * NK // 2), slice(G * H * NK // 2, G * H * NKEY)):
                    act.activation(sel[:, cols], sel[:, cols], ACT.Exp).then_inc(e0_done, 1)

            def l0_ptne():
                copy("ptn", RB, ptn[:, :], RB.bank("ptn")[0:G * H, 0:NQ])

            def l0_pte(g):
                copy(f"pt{g}", RB, pt0[:, g % 2, :, :].rearrange("p a b -> p (a b)"), RB.bank(f"pt{g}")[:, :])

            def l0_oe(g):
                copy(f"o{g}", RB, ob[:, g, :], RB.bank(f"o{g}")[:, 0:D])

            def l0_yTe():
                act.wait_ge(yT_fill, 1)
                act.activation(lp[:, 1, :], NBK[:, :], ACT.Copy).then_inc(yT_read, 1)

            def l1_xTe():
                copy("xT", TB, x2T[:, :], TB.bank("xT")[:, :])

            def l1_gates():
                act.wait_ge(*TB.was_read("gates"))
                act.activation(sg[:, :], zg[:, :], ACT.Exp, scale=-1.0).then_inc(ex_s, 1)
                act.wait_ge(*TB.filled("si"))
                act.activation(xn2[ST_ROWS, :, :].rearrange("p a b -> p (a b)"), TB.bank("si")[GT_ROW:GT_ROW + SD, :], ACT.Tanh,
                               bias=bgt_s[:, 0:1], scale=0.5).then_inc(gt_read, 1)
                act.wait_ge(x1_free, 1)
                act.activation(x1[:, :, :], xr[:, :, :], ACT.Copy).then_inc(x1_copied, 1)

            def l1_chunk(n):
                for kind, u, lag in ((QUERY, "q", Q_LAG), (KEY, "k", K_LAG)):
                    c = n - lag
                    if 0 <= c < NCHUNK and chunk_kind(c)[1:] == (kind, E - 1):
                        t = chunk_kind(c)[0]
                        copy(f"{u}{t}", TB, qk[:, kind, :, t * P:(t + 1) * P],
                             TB.bank(f"{u}{t}")[:, :].rearrange("p (c n) -> p c n", c=HP))

            def l1_att(a):
                n = a - PT_LAG
                if 0 <= n < NATT:
                    if n >= 3:
                        act.wait_ge(pv_done, (n - 3) // 2 + 1)
                    copy(f"pt{n}", TB, pt[:, n % 3, :, :].rearrange("p a b -> p (a b)"), TB.bank(f"pt{n}")[:, :])
                if a < NATT:
                    act.wait_ge(max_done, a + 1)
                    if a == 2:
                        act.wait_ge(sum_add, adds_before(NCHUNK))
                    if a >= 3:
                        act.wait_ge(*TB.filled(f"pt{a - 3}"))
                    act.activation(pr[:, a % 3, :], YB.bank(f"s{a}")[:, :], ACT.Exp, bias=nmax[:, a:a + 1],
                                   accum_out=den[:, a:a + 1]).then_inc(y_act, 1)

            def l1_ze(t):
                act.wait_ge(*TB.filled(f"z{t}"))
                act.activation(zT[:, 0:2, :].rearrange("p a b -> p (a b)"), TB.bank(f"z{t}")[:, 0:2 * P],
                               ACT.Copy).then_inc(zt_done, 1)
                act.activation(zst[0:DH, t * P:(t + 1) * P], TB.bank(f"z{t}")[0:DH, 2 * P:3 * P], ACT.Copy).then_inc(t_act, 1)

            st = {("l0", "tanh"): l0_tanh, ("l0", "lerp"): l0_lerp, ("l0", "lerp2"): l0_lerp2, ("l0", "vre"): l0_vre, ("l0", "kwe"): l0_kwe, ("l0", "ge"): l0_ge,
                  ("l0", "gqe"): l0_gqe, ("l0", "gke"): l0_gke, ("l0", "smalle"): l0_smalle, ("l0", "axe"): l0_axe,
                  ("l0", "exp"): l0_exp, ("l0", "ptne"): l0_ptne, ("l0", "pte"): l0_pte, ("l0", "oe"): l0_oe,
                  ("l0", "yTe"): l0_yTe, ("l1", "xTe"): l1_xTe, ("l1", "gates"): l1_gates,
                  ("l1", "chunk"): l1_chunk, ("l1", "att"): l1_att, ("l1", "ze"): l1_ze}
            run({**st, ("p", "foldc"): p_foldc, ("p", "nulls"): p_nulls, ("p", "scan_weights"): p_scan_weights}, FIRST)
            step_over(act, 1)
            with act.Fori(0, B - 1) as i:
                run(st, BODY)
                step_over(act, i + 2)
            run(st, L1)

        @block.tensor
        def _(pe):
            def open_(banks, unit):
                f = banks.free_for(unit)
                if f is not None:
                    pe.wait_ge(*f)
                return banks.bank(unit)

            def logits(b):
                pe.wait_ge(*PB.was_read(f"xT{b}"))
                pe.matmul(LG[0:64, :], wr_pad[:, b, :], xt_ev[:, b % 2, :], start=(b == 0), stop=(b == B - 1))\
                  .then_inc(p_log, 1)
            pe.wait_ge(p_blk, 1)
            pe.wait_ge(p_cst, 11)
            for b in range(B):
                bk = open_(PB, f"xT{b}")
                pe.wait_ge(p_xn, NT * (b + 1))
                src, k = (xa, b) if b < 4 else (xb, b - 4)
                for t in range(NT):
                    mm = pe.transpose(bk[:, t * P:(t + 1) * P], src[:, k * T + t * D:k * T + (t + 1) * D], ident[:, :])
                mm.then_inc(p_fill, 1)
                if b >= 1:
                    logits(b - 1)
            logits(B - 1)
            pe.wait_ge(p_ldm, 16 * N_LOADS_M)

            def p_xT():
                pe.wait_ge(ld_xT, 16)

            def p_fold(k):
                if k == 0:
                    pe.wait_ge(p_ld, 16 * N_LOADS)
                g = k // 2 % G
                bk = open_(PB, f"fold{k}")
                hp = slice(k % 2 * DH, k % 2 * DH + DH)
                l, r = (stage["wk"], stage["wq"]) if k < 2 * G else (stage["wv"], stage["wo"])
                for c in range(HP):
                    mm = pe.matmul(bk[:, c * P:(c + 1) * P], l[hp, g, c, :], r[hp, g, c, :], start=True, stop=True)
                mm.then_inc(p_fill, 1)

            def p_nulls():
                pe.wait_ge(p_blk, 4)
                bk = open_(PB, "u")
                for g in range(G):
                    for c in range(HP):
                        mm = pe.matmul(bk[:, g * H + 2 * c:g * H + 2 * c + 2], stage["wq"][:, g, c, :], nkb[:, g, c, :],
                                       start=True, stop=True)
                mm.then_inc(p_fill, 1)
                pe.wait_ge(*PB.was_read("u"))

            def p_scan_weights():
                bk = open_(PB, "nvw")
                for g in range(G):
                    for c in range(HP):
                        mm = pe.matmul(bk[0:G * H, g * D:(g + 1) * D], nvb[:, g, c * 32:(c + 1) * 32], stage["wo"][:, g, c, :],
                                       start=(c == 0), stop=(c == HP - 1))
                mm.then_inc(p_fill, 1)
                bk = open_(PB, "wf")
                pe.matmul(bk[:, 0:D], winT_s, wout_s, start=True, stop=True).then_inc(p_fill, 1)
                bk = open_(PB, "ws9")
                pe.matmul(bk[LAST_ROWS, 0:D], bcol9, wout_s, start=True, stop=False)
                pe.matmul(bk[LAST_ROWS, 0:D], ident[0:SD + 1, 0:SD + 1], wout9_s, start=False, stop=True).then_inc(p_fill, 1)
                bk = open_(PB, "wmisc")
                pe.matmul(bk[:, 0:SD], winT_s, wg_s, start=True, stop=False)
                pe.matmul(bk[:, 0:SD], winT8_s, wg8_s, start=False, stop=True)
                pe.matmul(bk[ST_ROWS, SD:SD + 1], wg_s, bin_s, start=True, stop=False)
                pe.matmul(bk[ST_ROWS, SD:SD + 1], wg8_s, bin8_s, start=False, stop=True).then_inc(p_fill, 1)

                pe.wait_ge(*PB.was_read("ws9"))

            def p_picked():
                pe.wait_ge(p_pos, 1)
                for t in range(NT):
                    mm = pe.transpose(LG[:, t * 64:(t + 1) * 64], cum[:, t * P:(t + 1) * P], ident[0:64, 0:64])
                mm.then_inc(p_posT, 1)

            def l0_dd():
                bk = open_(RB, "dd")
                pe.matmul(bk[:, :], ddw_s[:, :], xTp[:, 0:T], start=True, stop=True).then_inc(r_fill, 1)

            def project(m):
                bk = open_(RB, "vrkw"[m])
                pe.wait_ge(lerp_ready, m + 1)
                pe.matmul(bk[:, :], projw_s[:, m, :], lp[:, m % 2, :], start=True, stop=True).then_inc(r_fill, 1)

            def l0_vr():
                project(0)
                project(1)

            def l0_kw():
                project(2)
                project(3)

            def l0_g():
                bk = open_(RB, "g")
                pe.wait_ge(lerp_ready, 5)
                for t in range(NT):
                    mm = pe.matmul(bk[:, t * P:(t + 1) * P], lp[:, 0, t * P:(t + 1) * P], projw_s[:, 4, :],
                                   start=True, stop=True)
                mm.then_inc(r_fill, 1)

            def gather(n, u, w):
                bk = open_(RB, u)
                pe.wait_ge(sel_ready, n)
                for t in range(NT):
                    mm = pe.matmul(bk[:, 0:G * w], xn[:, t, :], sel[:, t * G * w:(t + 1) * G * w],
                                   start=(t == 0), stop=(t == NT - 1))
                mm.then_inc(r_fill, 1)

            def l0_gq():
                pe.wait_ge(ld_xn, 16)
                gather(2, "gq", NQ)

            def l0_gk():
                gather(3, "gk", NK)

            def l0_small():
                bk = open_(RB, "small")
                pe.wait_ge(*RB.was_read("gk"))
                for g in range(G):
                    n = G * (H + 1) + g
                    pe.matmul(bk[:, g * (H + 1):(g + 1) * (H + 1)], xq[:, g * NQ:(g + 1) * NQ], u9_s[:, g, :],
                              start=True, stop=True)
                    pe.matmul(bk[0:NK, n:n + 1], xk[:, g * NK:(g + 1) * NK], qkr_s[:, G + g:G + g + 1],
                              start=True, stop=True)
                    mm = pe.matmul(bk[NK:2 * NK, n:n + 1], xk[:, g * NK:(g + 1) * NK], qkr_s[:, G + g:G + g + 1],
                                   start=True, stop=True)
                mm.then_inc(r_fill, 1)

            def l0_ax(g):
                bk = open_(RB, f"ax{g}")
                for h in range(H):
                    mm = pe.matmul(bk[:, h * NK:(h + 1) * NK], A_s[:, g, h % 2, h // 2, :], xk[:, g * NK:(g + 1) * NK],
                                   start=True, stop=True)
                mm.then_inc(r_fill, 1)

            def l0_s(g):
                bk = open_(RB, f"s{g}")
                pe.wait_ge(*RB.was_read(f"ax{g}"))
                pe.matmul(bk[:, :], xq[:, g * NQ:(g + 1) * NQ], ax[:, g % 2, :], start=True, stop=True).then_inc(r_fill, 1)

            def l0_wsum(q):
                bk = NBK
                pe.wait_ge(prod_done, q + 1)
                for j in range(2):
                    for t in range(NT):
                        first, last = q == 0 and j == 0 and t == 0, q == NPAIR - 1 and j == 1
                        mm = pe.matmul(bk[:, t * P:(t + 1) * P], vb[:, q % 2, j, t * P:(t + 1) * P], ident[:, :],
                                       is_transpose=True, start=first, stop=last, skip_group_check=True)
                mm.then_inc(ot_done, 1)

            def l0_yT():
                pe.wait_ge(gn, 2)
                pe.wait_ge(y_ready, 1)
                for t in range(NT):
                    mm = pe.transpose(NBK[:, t * P:(t + 1) * P], th[:, t * P:(t + 1) * P], ident[:, :])
                mm.then_inc(yT_fill, 1)

            def l0_att():
                pe.wait_ge(yT_read, 1)
                for t in range(NT):
                    mm = pe.matmul(NBK[:, t * P:(t + 1) * P], lp[:, 1, t * P:(t + 1) * P], oww_s[:, :], start=True, stop=True)
                mm.then_inc(att_fill, 1)

            def l0_ptn():
                bk = open_(RB, "ptn")
                pe.wait_ge(p0_ready, 2)
                pe.transpose(bk[0:G * H, 0:NQ], snull, ident[:, :]).then_inc(r_fill, 1)

            def l0_pt(g):
                bk = open_(RB, f"pt{g}")
                for c in range(HP):
                    mm = pe.transpose(bk[:, c * NQ:(c + 1) * NQ], sel[:, (g * HP + c) * P:(g * HP + c + 1) * P], ident[:, :])
                mm.then_inc(r_fill, 1)

            def l0_vw(g):
                bk = open_(RB, f"vw{g}")
                for hp in range(2):
                    mm = pe.matmul(bk[hp * NK:(hp + 1) * NK, :], xk[:, g * NK:(g + 1) * NK],
                                   M_s[:, g, hp, :, :].rearrange("p a b -> p (a b)"), start=True, stop=True)
                mm.then_inc(r_fill, 1)

            def l0_o(g):
                bk = open_(RB, f"o{g}")
                pe.wait_ge(*RB.was_read(f"pt{g}"))
                pe.wait_ge(*RB.was_read(f"vw{g}"))
                for c in range(HP):
                    pe.matmul(bk[:, 0:D], pt0[:, g % 2, c, :], vw[:, g % 2, c, :], start=(c == 0), stop=False)
                pe.matmul(bk[:, 0:D], ptn[:, :], nvw_s[:, g, :], start=False, stop=True).then_inc(r_fill, 1)

            def l0_scat():
                bk = open_(RB, "scat")
                pe.wait_ge(selT_ready, 1)
                pe.wait_ge(*RB.was_read(f"o{G - 1}"))
                for t in range(NT):
                    for g in range(G):
                        mm = pe.matmul(bk[:, t * P:(t + 1) * P], selT[:, g, t * P:(t + 1) * P], ob[:, g, :],
                                       start=(g == 0), stop=(g == G - 1))
                mm.then_inc(r_fill, 1)

            def l1_xT():
                bk = open_(TB, "xT")
                for t in range(NT):
                    mm = pe.transpose(bk[:, t * P:(t + 1) * P], xn2[:, t, :], ident[:, :])
                mm.then_inc(t_fill, 1)

            def l1_gates():
                bk = open_(TB, "gates")
                pe.wait_ge(*TB.was_read("xT"))
                n = 2 * H * E
                for t in range(NT):
                    mm = pe.matmul(bk[:, t * n:(t + 1) * n], x2T[:, t * P:(t + 1) * P], wsd_s[:, :], start=True, stop=True)
                mm.then_inc(t_fill, 1)
                bk = open_(TB, "si")
                pe.matmul(bk[0:GT_ROW + SD, :], wst_s[:, :], x2T[:, :], start=True, stop=True).then_inc(t_fill, 1)

            def l1_chunk(n):
                if n < NCHUNK:
                    t, kind, e = chunk_kind(n)
                    bk = open_(YB, f"y{n}")
                    pe.matmul(bk[:, :], x2T[:, t * P:(t + 1) * P], wqkv_s[:, kind, e, :], start=True, stop=True)\
                      .then_inc(y_fill, 1)
                c = n - Q_LAG
                if 0 <= c < NCHUNK and chunk_kind(c)[1] == QUERY and chunk_kind(c)[2] in TURNED:
                    t, _, e = chunk_kind(c)
                    u = f"q{t}"
                    bk = open_(TB, u) if e == TURNED[0] else TB.bank(u)
                    if e in TAKES:
                        pe.wait_ge(q_add, takes_before(c + 1))
                    else:
                        pe.wait_ge(y_dve, YB.was_read(f"y{c}")[1])
                    src = gated(c)
                    for p_ in range(HP):
                        mm = pe.matmul(bk[:, p_ * P:(p_ + 1) * P], src[:, p_ * P:(p_ + 1) * P], ident[:, :],
                                       is_transpose=True, start=(e == TURNED[0] and p_ == 0), stop=(e == E - 1),
                                       skip_group_check=True)
                    mm.then_inc(t_fill if e == E - 1 else tr_part, 1)
                c = n - K_LAG
                if 0 <= c < NCHUNK and chunk_kind(c)[1:] == (KEY, E - 1):
                    t = chunk_kind(c)[0]
                    bk = open_(TB, f"k{t}")
                    pe.wait_ge(sum_add, adds_before(c + 1))
                    for p_ in range(HP):
                        mm = pe.transpose(bk[:, p_ * P:(p_ + 1) * P], k_or_v_sum(t, KEY)[:, p_ * P:(p_ + 1) * P], ident[:, :])
                    mm.then_inc(t_fill, 1)

            def l1_att(a):
                if a < NATT:
                    t, h = a // H, a % H
                    hs = slice((h % 2) * DH, (h % 2) * DH + DH)
                    bk = open_(YB, f"s{a}")
                    if a == 0:
                        pe.wait_ge(*TB.was_read(f"q{NT - 1}"))
                    pe.matmul(bk[:, :], qk[hs, 0, h // 2, t * P:(t + 1) * P], qk[hs, 1, h // 2, :], start=True, stop=True)\
                      .then_inc(y_fill, 1)
                n = a - PT_LAG
                if 0 <= n < NATT:
                    bk = open_(TB, f"pt{n}")
                    pe.wait_ge(*YB.was_read(f"s{n}"))
                    for c in range(NT):
                        mm = pe.transpose(bk[:, c * P:(c + 1) * P], pr[:, n % 3, c * P:(c + 1) * P], ident[:, :])
                    mm.then_inc(t_fill, 1)
                n = a - PV_LAG
                if 0 <= n < NATT and n % 2 == 1:
                    t, h = n // H, n % H
                    if n == 1:
                        pe.wait_ge(sum_add, adds_before(NCHUNK))
                        pe.wait_ge(*YB.was_read("s0"))
                    if t > 0 and h == 1:
                        pe.wait_ge(o_read, t)
                    pe.wait_ge(*TB.was_read(f"pt{n}"))
                    for c in range(NT):
                        for hp in range(2):
                            k = (h // 2 * 2 + hp) * DH
                            mm = pe.matmul(OBK[hp * DH:(hp + 1) * DH, h // 2 * P:(h // 2 + 1) * P], vv[:, c, k:k + DH],
                                           pt[:, (n - 1 + hp) % 3, c, :], start=(c == 0), stop=(c == NT - 1))
                    mm.then_inc(pv_done, 1)

            def l1_turn(t):
                bk = open_(TB, f"o{t}")
                pe.wait_ge(o_read, t + 1)
                for c in range(HP):
                    mm = pe.transpose(bk[:, c * P:(c + 1) * P], oo[:, 1, c * P:(c + 1) * P], ident[:, :])
                mm.then_inc(t_fill, 1)

            def l1_z(t):
                bk = open_(TB, f"z{t}")
                n = 1 if t + 1 < NT else H
                if t + 1 < NT:
                    pe.wait_ge(half_add, 4 * t + 4)
                for h in range(n):
                    if t + 1 == NT and h == 0:
                        pe.wait_ge(zm_dve, 1)
                    if t + 1 == NT and h == HALF:
                        pe.wait_ge(zm_ready, 2 * t + 1)
                    for c in range(3):
                        w = min(P, E * DH - c * P)
                        k = (h + (HALF if t + 1 == NT else 0)) % H * E * DH + c * P
                        mm = pe.matmul(bk[0:w, c * P:(c + 1) * P], yg[:, k:k + w], ident[:, :], is_transpose=True,
                                       start=(h == 0 and c == 0), stop=(h == n - 1), skip_group_check=True)
                mm.then_inc(t_fill, 1)

            def l1_fin(t):
                bk = open_(TB, f"f{t}")[:, 0:D]
                ts = slice(t * P, (t + 1) * P)
                if t == 0:
                    pe.wait_ge(st_ready, 1)
                pe.matmul(bk, x2T[:, ts], wfold_s[:, :], start=True, stop=False)
                pe.wait_ge(zt_done, t + 1)
                pe.wait_ge(*TB.was_read(f"z{t}"))
                pe.matmul(bk, zT[:, 0, :], wor_s[:, 0, :], start=False, stop=False)
                pe.matmul(bk, zT[:, 1, :], wor_s[:, 1, :], start=False, stop=False)
                pe.matmul(bk, zst[:, ts], wor_s[0:DH + SD + 1, 2, :], start=False, stop=True).then_inc(t_fill, 1)

            st = {("l0", "dd"): l0_dd, ("l0", "vr"): l0_vr, ("l0", "kw"): l0_kw, ("l0", "g"): l0_g, ("l0", "gq"): l0_gq,
                  ("l0", "gk"): l0_gk, ("l0", "small"): l0_small, ("l0", "ax"): l0_ax, ("l0", "s"): l0_s,
                  ("l0", "wsum"): l0_wsum, ("l0", "yT"): l0_yT, ("l0", "att"): l0_att, ("l0", "ptn"): l0_ptn,
                  ("l0", "pt"): l0_pt, ("l0", "vw"): l0_vw, ("l0", "o"): l0_o, ("l0", "scat"): l0_scat,
                  ("l1", "xT"): l1_xT, ("l1", "gates"): l1_gates, ("l1", "chunk"): l1_chunk,
                  ("l1", "att"): l1_att, ("l1", "turn"): l1_turn, ("l1", "z"): l1_z, ("l1", "fin"): l1_fin}
            run({**st, ("p", "fold"): p_fold, ("p", "xT"): p_xT, ("p", "nulls"): p_nulls, ("p", "scan_weights"): p_scan_weights, ("p", "picked"): p_picked}, FIRST)
            step_over(pe, 1)
            with pe.Fori(0, B - 1) as i:
                run(st, BODY)
                step_over(pe, i + 2)
            run(st, L1)

        @block.vector
        def _(dve):
            dve.memset(wr_pad, 0.0).then_inc(p_zero, 1)
            dve.memset(nkb, 0.0).then_inc(p_zero, 1)
            dve.memset(nvb, 0.0).then_inc(p_zero, 1)
            dve.wait_ge(p_zero, 3)
            dve.wait_ge(p_ldw, 16)
            for b in range(B):
                for k in range(2):
                    last = dve.tensor_copy(wr_pad[:, b, k * 32 + b * G:k * 32 + (b + 1) * G], qkr_s[:, k * G:(k + 1) * G])
            last.then_inc(p_blk, 1)
            def batch(b):
                src, k = (xa, b) if b < 4 else (xb, b - 4)
                return src[:, k * T:(k + 1) * T]

            n0 = 0
            for half in range(2):
                dve.wait_ge(p_ldx[half], 16 * B // 2)
                tiles = range(half * B * NT // 2, (half + 1) * B * NT // 2)
                ts = slice(tiles.start, tiles.stop)
                for n in tiles:
                    last = dve.bn_stats(stats[:, n, :], batch(n // NT)[:, n % NT * D:(n % NT + 1) * D])
                last.then_inc(p_bn, 1)
                dve.wait_ge(p_bn, 2 * half + 1)
                for n in tiles:
                    last = dve.bn_aggr(mv[:, n, :], stats[:, n, :])
                last.then_inc(p_bn, 1)
                dve.wait_ge(p_bn, 2 * half + 2)
                dve.tensor_scalar(lv[:, ts], mv[:, ts, 1], LN_EPS, None, ALU.add).then_inc(p_nt, 1)
                dve.wait_ge(p_nt, n0 + 1)
                newton(dve, ly[:, ts], lv[:, ts], lw[:, ts], len(tiles), p_nt, n0 + 1)
                n0 += 1 + NEWTON
                for n in tiles:
                    xt = batch(n // NT)[:, n % NT * D:(n % NT + 1) * D]
                    dve.tensor_scalar(xt, xt, mv[:, n, 0:1], ly[:, n:n + 1], ALU.subtract, ALU.mult).then_inc(p_xn, 1)
            dve.wait_ge(p_ld, 16 * N_LOADS)
            dve.memset(bcol9, 0.0).then_inc(p_zero, 1)
            dve.wait_ge(p_zero, 4)
            dve.tensor_copy(bcol9[:, SD:SD + 1], bin_s)
            for hp in range(2):
                ps = slice(hp * DH, (hp + 1) * DH)
                dve.tensor_copy(nkb[ps, :, :, hp], nkt[ps, :, :])
                for g in range(G):
                    first = g * H + hp
                    dve.tensor_copy(nvb[ps, g, first:first + 34 * (HP - 1) + 1:34], nvt[ps, g, :])
            dve.tensor_copy(u9_s[:, :, H], qkr_s[:, 0:G])
            dve.tensor_scalar(gnw_s[:, :], gnw_s[:, :], 0.5, None, ALU.mult)
            dve.tensor_scalar(gnb_s[:, :], gnb_s[:, :], 0.5, None, ALU.mult).then_inc(p_blk, 3)
            dve.wait_ge(p_cst, 11)
            dve.wait_ge(p_log, B)
            dve.tensor_copy(lgw, LG[0:64, :]).then_inc(p_top, 1)

            def p_round(k):
                rows = slice(0, 64 if k < ROUNDS_K else 32)
                dve.wait_ge(p_top, 2 * k + 1)
                dve.max(top8[rows], lgw[rows]).then_inc(p_top, 1)
                dve.wait_ge(p_top, 2 * k + 2)
                dve.match_replace(lgw[rows], top8[rows], lgw[rows], PICKED).then_inc(p_top, 1)

            def p_picked():
                n = 2 * ROUNDS_Q + 1
                dve.wait_ge(p_top, n)
                dve.tensor_scalar(msk, lgw, PICKED, None, ALU.is_le).then_inc(p_top, 1)
                dve.wait_ge(p_top, n + 1)
                dve.tensor_tensor_scan(cum, onesr, msk, 0.0, ALU.mult, ALU.add).then_inc(p_top, 1)
                dve.wait_ge(p_top, n + 2)
                dve.tensor_tensor(cum, cum, msk, ALU.mult).then_inc(p_pos, 1)
                dve.wait_ge(p_posT, 1)
                for k in range(2):
                    last = dve.tensor_copy(posTb[:, :, :, k, :],
                                           LG[:, 0:NT * 64].rearrange("p (t k b g) -> p k b t g", t=NT, k=2, b=B)[:, k])
                last.then_inc(p_pos, 1)

            def p_scan_weights():
                dve.wait_ge(*PB.filled("wmisc"))
                wm = PB.bank("wmisc")
                dve.tensor_copy(wgt_s, wm[:, 0:SD])
                dve.tensor_scalar(bgt_s[:, :], wm[ST_ROWS, SD:SD + 1], bg_s, 0.5, ALU.add, ALU.mult).then_inc(p_dve, 1)

            def l0_lerp():
                dve.wait_ge(th_done, 1)
                dve.wait_ge(dif_ready, 1)
                dve.scalar_tensor_tensor(out=th[:, :], in0=th[:, :], scalar=1.0, in1=dif[:, :],
                                         op0=ALU.add, op1=ALU.mult).then_inc(e_done, 1)
                dve.wait_ge(e_done, 1)
                dve.scalar_tensor_tensor(out=aa[:, :], in0=th[:, :], scalar=0.5, in1=xTp[:, 0:T],
                                         op0=ALU.mult, op1=ALU.add).then_inc(af_ready, 1)
                dve.scalar_tensor_tensor(out=dif[:, :], in0=th[:, :], scalar=-0.5, in1=dif[:, :],
                                         op0=ALU.mult, op1=ALU.add).then_inc(af_ready, 1)

            def l0_ge():
                half = 0.5 * 0.6065306597126334
                dve.wait_ge(*RB.was_read("w"))
                dve.tensor_scalar(dec[:, 1:T], dec[:, 1:T], half, half, ALU.mult, ALU.add).then_inc(dec_ready, 1)
                dve.wait_ge(tg_done, 1)
                dve.wait_ge(*RB.filled("g"))
                dve.scalar_tensor_tensor(out=silu[:, :], in0=silu[:, :], scalar=1.0, in1=RB.bank("g")[:, :],
                                         op0=ALU.add, op1=ALU.mult).then_inc(r_dve, 1)

            def selection(k, w, tiles):
                n = tiles.stop - tiles.start
                dve.tensor_tensor(sel[:, 0:NT * G * w].rearrange("p (t g j) -> p t g j", t=NT, g=G)[:, tiles],
                                  iota1[:, 0:w].unsqueeze(1).unsqueeze(1).broadcast_to((P, n, G, w)),
                                  posT[:, tiles, k, :].unsqueeze(3).broadcast_to((P, n, G, w)), ALU.is_equal)\
                   .then_inc(sel_ready, 1)

            def l0_selq(half):
                dve.wait_ge(ld_posT, 16)
                selection(0, NQ, slice(half * NT // 2, (half + 1) * NT // 2))

            def l0_gqe():
                dve.wait_ge(*RB.filled("gq"))
                selection(1, NK, slice(0, NT))
                dve.tensor_scalar(cnt4[:, :, :], posT[:, :, 0, :], 0.5, None, ALU.is_gt).then_inc(cnt_s, 1)
                dve.wait_ge(cnt_s, 1)
                dve.tensor_reduce(cnt[:, :], cnt4[:, :, :], X, ALU.add).then_inc(cnt_s, 1)
                dve.wait_ge(cnt_s, 2)
                dve.tensor_scalar(nz[:, :], cnt[:, :], 0.5, None, ALU.is_lt).then_inc(cnt_s, 1)
                dve.tensor_scalar(rcnt[:, :], cnt[:, :], 1.0, None, ALU.max).then_inc(cnt_s, 1)
                dve.wait_ge(cnt_s, 4)
                dve.reciprocal(rcnt[:, :], rcnt[:, :]).then_inc(cnt_s, 1)

            def l0_gke():
                dve.wait_ge(ld_pos, 16)
                dve.tensor_scalar(selT[:, :, :], selT[:, :, :], iotac[:, 0:1], None, ALU.is_equal).then_inc(selT_ready, 1)

            def l0_scan(q):
                if q == 0:
                    dve.wait_ge(dec_ready, 1)
                dve.wait_ge(kv_done, q + 1)
                for j in range(2):
                    v1 = vb[:, q % 2, j, :]
                    dve.tensor_tensor_scan(v1, dec[:, :], v1, 0.0, ALU.mult, ALU.add).then_inc(scan_done, 1)

            def l0_smalle():
                dve.wait_ge(*RB.filled("small"))
                dve.tensor_copy(sm[:, :], RB.bank("small")[:, 0:G * (H + 1) + G]).then_inc(r_dve, 1)
                dve.wait_ge(*RB.was_read("small"))
                dve.tensor_copy(snull.rearrange("p (g h) -> p g h", g=G),
                                sm[:, 0:G * (H + 1)].rearrange("p (g n) -> p g n", g=G)[:, :, 0:H]).then_inc(soft, 1)

            def l0_se(g):
                dve.wait_ge(*RB.filled(f"s{g}"))
                dve.tensor_copy(sel[:, g * H * NK:(g + 1) * H * NK], RB.bank(f"s{g}")[:, :]).then_inc(r_dve, 1)

            def gh(half):
                return slice(half * G * H // 2, (half + 1) * G * H // 2)

            def l0_soft(half):
                dve.wait_ge(*RB.was_read(f"s{G - 1}"))
                dve.tensor_reduce(hmax[:, gh(half)], skeys[:, gh(half), :], X, ALU.max).then_inc(soft, 1)
                if half == 1:
                    dve.wait_ge(soft, 3)
                    dve.tensor_tensor(hmax[:, :], hmax[:, :], snull, ALU.max).then_inc(soft, 1)

            def l0_shift(half):
                if half == 0:
                    dve.wait_ge(soft, 4)
                    dve.tensor_tensor(snull, snull, hmax[:, :], ALU.subtract).then_inc(soft, 1)
                dve.tensor_tensor(skeys[:, gh(half), :], skeys[:, gh(half), :],
                                  hmax[:, gh(half)].unsqueeze(2).broadcast_to((P, G * H // 2, NK)), ALU.subtract)\
                   .then_inc(soft, 1)

            def l0_sums(half):
                dve.wait_ge(e0_done, half + 1)
                dve.tensor_reduce(hsum[:, gh(half)], skeys[:, gh(half), :], X, ALU.add).then_inc(soft, 1)
                if half == 0:
                    dve.wait_ge(smt_done, 1)
                    dve.tensor_scalar(smt[:, :], smt[:, :], 0.5, 0.5, ALU.mult, ALU.add).then_inc(sig_ready, 1)
                    return
                dve.wait_ge(soft, 9)
                dve.tensor_tensor(hsum[:, :], hsum[:, :], snull, ALU.add).then_inc(soft, 1)
                dve.wait_ge(soft, 10)
                dve.reciprocal(hsum[:, :], hsum[:, :]).then_inc(soft, 1)
                dve.wait_ge(soft, 11)
                dve.wait_ge(sig_ready, 1)
                dve.wait_ge(soft, 8)
                dve.wait_ge(sig_ready, 1)
                dve.tensor_tensor(hsum[:, :].rearrange("p (g h) -> p g h", g=G),
                                  hsum[:, :].rearrange("p (g h) -> p g h", g=G),
                                  smt[:, 0:G * (H + 1)].rearrange("p (g n) -> p g n", g=G)[:, :, H:H + 1]
                                  .broadcast_to((P, G, H)), ALU.mult).then_inc(soft, 1)

            def l0_vwe(g):
                dve.wait_ge(*RB.filled(f"vw{g}"))
                n = G * (H + 1) + g
                dve.tensor_scalar(vw[:, g % 2, :, :].rearrange("p c d -> p (c d)"), RB.bank(f"vw{g}")[:, :],
                                  smt[:, n:n + 1], None, ALU.mult).then_inc(r_dve, 1)

            def l0_gn1():
                dve.wait_ge(ot_done, NPAIR)
                o3 = NBK[:, :].rearrange("p (n k) -> p n k", k=ADH)
                c3 = th[:, :].rearrange("p (n k) -> p n k", k=ADH)
                n = NT * AH
                dve.tensor_reduce(mu[:, :], o3, X, ALU.add).then_inc(gn, 1)
                dve.wait_ge(gn, 1)
                dve.scalar_tensor_tensor(out=c3, in0=mu[:, :].unsqueeze(2).broadcast_to((P, n, ADH)), scalar=-1.0 / ADH,
                                         in1=o3, op0=ALU.mult, op1=ALU.add).then_inc(gn, 1)

            def l0_gn2():
                n = NT * AH
                dve.wait_ge(sq_done, 1)
                dve.tensor_reduce(va[:, :], lp[:, 0, :].rearrange("p (n k) -> p n k", k=ADH), X, ALU.add).then_inc(gn, 1)
                dve.wait_ge(gn, 3)
                dve.tensor_scalar(va[:, :], va[:, :], 1.0 / ADH, GN_EPS, ALU.mult, ALU.add).then_inc(gn, 1)
                dve.wait_ge(gn, 4)
                newton_start(dve, ya, va, wa, n, gn, 4)

            def l0_root(k):
                n = NT * AH
                newton_step(dve, ya, va, wa, n, gn, 4, k)
                if k < 2:
                    return
                c3 = th[:, :].rearrange("p (n k) -> p n k", k=ADH)
                dve.tensor_tensor(c3, c3, ya[:, :].unsqueeze(2).broadcast_to((P, n, ADH)), ALU.mult).then_inc(gn, 1)

            def l0_x0():
                dve.wait_ge(base_s, 2)
                dve.wait_ge(att_fill, 1)
                flat = xr[:, :, :].rearrange("p t d -> p (t d)")
                dve.tensor_tensor(flat, flat, NBK[:, :], ALU.add).then_inc(x0_new, 1)

            def l0_join():
                x3 = xq[:, :].rearrange("p (t d) -> p t d", t=NT)
                dve.wait_ge(*RB.filled("scat"))
                dve.wait_ge(cnt_s, 5)
                dve.tensor_tensor(x3, RB.bank("scat")[:, :].rearrange("p (t d) -> p t d", t=NT),
                                  rcnt[:, :].unsqueeze(2).broadcast_to((P, NT, D)), ALU.mult).then_inc(r_dve, 1)
                dve.wait_ge(*RB.was_read("scat"))
                dve.wait_ge(x0_new, 1)
                dve.tensor_tensor(xr[:, :, :], xr[:, :, :], x3, ALU.add).then_inc(x1_new, 1)

            def l0_ln():
                dve.wait_ge(x1_new, 1)
                for t in range(NT):
                    last = dve.bn_stats(stats[:, t, :], xr[:, t, :])
                last.then_inc(ln_s, 1)
                dve.wait_ge(ln_s, 1)
                for t in range(NT):
                    last = dve.bn_aggr(mv[:, t, :], stats[:, t, :])
                last.then_inc(ln_s, 1)
                dve.wait_ge(ln_s, 2)
                dve.tensor_scalar(lv[:, 0:NT], mv[:, 0:NT, 1], LN_EPS, None, ALU.add).then_inc(ln_s, 1)
                dve.wait_ge(ln_s, 3)
                newton(dve, ly, lv, lw, NT, ln_s, 3)
                for t in range(NT):
                    dve.tensor_scalar(xn2[:, t, :], xr[:, t, :], mv[:, t, 0:1], ly[:, t:t + 1],
                                      ALU.subtract, ALU.mult)

            NG = NT * 2 * H
            z3 = zg[:, :].rearrange("p (n e) -> p n e", e=E)
            w3 = wins[:, :].rearrange("p (n e) -> p n e", e=E)

            def l1_gates():
                dve.wait_ge(*TB.filled("gates"))
                dve.tensor_scalar(zg[:, :], TB.bank("gates")[:, 0:NG * E], Z_HI, Z_LO, ALU.min, ALU.max).then_inc(t_dve, 1)
                dve.tensor_copy(w3, rank0[:, :].unsqueeze(1).broadcast_to((P, NG, E))).then_inc(rank_s, 1)
                dve.wait_ge(*TB.was_read("gates"))

                for d in range(1, E):
                    dve.tensor_tensor(beats(d), z3[:, :, 0:E - d], z3[:, :, d:E], ALU.is_ge).then_inc(rank_s, 1)

            def beats(d):
                first = sum(NG * (E - k) for k in range(1, d))
                return beat[:, first:first + NG * (E - d)].rearrange("p (n e) -> p n e", e=E - d)

            def l1_rank(d):
                n = E + 2 * (d - 1)
                dve.wait_ge(rank_s, n)
                dve.tensor_tensor(w3[:, :, 0:E - d], w3[:, :, 0:E - d], beats(d), ALU.add).then_inc(rank_s, 1)
                if d == 1:
                    dve.wait_ge(ex_s, 1)
                    dve.tensor_scalar(sg[:, :], sg[:, :], 1.0, None, ALU.add).then_inc(sig_s, 1)
                dve.wait_ge(rank_s, n + 1)
                dve.tensor_tensor(w3[:, :, d:E], w3[:, :, d:E], beats(d), ALU.subtract).then_inc(rank_s, 1)
                if d == 1:
                    dve.wait_ge(sig_s, 1)
                    dve.reciprocal(sg[:, :], sg[:, :]).then_inc(sig_s, 1)

            def l1_sig():
                n = E + 2 * (E - 1)
                dve.wait_ge(rank_s, n)
                dve.tensor_scalar(wins[:, :], wins[:, :], E - TOPK - 0.5, None, ALU.is_gt).then_inc(rank_s, 1)
                dve.wait_ge(rank_s, n + 1)
                dve.wait_ge(sig_s, 2)
                g4 = sg[:, :].rearrange("p (t k n) -> p t k n", t=NT, k=2)
                m4 = wins[:, :].rearrange("p (t k n) -> p t k n", t=NT, k=2)
                dve.tensor_tensor(g4[:, :, 0, :], g4[:, :, 0, :], m4[:, :, 0, :], ALU.mult).then_inc(gates_ready, 1)
                dve.scalar_tensor_tensor(out=g4[:, :, 1, :], in0=g4[:, :, 1, :], scalar=SCALE, in1=m4[:, :, 1, :],
                                         op0=ALU.mult, op1=ALU.mult).then_inc(gates_ready, 1)
                dve.wait_ge(gates_ready, 2)

            def l1_state():
                gate, inp = xn2[ST_ROWS, :, :].rearrange("p a b -> p (a b)"), pr[ST_ROWS, 0, :]
                dve.wait_ge(gt_read, 1)
                dve.tensor_scalar(inp, gate, -0.5, 0.5, ALU.mult, ALU.add).then_inc(sc_s, 1)
                dve.wait_ge(sc_s, 1)
                dve.tensor_scalar(gate, gate, 0.5, 0.5, ALU.mult, ALU.add).then_inc(sc_s, 1)
                dve.wait_ge(*TB.filled("si"))
                dve.scalar_tensor_tensor(out=inp, in0=TB.bank("si")[ST_ROWS, :], scalar=bsi_s[:, 0:1], in1=inp,
                                         op0=ALU.add, op1=ALU.mult).then_inc(si_read, 1)
                dve.wait_ge(sc_s, 2)
                dve.wait_ge(*TB.was_read("si"))
                dve.tensor_tensor_scan(zst[ST_ROWS, :], gate, inp, 0.0, ALU.mult, ALU.add).then_inc(st_ready, 1)
                dve.wait_ge(st_ready, 1)

            g5 = sg[:, :].rearrange("p (t k h e) -> p t k h e", t=NT, k=2, h=H)

            def l1_chunk(n):
                c = n - G_LAG
                if not 0 <= c < NCHUNK:
                    return
                t, kind, e = chunk_kind(c)
                if kind == QUERY:
                    old = [k for k in range(c) if chunk_kind(k)[1] == QUERY]
                    if len(old) >= 3:
                        ot, _, oe = chunk_kind(old[-3])
                        if oe == E - 1:
                            dve.wait_ge(*TB.filled(f"q{ot}"))
                        elif oe in TURNED:
                            dve.wait_ge(tr_part, sum(1 for k in old[:-2] if chunk_kind(k)[2] in TURNED[:-1]))
                        else:
                            dve.wait_ge(q_add, takes_before(old[-3]) + 1 + (oe in TAKES))
                elif e == 0:
                    if kind == KEY and t >= 2:
                        dve.wait_ge(*TB.filled(f"k{t - 2}"))
                elif adds_before(c) >= 3:
                    dve.wait_ge(sum_add, adds_before(c) - 2)
                dve.wait_ge(*YB.filled(f"y{c}"))
                dve.tensor_tensor(gated(c).rearrange("p (h d) -> p h d", h=H),
                                  YB.bank(f"y{c}")[:, :].rearrange("p (h d) -> p h d", h=H),
                                  g5[:, t, 1 if kind == QUERY else 0, :, e].unsqueeze(2).broadcast_to((P, H, DH)),
                                  ALU.mult).then_inc(y_dve, 1)
                if kind == QUERY and e in TAKES:
                    dve.wait_ge(*YB.was_read(f"y{c}"))
                    if e - 1 in TAKES:
                        dve.wait_ge(q_add, takes_before(c))
                    dve.tensor_tensor(gated(c), gated(c), gated(c - 1), ALU.add).then_inc(q_add, 1)

            def l1_att(a):
                t, r = divmod(a - D_LAG, H)
                if r == 0 and 0 <= t < NT:
                    hs = slice(t * H, (t + 1) * H)
                    dve.wait_ge(*YB.was_read(f"s{H * t + H - 1}"))
                    dve.reciprocal(rden[:, hs], den[:, hs]).then_inc(rden_s, 1)
                    dve.wait_ge(pv_done, HP * (t + 1))
                    dve.tensor_copy(oo[:, 1, :], OBK[:, :]).then_inc(o_read, 1)
                if a < NATT:
                    dve.wait_ge(*YB.filled(f"s{a}"))
                    dve.tensor_reduce(nmax[:, a:a + 1], YB.bank(f"s{a}")[:, :], X, ALU.max, negate=True)\
                       .then_inc(max_done, 1)
                for part in range(3):
                    t, r = divmod(a - A_LAG[part], H)
                    if r != 0 or not 0 <= t < NT - 1:
                        continue
                    if part < 2:
                        n = HALF * E * DH
                        k = slice(part * n // 2, (part + 1) * n // 2)
                        if part == 0:
                            dve.wait_ge(zm_ready, 2 * t + 2)
                        dve.tensor_tensor(yg[:, k], yg[:, k], yg[:, n + k.start:n + k.stop], ALU.add).then_inc(half_add, 1)
                    else:
                        for j, n in enumerate((2 * E * DH, E * DH)):
                            dve.wait_ge(half_add, 4 * t + 2 + j)
                            dve.tensor_tensor(yg[:, 0:n], yg[:, 0:n], yg[:, n:2 * n], ALU.add).then_inc(half_add, 1)

            def l1_turn(t):
                hs = slice(t * H, (t + 1) * H)
                dve.wait_ge(rden_s, t + 1)
                if t >= 1:
                    dve.wait_ge(zm_ready, 2 * t)
                dve.wait_ge(*TB.filled(f"o{t}"))
                dve.tensor_tensor(oo[:, 0, :].rearrange("p (h d) -> p h d", h=H),
                                  TB.bank(f"o{t}")[:, :].rearrange("p (h d) -> p h d", h=H),
                                  rden[:, hs].unsqueeze(2).broadcast_to((P, H, DH)), ALU.mult).then_inc(t_dve, 1)
                if t + 1 == NT:
                    dve.wait_ge(*TB.was_read(f"o{t}"))
                    dve.wait_ge(*TB.filled(f"z{t - 1}"))
                    masked(dve, t, 1, zm_dve)

            def l1_fin(t):
                dve.wait_ge(*TB.filled(f"f{t}"))
                if t == 0:
                    dve.wait_ge(x1_copied, 1)
                dve.tensor_tensor(x1[:, t, :], x1[:, t, :], TB.bank(f"f{t}")[:, 0:D], ALU.add).then_inc(t_dve, 1)

            st = {("l0", "lerp"): l0_lerp, ("l0", "ge"): l0_ge, ("l0", "x0"): l0_x0,
                  ("l0", "selq"): l0_selq, ("l0", "gqe"): l0_gqe, ("l0", "gke"): l0_gke, ("l0", "scan"): l0_scan,
                  ("l0", "smalle"): l0_smalle, ("l0", "se"): l0_se, ("l0", "soft"): l0_soft, ("l0", "sums"): l0_sums,
                  ("l0", "vwe"): l0_vwe, ("l0", "gn1"): l0_gn1, ("l0", "gn2"): l0_gn2, ("l0", "root"): l0_root, ("l0", "join"): l0_join,
                  ("l0", "shift"): l0_shift, ("l0", "ln"): l0_ln,
                  ("l1", "gates"): l1_gates, ("l1", "rank"): l1_rank, ("l1", "sig"): l1_sig, ("l1", "state"): l1_state, ("l1", "chunk"): l1_chunk,
                  ("l1", "att"): l1_att, ("l1", "turn"): l1_turn, ("l1", "fin"): l1_fin}
            run({**st, ("p", "round"): p_round, ("p", "picked"): p_picked, ("p", "scan_weights"): p_scan_weights}, FIRST)
            step_over(dve, 1)
            with dve.Fori(0, B - 1) as i:
                run(st, BODY)
                step_over(dve, i + 2)
            run(st, L1)


def kernel(**inputs):
    import numpy as np
    import concourse.bacc as _bacc
    from concourse import mybir as _mybir
    from concourse.bass_utils import run_bass_kernel_spmd as _run

    a = {k: np.asarray(v) for k, v in inputs.items()}
    heads = lambda w: w.reshape(G, HP, P, D).transpose(2, 0, 1, 3)
    wkv = a["L0_ffn_w_kv"]
    null = a["L0_ffn_null_kv"].reshape(2, G, HP, P).transpose(0, 3, 1, 2)
    wq5 = a["L1_ffn_Wq"].reshape(D, H, E, DH).transpose(0, 2, 1, 3).reshape(D, 1, E, CW)
    wkv5 = a["L1_ffn_Wkv"].reshape(D, 2, H, E, DH).transpose(0, 1, 3, 2, 4).reshape(D, 2, E, CW)
    wo5 = a["L1_ffn_Wo"].reshape(DH, E, D).transpose(1, 0, 2).reshape(E * DH, D)
    wor = np.zeros((3 * P, D), wo5.dtype)
    wor[:E * DH] = wo5
    win, bin_ = a["L1_attn_W_in"], a["L1_attn_b_in"]
    laid = {
        "x": a["L0_attn_x"],
        "ddw": a["L0_attn_ddlerp_w"].T,
        "mixes": np.stack([a[f"L0_attn_mix_{n}"] for n in "vrkwg"], axis=1),
        "projw": np.stack([a[f"L0_attn_{n}_w"].T for n in ("v", "r", "k", "w", "g", "out")], axis=1),
        "gnw": a["L0_attn_gn_weight"], "gnb": a["L0_attn_gn_bias"],
        "qkr": np.concatenate([a["L0_ffn_w_qr"], a["L0_ffn_w_kvr"]]).T,
        "wqn": heads(a["L0_ffn_w_q"]), "wkn": heads(wkv[:, :H * DH]), "wvn": heads(wkv[:, H * DH:]),
        "won": heads(a["L0_ffn_w_out"].transpose(0, 2, 1)),
        "nkT": null[0], "nvT": null[1], "null_token": a["L0_ffn_null_token"].reshape(D),
        "winT": win[:, :D].T, "winT8": win[:, D:].T, "wcat": win[:, D:],
        "wg": a["L1_attn_W_g"][:D], "wg8": a["L1_attn_W_g"][D:],
        "bin_": bin_[:D, None], "bin8": bin_[D:, None], "bg": a["L1_attn_b_g"][:, None],
        "wout": a["L1_attn_W_out"][:D],
        "wout9": np.concatenate([a["L1_attn_W_out"][D:], a["L1_attn_b_out"][None]]),
        "wqkv": np.concatenate([wq5, wkv5], axis=1),
        "wsd": np.concatenate([a["L1_ffn_Ws"], a["L1_ffn_Wd"]], axis=1),
        "wor": wor.reshape(3, P, D),
    }
    nc = _bacc.Bacc("TRN2", target_bir_lowering=False, num_devices=1)
    arrays, args = {}, []
    for name, arr in laid.items():
        arr = np.ascontiguousarray(arr)
        arrays[f"in_{name}_dram"] = arr
        args.append(nc.dram_tensor(f"in_{name}_dram", arr.shape, _mybir.dt.from_np(arr.dtype), kind="ExternalInput").ap())
    args.append(nc.dram_tensor("out_0_dram", (B, T, D), F32, kind="ExternalOutput").ap())
    layers(nc, *args)
    r = _run(nc, [arrays], core_ids=[0])
    return r.results[0]["out_0_dram"]
```
